# Optimizing a Trainium2 kernel written in Bass

```python
import numpy as np
import jax
import jax.numpy as jnp

def _softmax(x, axis=-1):
    return jax.nn.softmax(x, axis=axis)

def _gelu(x):
    return jax.nn.gelu(x, approximate=True)

def _silu(x):
    return jax.nn.silu(x)

def _sigmoid(x):
    return jax.nn.sigmoid(x)

def _layernorm(x, axis=-1, eps=1e-05):
    m = jnp.mean(x, axis=axis, keepdims=True)
    v = jnp.var(x, axis=axis, keepdims=True)
    return (x - m) / jnp.sqrt(v + eps)

def _scatter_add(tgt, idx, src, axis=0):
    return tgt.at[idx].add(src)

def _segment_sum(src, seg, n):
    return jax.ops.segment_sum(src, seg, n)
kernel_name = 'mk_audio_tower_d4_tok_audfeat256_r4_e963ac'

def setup_inputs(seed: int=0):
    np.random.seed(seed)
    _w = jnp.asarray

    def _rec_inputs():
        import jax
        import jax.numpy as jnp
        _rk = jax.random.key(seed)
        x = 7.22013e-05 + 1.00017 * jax.random.normal(jax.random.fold_in(_rk, 1), (16, 250, 64), jnp.float32)
        return x
    x = _rec_inputs()

    def _L0_tok_setup():
        import jax, jax.numpy as jnp
        import numpy as np
        WIN = 9
        key = jax.random.key(seed)
        ks = jax.random.split(key, 4)
        N, L, C, U = (8, 1024, 64, 64)
        x = jax.random.normal(ks[0], (N, L, C), dtype=jnp.float32)
        W_qry = jax.random.normal(ks[1], (C, U), dtype=jnp.float32) * 0.05
        W_key = jax.random.normal(ks[2], (C, U), dtype=jnp.float32) * 0.05
        v = jax.random.normal(ks[3], (U,), dtype=jnp.float32) * 0.05
        b = jnp.zeros((U,), dtype=jnp.float32)
        return {'x': x, 'W_qry': W_qry, 'W_key': W_key, 'v': v, 'b': b}
    _L0_tok_all = _L0_tok_setup()
    _L0_tok_in = {k: v for k, v in _L0_tok_all.items() if k in ('W_qry', 'W_key', 'v', 'b')}
    del _L0_tok_all

    def _L0_attn_setup():
        import jax, jax.numpy as jnp
        import numpy as np
        key = jax.random.key(seed)
        k1, k2, k3 = jax.random.split(key, 3)
        d = 64
        x = jax.random.normal(k1, (8, 512, d), dtype=jnp.float32)
        Wq = jax.random.normal(k2, (d, d), dtype=jnp.float32) * d ** (-0.5)
        Wk = jax.random.normal(k3, (d, d), dtype=jnp.float32) * d ** (-0.5)
        return {'x': x, 'Wq': Wq, 'Wk': Wk}
    _L0_attn_all = _L0_attn_setup()
    _L0_attn_in = {k: v for k, v in _L0_attn_all.items() if k in ('Wq', 'Wk')}
    del _L0_attn_all

    def _L0_ffn_setup():
        import jax, jax.numpy as jnp
        import numpy as np
        TOP_K = 6
        LN_EPS = 1e-05
        key = jax.random.key(seed)
        ks = jax.random.split(key, 4)
        B, S, D, E = (2, 64, 64, 64)
        x = jax.random.normal(ks[0], (B, S, D), dtype=jnp.float32)
        gate_w = jax.random.normal(ks[1], (E, D), dtype=jnp.float32) * 0.02
        lattice_weights = jax.random.normal(ks[2], (E, D, D), dtype=jnp.float32) * 0.02
        out_w = jax.random.normal(ks[3], (D, D), dtype=jnp.float32) * 0.02
        out_b = jnp.zeros((D,), dtype=jnp.float32)
        ln_g = jnp.ones((D,), dtype=jnp.float32)
        ln_b = jnp.zeros((D,), dtype=jnp.float32)
        return {'x': x, 'gate_w': gate_w, 'lattice_weights': lattice_weights, 'out_w': out_w, 'out_b': out_b, 'ln_g': ln_g, 'ln_b': ln_b}
    _L0_ffn_all = _L0_ffn_setup()
    _L0_ffn_in = {k: v for k, v in _L0_ffn_all.items() if k in ('gate_w', 'lattice_weights', 'out_w', 'out_b', 'ln_g', 'ln_b')}
    del _L0_ffn_all

    def _L1_attn_setup():
        import jax, jax.numpy as jnp
        import numpy as np
        MIDC = 64
        HEADS = 16
        HEADC = MIDC // HEADS
        EPS = 1e-05

        def _layernorm(x, w, b):
            mean = jnp.mean(x, axis=-1, keepdims=True)
            std = jnp.std(x, axis=-1, keepdims=True, ddof=1)
            return w * (x - mean) / (std + EPS) + b
        key = jax.random.key(seed)
        ks = jax.random.split(key, 3)
        B, HW = (8, 4096)
        x = jax.random.normal(ks[0], (B, HW, MIDC), dtype=jnp.float32)
        W_qkv = jax.random.normal(ks[1], (3 * MIDC, MIDC), dtype=jnp.float32) * 0.02
        b_qkv = jnp.zeros((3 * MIDC,), dtype=jnp.float32)
        kln_w = jnp.ones((HEADS, 1, HEADC), dtype=jnp.float32)
        kln_b = jnp.zeros((HEADS, 1, HEADC), dtype=jnp.float32)
        vln_w = jnp.ones((HEADS, 1, HEADC), dtype=jnp.float32)
        vln_b = jnp.zeros((HEADS, 1, HEADC), dtype=jnp.float32)
        W_proj = jax.random.normal(ks[2], (MIDC, MIDC), dtype=jnp.float32) * 0.02
        b_proj = jnp.zeros((MIDC,), dtype=jnp.float32)
        return {'x': x, 'W_qkv': W_qkv, 'b_qkv': b_qkv, 'kln_w': kln_w, 'kln_b': kln_b, 'vln_w': vln_w, 'vln_b': vln_b, 'W_proj': W_proj, 'b_proj': b_proj}
    _L1_attn_all = _L1_attn_setup()
    _L1_attn_in = {k: v for k, v in _L1_attn_all.items() if k in ('W_qkv', 'b_qkv', 'kln_w', 'kln_b', 'vln_w', 'vln_b', 'W_proj', 'b_proj')}
    del _L1_attn_all

    def _L1_ffn_setup():
        import jax, jax.numpy as jnp
        import numpy as np
        C = 64
        HID = 256
        E = 8
        TEMP = 1.0
        key = jax.random.key(seed)
        ks = jax.random.split(key, 7)
        x = jax.random.normal(ks[0], (8, 4096, C), dtype=jnp.float32)
        W1 = jax.random.normal(ks[1], (C, HID), dtype=jnp.float32) * 0.02
        b1 = jnp.zeros((HID,), dtype=jnp.float32)
        Wg = jax.random.normal(ks[2], (HID, E), dtype=jnp.float32) * 0.02
        bg = jnp.zeros((E,), dtype=jnp.float32)
        Wd = jax.random.normal(ks[3], (E, HID, C), dtype=jnp.float32) * 0.02
        bd = jnp.zeros((E, C), dtype=jnp.float32)
        return {'x': x, 'W1': W1, 'b1': b1, 'Wg': Wg, 'bg': bg, 'Wd': Wd, 'bd': bd}
    _L1_ffn_all = _L1_ffn_setup()
    _L1_ffn_in = {k: v for k, v in _L1_ffn_all.items() if k in ('W1', 'b1', 'Wg', 'bg', 'Wd', 'bd')}
    del _L1_ffn_all

    def _L2_attn_setup():
        import jax, jax.numpy as jnp
        import numpy as np
        HEAD_SIZE = 64
        HEAD_SIZE_R = HEAD_SIZE // 4
        HEAD_SIZE_C = HEAD_SIZE - HEAD_SIZE_R
        N_EMBD = 64

        def rope(x, start_pos=0):
            B, T, d = x.shape
            half = d // 2
            theta = 1.0 / 10000.0 ** (jnp.arange(half, dtype=x.dtype) / half)
            idx = jnp.arange(start_pos, start_pos + T, dtype=x.dtype)[:, None] * theta[None, :]
            sin, cos = (jnp.sin(idx), jnp.cos(idx))
            xs = x.reshape(B, T, half, 2)
            x1, x2 = (xs[..., 0], xs[..., 1])
            rot = jnp.stack([x1 * cos - x2 * sin, x1 * sin + x2 * cos], axis=-1)
            return rot.reshape(B, T, d)

        def _reference_tuple_inner(x, Wq_comp, Wkv_comp, Wqc, Wqr, Wkc, Wkr, Wv):
            c_q = x @ Wq_comp
            c_kv = x @ Wkv_comp
            q_c = c_q @ Wqc
            q_r = rope(c_q @ Wqr, start_pos=0)
            q = jnp.concatenate([q_c, q_r], axis=-1)
            k_c = c_kv @ Wkc
            k_r = rope(c_kv @ Wkr, start_pos=0)
            k = jnp.concatenate([k_c, k_r], axis=-1)
            v = c_kv @ Wv
            scale = 1.0 / jnp.sqrt(jnp.asarray(HEAD_SIZE, dtype=x.dtype))
            wei = jnp.einsum('bqd,bkd->bqk', q, k) * scale
            T_q = q.shape[1]
            mask = jnp.tril(jnp.ones((T_q, T_q), dtype=bool))
            wei = jnp.where(mask, wei, jnp.asarray(-jnp.inf, dtype=wei.dtype))
            wei = jax.nn.softmax(wei, axis=-1)
            out = jnp.einsum('bqk,bkd->bqd', wei, v)
            return (out, (k, v))
        key = jax.random.key(seed)
        ks = jax.random.split(key, 8)
        B, T = (32, 512)
        s = 0.05
        return {'x': jax.random.normal(ks[0], (B, T, N_EMBD), dtype=jnp.float32), 'Wq_comp': jax.random.normal(ks[1], (N_EMBD, N_EMBD), dtype=jnp.float32) * s, 'Wkv_comp': jax.random.normal(ks[2], (N_EMBD, N_EMBD), dtype=jnp.float32) * s, 'Wqc': jax.random.normal(ks[3], (N_EMBD, HEAD_SIZE_C), dtype=jnp.float32) * s, 'Wqr': jax.random.normal(ks[4], (N_EMBD, HEAD_SIZE_R), dtype=jnp.float32) * s, 'Wkc': jax.random.normal(ks[5], (N_EMBD, HEAD_SIZE_C), dtype=jnp.float32) * s, 'Wkr': jax.random.normal(ks[6], (N_EMBD, HEAD_SIZE_R), dtype=jnp.float32) * s, 'Wv': jax.random.normal(ks[7], (N_EMBD, HEAD_SIZE), dtype=jnp.float32) * s}
    _L2_attn_all = _L2_attn_setup()
    _L2_attn_in = {k: v for k, v in _L2_attn_all.items() if k in ('Wq_comp', 'Wkv_comp', 'Wqc', 'Wqr', 'Wkc', 'Wkr', 'Wv')}
    del _L2_attn_all

    def _L2_ffn_setup():
        import jax, jax.numpy as jnp
        import numpy as np
        DIM = 64
        HEADS = 8
        NUM_KEYS = 64
        NUM_KV = NUM_KEYS ** 2
        PK_TOPK = 16
        FINAL_TOPK = 16
        DIM_KEY = DIM // 2
        P = 2

        def _pk(x, Wq_pk, pk_keys):
            b, n, _ = x.shape
            q = (x @ Wq_pk).reshape(b, n, P, HEADS, DIM_KEY).transpose(2, 0, 1, 3, 4)
            sim = jnp.einsum('pbnhd,pkhd->pbnhk', q, pk_keys)
            scores, idx = jax.lax.top_k(sim, PK_TOPK)
            idx0 = idx[0]
            idx1 = idx[1] * NUM_KEYS
            index = (idx0[..., :, None] + idx1[..., None, :]).reshape(b, n, HEADS, PK_TOPK * PK_TOPK)
            score = (scores[0][..., :, None] + scores[1][..., None, :]).reshape(b, n, HEADS, PK_TOPK * PK_TOPK)
            final_scores, pk_idx = jax.lax.top_k(score, FINAL_TOPK)
            final_indices = jnp.take_along_axis(index, pk_idx, axis=-1)
            final_scores = jax.nn.softmax(final_scores, axis=-1)
            return (final_scores, final_indices)
        key = jax.random.key(seed)
        ks = jax.random.split(key, 7)
        b, n = (2, 256)
        std = 0.02
        x = jax.random.normal(ks[0], (b, n, DIM), dtype=jnp.float32)
        Wq_pk = jax.random.normal(ks[1], (DIM, P * HEADS * DIM_KEY), dtype=jnp.float32) * std
        pk_keys = jax.random.normal(ks[2], (P, NUM_KEYS, HEADS, DIM_KEY), dtype=jnp.float32) * std
        Wq = jax.random.normal(ks[3], (DIM, HEADS * DIM), dtype=jnp.float32) * std
        keys_table = jax.random.normal(ks[4], (NUM_KV * HEADS, DIM), dtype=jnp.float32) * std
        values_table = jax.random.normal(ks[5], (NUM_KV * HEADS, DIM), dtype=jnp.float32) * std
        Wo = jax.random.normal(ks[6], (DIM * HEADS, DIM), dtype=jnp.float32) * std
        return {'x': x, 'Wq_pk': Wq_pk, 'pk_keys': pk_keys, 'Wq': Wq, 'keys_table': keys_table, 'values_table': values_table, 'Wo': Wo}
    _L2_ffn_all = _L2_ffn_setup()
    _L2_ffn_in = {k: v for k, v in _L2_ffn_all.items() if k in ('Wq_pk', 'pk_keys', 'Wq', 'keys_table', 'values_table', 'Wo')}
    del _L2_ffn_all

    def _L3_attn_setup():
        import jax, jax.numpy as jnp
        import numpy as np
        NHEAD = 8
        ATT_EPS = 1e-06
        LN_EPS = 1e-05

        def _layernorm(x, g, b):
            mu = jnp.mean(x, axis=-1, keepdims=True)
            var = jnp.mean(jnp.square(x - mu), axis=-1, keepdims=True)
            return (x - mu) * jax.lax.rsqrt(var + LN_EPS) * g + b
        key = jax.random.key(seed)
        ks = jax.random.split(key, 7)
        N, L, C = (4, 4096, 64)
        s = 1.0 / np.sqrt(C)
        return {'x': jax.random.normal(ks[0], (N, L, C), jnp.float32), 'Wq': jax.random.normal(ks[1], (C, C), jnp.float32) * s, 'Wk': jax.random.normal(ks[2], (C, C), jnp.float32) * s, 'Wv': jax.random.normal(ks[3], (C, C), jnp.float32) * s, 'Wm': jax.random.normal(ks[4], (C, C), jnp.float32) * s, 'W1': jax.random.normal(ks[5], (2 * C, 2 * C), jnp.float32) * (1.0 / np.sqrt(2 * C)), 'W2': jax.random.normal(ks[6], (2 * C, C), jnp.float32) * (1.0 / np.sqrt(2 * C)), 'g1': jnp.ones((C,), jnp.float32), 'b1': jnp.zeros((C,), jnp.float32), 'g2': jnp.ones((C,), jnp.float32), 'b2': jnp.zeros((C,), jnp.float32)}
    _L3_attn_all = _L3_attn_setup()
    _L3_attn_in = {k: v for k, v in _L3_attn_all.items() if k in ('Wq', 'Wk', 'Wv', 'Wm', 'W1', 'W2', 'g1', 'b1', 'g2', 'b2')}
    del _L3_attn_all

    def _L3_ffn_setup():
        import jax, jax.numpy as jnp
        import numpy as np
        B, S, D = (8, 1024, 64)
        H = 4 * D
        CAPACITY = 0.5
        key = jax.random.key(seed)
        ks = jax.random.split(key, 6)
        x = jax.random.normal(ks[0], (B, S, D), dtype=jnp.float32)
        attention_mask = jnp.zeros((B, 1, 1, S), dtype=jnp.float32)
        wr = jax.random.normal(ks[1], (D, 1), dtype=jnp.float32) * 0.02
        br = jnp.zeros((1,), dtype=jnp.float32)
        w1 = jax.random.normal(ks[2], (D, H), dtype=jnp.float32) * 0.02
        b1 = jnp.zeros((H,), dtype=jnp.float32)
        w2 = jax.random.normal(ks[3], (H, D), dtype=jnp.float32) * 0.02
        b2 = jnp.zeros((D,), dtype=jnp.float32)
        return {'x': x, 'attention_mask': attention_mask, 'wr': wr, 'br': br, 'w1': w1, 'b1': b1, 'w2': w2, 'b2': b2}
    _L3_ffn_all = _L3_ffn_setup()
    _L3_ffn_in = {k: v for k, v in _L3_ffn_all.items() if k in ('attention_mask', 'wr', 'br', 'w1', 'b1', 'w2', 'b2')}
    del _L3_ffn_all
    return {'x': x, 'L0_tok_W_qry': _L0_tok_in['W_qry'], 'L0_tok_W_key': _L0_tok_in['W_key'], 'L0_tok_v': _L0_tok_in['v'], 'L0_tok_b': _L0_tok_in['b'], 'L0_attn_Wq': _L0_attn_in['Wq'], 'L0_attn_Wk': _L0_attn_in['Wk'], 'L0_ffn_gate_w': _L0_ffn_in['gate_w'], 'L0_ffn_lattice_weights': _L0_ffn_in['lattice_weights'], 'L0_ffn_out_w': _L0_ffn_in['out_w'], 'L0_ffn_out_b': _L0_ffn_in['out_b'], 'L0_ffn_ln_g': _L0_ffn_in['ln_g'], 'L0_ffn_ln_b': _L0_ffn_in['ln_b'], 'L1_attn_W_qkv': _L1_attn_in['W_qkv'], 'L1_attn_b_qkv': _L1_attn_in['b_qkv'], 'L1_attn_kln_w': _L1_attn_in['kln_w'], 'L1_attn_kln_b': _L1_attn_in['kln_b'], 'L1_attn_vln_w': _L1_attn_in['vln_w'], 'L1_attn_vln_b': _L1_attn_in['vln_b'], 'L1_attn_W_proj': _L1_attn_in['W_proj'], 'L1_attn_b_proj': _L1_attn_in['b_proj'], 'L1_ffn_W1': _L1_ffn_in['W1'], 'L1_ffn_b1': _L1_ffn_in['b1'], 'L1_ffn_Wg': _L1_ffn_in['Wg'], 'L1_ffn_bg': _L1_ffn_in['bg'], 'L1_ffn_Wd': _L1_ffn_in['Wd'], 'L1_ffn_bd': _L1_ffn_in['bd'], 'L2_attn_Wq_comp': _L2_attn_in['Wq_comp'], 'L2_attn_Wkv_comp': _L2_attn_in['Wkv_comp'], 'L2_attn_Wqc': _L2_attn_in['Wqc'], 'L2_attn_Wqr': _L2_attn_in['Wqr'], 'L2_attn_Wkc': _L2_attn_in['Wkc'], 'L2_attn_Wkr': _L2_attn_in['Wkr'], 'L2_attn_Wv': _L2_attn_in['Wv'], 'L2_ffn_Wq_pk': _L2_ffn_in['Wq_pk'], 'L2_ffn_pk_keys': _L2_ffn_in['pk_keys'], 'L2_ffn_Wq': _L2_ffn_in['Wq'], 'L2_ffn_keys_table': _L2_ffn_in['keys_table'], 'L2_ffn_values_table': _L2_ffn_in['values_table'], 'L2_ffn_Wo': _L2_ffn_in['Wo'], 'L3_attn_Wq': _L3_attn_in['Wq'], 'L3_attn_Wk': _L3_attn_in['Wk'], 'L3_attn_Wv': _L3_attn_in['Wv'], 'L3_attn_Wm': _L3_attn_in['Wm'], 'L3_attn_W1': _L3_attn_in['W1'], 'L3_attn_W2': _L3_attn_in['W2'], 'L3_attn_g1': _L3_attn_in['g1'], 'L3_attn_b1': _L3_attn_in['b1'], 'L3_attn_g2': _L3_attn_in['g2'], 'L3_attn_b2': _L3_attn_in['b2'], 'L3_ffn_attention_mask': _L3_ffn_in['attention_mask'], 'L3_ffn_wr': _L3_ffn_in['wr'], 'L3_ffn_br': _L3_ffn_in['br'], 'L3_ffn_w1': _L3_ffn_in['w1'], 'L3_ffn_b1': _L3_ffn_in['b1'], 'L3_ffn_w2': _L3_ffn_in['w2'], 'L3_ffn_b2': _L3_ffn_in['b2']}

def reference(x, L0_tok_W_qry, L0_tok_W_key, L0_tok_v, L0_tok_b, L0_attn_Wq, L0_attn_Wk, L0_ffn_gate_w, L0_ffn_lattice_weights, L0_ffn_out_w, L0_ffn_out_b, L0_ffn_ln_g, L0_ffn_ln_b, L1_attn_W_qkv, L1_attn_b_qkv, L1_attn_kln_w, L1_attn_kln_b, L1_attn_vln_w, L1_attn_vln_b, L1_attn_W_proj, L1_attn_b_proj, L1_ffn_W1, L1_ffn_b1, L1_ffn_Wg, L1_ffn_bg, L1_ffn_Wd, L1_ffn_bd, L2_attn_Wq_comp, L2_attn_Wkv_comp, L2_attn_Wqc, L2_attn_Wqr, L2_attn_Wkc, L2_attn_Wkr, L2_attn_Wv, L2_ffn_Wq_pk, L2_ffn_pk_keys, L2_ffn_Wq, L2_ffn_keys_table, L2_ffn_values_table, L2_ffn_Wo, L3_attn_Wq, L3_attn_Wk, L3_attn_Wv, L3_attn_Wm, L3_attn_W1, L3_attn_W2, L3_attn_g1, L3_attn_b1, L3_attn_g2, L3_attn_b2, L3_ffn_attention_mask, L3_ffn_wr, L3_ffn_br, L3_ffn_w1, L3_ffn_b1, L3_ffn_w2, L3_ffn_b2):
    import jax
    import jax.numpy as jnp

    def _L0_tok_ref(x, W_qry, W_key, v, b):
        import jax, jax.numpy as jnp
        import numpy as np
        WIN = 9
        N, L, C = x.shape
        n_w = L - WIN + 1
        idx = jnp.arange(n_w)[:, None] + jnp.arange(WIN)[None, :]
        x_win = x[:, idx]
        x_ctr = x[:, WIN // 2:WIN // 2 + n_w]
        key = jnp.einsum('nwsc,cu->nwsu', x_win, W_key)
        qry = jnp.einsum('nwc,cu->nwu', x_ctr, W_qry)
        score = jnp.einsum('nwsu,u->nws', jnp.tanh(qry[:, :, None, :] + key + b), v)
        weight = jax.nn.softmax(score, axis=2)
        out = jnp.einsum('nwsc,nws->nwc', x_win, weight)
        return out

    def _L0_attn_ref(x, Wq, Wk):
        import jax, jax.numpy as jnp
        import numpy as np
        d = x.shape[-1]
        scale = d ** (-0.5)
        q = jnp.einsum('bnd,ed->bne', x, Wq)
        k = jnp.einsum('bnd,ed->bne', x, Wk)
        sim = jnp.einsum('bid,bjd->bij', q, k) * scale
        attn = jax.nn.softmax(sim, axis=-1)
        out = jnp.einsum('bij,bjd->bid', attn, x)
        return out

    def _L0_ffn_ref(x, gate_w, lattice_weights, out_w, out_b, ln_g, ln_b):
        import jax, jax.numpy as jnp
        import numpy as np
        TOP_K = 6
        LN_EPS = 1e-05
        logits = jnp.einsum('bsd,ed->bse', x, gate_w)
        top_logits, indices = jax.lax.top_k(logits, TOP_K)
        scores = jax.nn.softmax(top_logits, axis=-1)
        W_sel = lattice_weights[indices]
        xW = jnp.einsum('bsd,bskde->bske', x, W_sel)
        lattice_out = jnp.einsum('bske,bsk->bse', xW, scores)
        proj = jnp.einsum('bsd,ed->bse', lattice_out, out_w) + out_b
        h = x + proj
        mu = jnp.mean(h, axis=-1, keepdims=True)
        var = jnp.mean(jnp.square(h - mu), axis=-1, keepdims=True)
        return (h - mu) * jax.lax.rsqrt(var + LN_EPS) * ln_g + ln_b

    def _L1_attn_ref(x, W_qkv, b_qkv, kln_w, kln_b, vln_w, vln_b, W_proj, b_proj):
        import jax, jax.numpy as jnp
        import numpy as np
        MIDC = 64
        HEADS = 16
        HEADC = MIDC // HEADS
        EPS = 1e-05

        def _layernorm(x, w, b):
            mean = jnp.mean(x, axis=-1, keepdims=True)
            std = jnp.std(x, axis=-1, keepdims=True, ddof=1)
            return w * (x - mean) / (std + EPS) + b
        B, HW, C = x.shape
        bias = x
        qkv = jnp.einsum('bnc,oc->bno', x, W_qkv) + b_qkv
        qkv = qkv.reshape(B, HW, HEADS, 3 * HEADC).transpose(0, 2, 1, 3)
        q, k, v = jnp.split(qkv, 3, axis=-1)
        k = _layernorm(k, kln_w, kln_b)
        v = _layernorm(v, vln_w, vln_b)
        kv = jnp.einsum('bhnd,bhne->bhde', k, v) / HW
        out = jnp.einsum('bhnd,bhde->bhne', q, kv)
        out = out.transpose(0, 2, 1, 3).reshape(B, HW, C)
        ret = out + bias
        proj = jnp.einsum('bnc,oc->bno', ret, W_proj) + b_proj
        return jax.nn.gelu(proj, approximate=False) + bias

    def _L1_ffn_ref(x, W1, b1, Wg, bg, Wd, bd):
        import jax, jax.numpy as jnp
        import numpy as np
        C = 64
        HID = 256
        E = 8
        TEMP = 1.0
        orig_shape = x.shape
        xf = x.reshape(-1, orig_shape[-1])
        H = jax.nn.gelu(xf @ W1 + b1, approximate=False)
        probs = jax.nn.softmax((H @ Wg + bg) / TEMP, axis=-1)
        assign = jnp.argmax(probs, axis=-1)
        out = jnp.zeros_like(xf)
        for e in range(Wd.shape[0]):
            y = H @ Wd[e] + bd[e]
            sel = (assign == e)[:, None]
            out = out + jnp.where(sel, probs[:, e:e + 1] * y, 0.0)
        return out.reshape(orig_shape)

    def _L2_attn_ref(x, Wq_comp, Wkv_comp, Wqc, Wqr, Wkc, Wkr, Wv):
        import jax, jax.numpy as jnp
        import numpy as np
        HEAD_SIZE = 64
        HEAD_SIZE_R = HEAD_SIZE // 4
        HEAD_SIZE_C = HEAD_SIZE - HEAD_SIZE_R
        N_EMBD = 64

        def rope(x, start_pos=0):
            B, T, d = x.shape
            half = d // 2
            theta = 1.0 / 10000.0 ** (jnp.arange(half, dtype=x.dtype) / half)
            idx = jnp.arange(start_pos, start_pos + T, dtype=x.dtype)[:, None] * theta[None, :]
            sin, cos = (jnp.sin(idx), jnp.cos(idx))
            xs = x.reshape(B, T, half, 2)
            x1, x2 = (xs[..., 0], xs[..., 1])
            rot = jnp.stack([x1 * cos - x2 * sin, x1 * sin + x2 * cos], axis=-1)
            return rot.reshape(B, T, d)

        def _reference_tuple_inner(x, Wq_comp, Wkv_comp, Wqc, Wqr, Wkc, Wkr, Wv):
            c_q = x @ Wq_comp
            c_kv = x @ Wkv_comp
            q_c = c_q @ Wqc
            q_r = rope(c_q @ Wqr, start_pos=0)
            q = jnp.concatenate([q_c, q_r], axis=-1)
            k_c = c_kv @ Wkc
            k_r = rope(c_kv @ Wkr, start_pos=0)
            k = jnp.concatenate([k_c, k_r], axis=-1)
            v = c_kv @ Wv
            scale = 1.0 / jnp.sqrt(jnp.asarray(HEAD_SIZE, dtype=x.dtype))
            wei = jnp.einsum('bqd,bkd->bqk', q, k) * scale
            T_q = q.shape[1]
            mask = jnp.tril(jnp.ones((T_q, T_q), dtype=bool))
            wei = jnp.where(mask, wei, jnp.asarray(-jnp.inf, dtype=wei.dtype))
            wei = jax.nn.softmax(wei, axis=-1)
            out = jnp.einsum('bqk,bkd->bqd', wei, v)
            return (out, (k, v))
        return _reference_tuple_inner(x, Wq_comp, Wkv_comp, Wqc, Wqr, Wkc, Wkr, Wv)[0]

    def _L2_ffn_ref(x, Wq_pk, pk_keys, Wq, keys_table, values_table, Wo):
        import jax, jax.numpy as jnp
        import numpy as np
        DIM = 64
        HEADS = 8
        NUM_KEYS = 64
        NUM_KV = NUM_KEYS ** 2
        PK_TOPK = 16
        FINAL_TOPK = 16
        DIM_KEY = DIM // 2
        P = 2

        def _pk(x, Wq_pk, pk_keys):
            b, n, _ = x.shape
            q = (x @ Wq_pk).reshape(b, n, P, HEADS, DIM_KEY).transpose(2, 0, 1, 3, 4)
            sim = jnp.einsum('pbnhd,pkhd->pbnhk', q, pk_keys)
            scores, idx = jax.lax.top_k(sim, PK_TOPK)
            idx0 = idx[0]
            idx1 = idx[1] * NUM_KEYS
            index = (idx0[..., :, None] + idx1[..., None, :]).reshape(b, n, HEADS, PK_TOPK * PK_TOPK)
            score = (scores[0][..., :, None] + scores[1][..., None, :]).reshape(b, n, HEADS, PK_TOPK * PK_TOPK)
            final_scores, pk_idx = jax.lax.top_k(score, FINAL_TOPK)
            final_indices = jnp.take_along_axis(index, pk_idx, axis=-1)
            final_scores = jax.nn.softmax(final_scores, axis=-1)
            return (final_scores, final_indices)
        b, n, d = x.shape
        q = (x @ Wq).reshape(b, n, HEADS, DIM) * DIM ** (-0.5)
        kv_scores, indices = _pk(x, Wq_pk, pk_keys)
        offsets = jnp.arange(HEADS, dtype=indices.dtype) * NUM_KV
        ind = indices + offsets[None, None, :, None]
        k = jnp.einsum('bnhk,bnhkd->bnhd', kv_scores, keys_table[ind])
        v = jnp.einsum('bnhk,bnhkd->bnhd', kv_scores, values_table[ind])
        sim = jnp.einsum('bihd,bjhd->bhij', q, k)
        neg = -jnp.finfo(sim.dtype).max
        causal = jnp.tril(jnp.ones((n, n), dtype=bool))
        sim = jnp.where(causal, sim, neg)
        attn = jax.nn.softmax(sim, axis=-1)
        out = jnp.einsum('bhij,bjhd->bhid', attn, v)
        out = out.transpose(0, 2, 1, 3).reshape(b, n, HEADS * DIM)
        return out @ Wo

    def _L3_attn_ref(x, Wq, Wk, Wv, Wm, W1, W2, g1, b1, g2, b2):
        import jax, jax.numpy as jnp
        import numpy as np
        NHEAD = 8
        ATT_EPS = 1e-06
        LN_EPS = 1e-05

        def _layernorm(x, g, b):
            mu = jnp.mean(x, axis=-1, keepdims=True)
            var = jnp.mean(jnp.square(x - mu), axis=-1, keepdims=True)
            return (x - mu) * jax.lax.rsqrt(var + LN_EPS) * g + b
        N, L, C = x.shape
        H = NHEAD
        D = C // H
        q = (x @ Wq).reshape(N, L, H, D)
        k = (x @ Wk).reshape(N, L, H, D)
        v = (x @ Wv).reshape(N, L, H, D)
        Q = jax.nn.elu(q) + 1.0
        K = jax.nn.elu(k) + 1.0
        v = v / L
        KV = jnp.einsum('nshd,nshv->nhdv', K, v)
        Z = 1.0 / (jnp.einsum('nlhd,nhd->nlh', Q, K.sum(axis=1)) + ATT_EPS)
        msg = jnp.einsum('nlhd,nhdv,nlh->nlhv', Q, KV, Z) * L
        msg = msg.reshape(N, L, C) @ Wm
        msg = _layernorm(msg, g1, b1)
        h = jnp.concatenate([x, msg], axis=-1) @ W1
        h = jax.nn.relu(h) @ W2
        msg = _layernorm(h, g2, b2)
        return x + msg

    def _L3_ffn_ref(x, attention_mask, wr, br, w1, b1, w2, b2):
        import jax, jax.numpy as jnp
        import numpy as np
        B, S, D = (8, 1024, 64)
        H = 4 * D
        CAPACITY = 0.5
        b, s, d = x.shape
        weights = (jnp.einsum('bsd,do->bso', x, wr) + br)[..., 0]
        k = max(1, int(CAPACITY * s))
        kk = k - 1 if k > 1 else 1
        _, idx = jax.lax.top_k(weights, k)
        sel_idx = idx[:, :kk]
        sel = jnp.take_along_axis(x, sel_idx[:, :, None], axis=1)
        h = jax.nn.gelu(jnp.einsum('bkd,dh->bkh', sel, w1) + b1)
        y = jnp.einsum('bkh,hd->bkd', h, w2) + b2
        w_sel = jnp.take_along_axis(weights, sel_idx, axis=1)
        y = y * w_sel[..., None]
        batch_idx = jnp.arange(b)[:, None]
        processed = jnp.zeros_like(x).at[batch_idx, sel_idx].set(y)
        return processed + x
    h = _L0_tok_ref(x, L0_tok_W_qry, L0_tok_W_key, L0_tok_v, L0_tok_b)
    h = h + _L0_attn_ref(_layernorm(h, axis=-1), L0_attn_Wq, L0_attn_Wk)
    h = h + _L0_ffn_ref(_layernorm(h, axis=-1), L0_ffn_gate_w, L0_ffn_lattice_weights, L0_ffn_out_w, L0_ffn_out_b, L0_ffn_ln_g, L0_ffn_ln_b)
    h = h + _L1_attn_ref(_layernorm(h, axis=-1), L1_attn_W_qkv, L1_attn_b_qkv, L1_attn_kln_w, L1_attn_kln_b, L1_attn_vln_w, L1_attn_vln_b, L1_attn_W_proj, L1_attn_b_proj)
    h = h + _L1_ffn_ref(_layernorm(h, axis=-1), L1_ffn_W1, L1_ffn_b1, L1_ffn_Wg, L1_ffn_bg, L1_ffn_Wd, L1_ffn_bd)
    h = h + _L2_attn_ref(_layernorm(h, axis=-1), L2_attn_Wq_comp, L2_attn_Wkv_comp, L2_attn_Wqc, L2_attn_Wqr, L2_attn_Wkc, L2_attn_Wkr, L2_attn_Wv)
    h = h + _L2_ffn_ref(_layernorm(h, axis=-1), L2_ffn_Wq_pk, L2_ffn_pk_keys, L2_ffn_Wq, L2_ffn_keys_table, L2_ffn_values_table, L2_ffn_Wo)
    h = h + _L3_attn_ref(_layernorm(h, axis=-1), L3_attn_Wq, L3_attn_Wk, L3_attn_Wv, L3_attn_Wm, L3_attn_W1, L3_attn_W2, L3_attn_g1, L3_attn_b1, L3_attn_g2, L3_attn_b2)
    h = h + _L3_ffn_ref(_layernorm(h, axis=-1), L3_ffn_attention_mask, L3_ffn_wr, L3_ffn_br, L3_ffn_w1, L3_ffn_b1, L3_ffn_w2, L3_ffn_b2)
    return h

_drawn_inputs = setup_inputs


def setup_inputs(seed=0):
    import zlib

    import numpy as np

    out = dict(_drawn_inputs(seed))
    spreads = {'L0_tok_b': (0.0, 0.8),
     'L0_ffn_out_b': (0.0, 0.1),
     'L0_ffn_ln_g': (1.0, 0.2),
     'L0_ffn_ln_b': (0.0, 0.1),
     'L1_attn_b_qkv': (0.0, 0.8),
     'L1_attn_kln_w': (1.0, 0.6),
     'L1_attn_kln_b': (0.0, 0.8),
     'L1_attn_vln_w': (1.0, 0.6),
     'L1_attn_vln_b': (0.0, 0.8),
     'L1_attn_b_proj': (0.0, 0.417),
     'L1_ffn_b1': (0.0, 0.8),
     'L1_ffn_bg': (0.0, 0.8),
     'L1_ffn_bd': (0.0, 0.8),
     'L3_attn_g1': (1.0, 0.2),
     'L3_attn_b1': (0.0, 0.397),
     'L3_attn_g2': (1.0, 0.2),
     'L3_attn_b2': (0.0, 0.288),
     'L3_ffn_b1': (0.0, 0.8),
     'L3_ffn_b2': (0.0, 0.8)}
    factors = {'L0_ffn_gate_w': 8.0,
     'L0_ffn_lattice_weights': 7.967,
     'L0_ffn_out_w': 7.831,
     'L1_attn_W_qkv': 8.0,
     'L1_ffn_W1': 8.0,
     'L1_ffn_Wg': 8.0,
     'L1_ffn_Wd': 8.0,
     'L2_attn_Wq_comp': 8.0,
     'L2_attn_Wqc': 8.0,
     'L2_attn_Wqr': 8.0,
     'L2_attn_Wkc': 8.0,
     'L2_attn_Wkr': 8.0,
     'L2_ffn_Wq_pk': 8.0,
     'L2_ffn_pk_keys': 8.0,
     'L2_ffn_Wq': 64.0,
     'L2_ffn_keys_table': 64.0,
     'L2_ffn_values_table': 8.0,
     'L2_ffn_Wo': 8.0,
     'L3_attn_Wq': 5.826,
     'L3_attn_Wk': 3.393,
     'L3_ffn_wr': 8.0,
     'L3_ffn_w1': 8.0,
     'L3_ffn_w2': 8.0}
    for name, (base, spread) in spreads.items():
        noise = np.random.default_rng([zlib.crc32(name.encode()), seed]).standard_normal(out[name].shape)
        drawn = base * np.exp(spread * noise) if base else spread * noise
        out[name] = jnp.asarray(drawn.astype(out[name].dtype))
    for name, factor in factors.items():
        out[name] = (out[name] * factor).astype(out[name].dtype)
    return out
```

```python
from contextlib import ExitStack

import numpy as np
import concourse.bass as bass
from concourse import mybir

B, T_IN, C = 16, 250, 64
WIN = 9
T = T_IN - WIN + 1
P = T // 2
TOPK_E, EXPERTS0 = 6, 64
H1, D1 = 16, 4
HID, E1 = 256, 8
ROPE = 16
H2, NK, PK = 8, 64, 16
NKV = NK * NK
H3, D3 = 8, 8
CAP = T // 2 - 1
SLOTS = 8
NEG = -3.0e38

CAND, n_cand = [], 0
for i0, i1 in ((0, 1), (1, 2), (2, 3), (3, 4), (4, 5), (5, 8), (8, 16)):
    CAND.append((i0, i1, PK // (i0 + 1), n_cand))
    n_cand += (i1 - i0) * (PK // (i0 + 1))

W64 = [("tok_key", 64), ("tok_qry2", 128), ("l0_wq", 64), ("l0_wk", 64), ("gate", 64), ("out_w", 64),
       ("l1_q", 64), ("l1_kv", 128), ("l1_proj", 64), ("l1_w1", HID), ("qcomp", 64), ("kvcomp", 64),
       ("q_rcs", 80), ("kv_rcsv", 144), ("l2f_q", 512), ("l2f_o", 512), ("l3_q", 64), ("l3_k", 64),
       ("l3_v", 64), ("l3_m", 64), ("l3_w1x", 128), ("l3_w1m", 128), ("cap_w1", HID), ("cap_wr", P)]
W128 = [("tok_v", 2), ("tok_b", 1), ("l1_bq", 1), ("l1_b1", 2), ("cap_b1", 2), ("l1_wg", 2 * E1),
        ("l1_wd", 2 * E1 * C), ("l3_w2", C), ("cap_w2", 2 * C)]
ROWS = [("out_b", 64), ("ln_g", 64), ("ln_b", 64), ("l1_bkv", 128), ("l1_w", 128), ("l1_b", 128),
        ("l1_bproj", 64), ("l1_bg", E1), ("g1", 64), ("b1", 64), ("g2", 64), ("b2", 64),
        ("cap_b2", 64), ("cap_br", 1), ("bd", E1 * C)]
CONST = [("ident", 128), ("causal", 2 * T), ("tri", 2 * T), ("own", 2 * T), ("iota", n_cand),
         ("head_base", H2), ("cos", T), ("sin", T), ("mask1", 64), ("mask3", 72), ("ones", P)]


def places(table):
    out, at = {}, 0
    for name, n in table:
        out[name] = (at, at + n)
        at += n
    return out, at


class Count:

    def __init__(self):
        self.values, self.steps = {}, 0

    def __call__(self, sem, n=1):
        self.values[sem.name] = self.values.get(sem.name, 0) + n
        return self.values[sem.name]

    def one(self):
        self.steps += 1
        return 1


def tower(nc, x, xT, w64, w128, lattice, pk_q, pk_k, rows, const, table, out):
    fp32, u32 = mybir.dt.float32, mybir.dt.uint32
    ALU, ACT, AX = mybir.AluOpType, mybir.ActivationFunctionType, mybir.AxisListType
    p64, n64 = places(W64)
    p128, n128 = places(W128)
    prow, nrow = places(ROWS)
    pconst, nconst = places(CONST)
    ctx = ExitStack()

    def sb(name, shape, dt=fp32):
        return ctx.enter_context(nc.sbuf_tensor(name, shape, dt))

    with ctx:
        w64_sb, w128_sb = sb("w64_sb", [64, n64]), sb("w128_sb", [128, n128])
        rows_sb, const_sb = sb("rows_sb", [P, nrow]), sb("const_sb", [128, nconst])
        pk_sb = sb("pk_sb", [32, 2, 16 * 64])
        l0_a = sb("l0_a", [64, 64])
        latt = sb("latt", [64, EXPERTS0 * C])
        l2_qw, l2_kvw = sb("l2_qw", [64, 80]), sb("l2_kvw", [64, 144])
        pk_w = sb("pk_w", [64, 16 * NK])
        hF, hG, hB = sb("hF", [P, 2, C]), sb("hG", [P, 2, C]), sb("hB", [P, 2, C])
        yTF, yTG, yTB = sb("yTF", [C, T]), sb("yTG", [C, T]), sb("yTB", [C, T])
        idxF, idxG = sb("idxF", [P, 2, H2, PK], u32), sb("idxG", [P, 2, H2, PK], u32)
        wgtF, wgtG = sb("wgtF", [P, 2, H2, PK]), sb("wgtG", [P, 2, H2, PK])
        rowbuf = sb("rowbuf", [P, SLOTS, PK, 2 * C])
        kv = sb("kv", [P, 2, H2, 2 * C])
        odd = sb("odd", [P, 2 * C])
        xT_sb, xwin = sb("xT_sb", [C, T_IN]), sb("xwin", [P, 2, WIN * C])
        e9, s2 = sb("e9", [P, 2, WIN]), sb("s2", [P, 4, 2])
        y, yT = sb("y", [P, 2, C]), sb("yT", [C, T])
        stat, mv, std, rstd = sb("stat", [P, 2, 6]), sb("mv", [P, 2, 2]), sb("std", [P, 2]), sb("rstd", [P, 2])
        qT, kT = sb("qT", [C, 2, T]), sb("kT", [C, 2, T])
        sm, pr, prT = sb("sm", [P, 2, T]), sb("pr", [P, 2, 2 * T]), sb("prT", [P, 2, 2 * T])
        nmax, rsum, rinv = sb("nmax", [P, 2, 2]), sb("rsum", [P, 2, 2]), sb("rinv", [P, 2, 2])
        lg, m8, rep, sc = sb("lg", [P, 2, 64]), sb("m8", [P, 2, 8]), sb("rep", [P, 2, 64]), sb("sc", [P, 2, 64])
        lw = sb("lw", [P, 4, 512])
        t64, u64 = sb("t64", [P, 2, 2 * C]), sb("u64", [P, 2, 2 * C])
        kvn = sb("kvn", [P, 2, 2 * C])
        g64 = sb("g64", [P, 2, 32])
        m64 = sb("m64", [64, 72])
        actT = sb("actT", [128, 2, T])
        rope2 = sb("rope2", [ROPE, 2, T])
        v_sb = sb("v_sb", [P, 2, 72])
        pks_all = sb("pks_all", [128, 2 * 16 * NK])
        pks = pks_all[0:P].rearrange("p (t n) -> p t n", t=2)
        th = pks_all[:, 0:5 * T].rearrange("p (n t) -> p n t", n=5)
        pkr = xwin[:].rearrange("p t n -> p (t n)")[:, 0:16 * NK]
        v16, i16, f16 = sb("v16", [P, 16, PK]), sb("i16", [P, 16, PK], u32), sb("f16", [P, 16, PK])
        cs, cr, ci = sb("cs", [P, H2, n_cand]), sb("cr", [P, H2, n_cand]), sb("ci", [P, H2, n_cand])
        bv, bi, bf = sb("bv", [P, H2, PK]), sb("bi", [P, H2, PK], u32), sb("bf", [P, H2, PK])
        hot = lw[:].rearrange("p a b -> p (a b)")[:, 0:2 * PK * n_cand].rearrange("p (k n) -> p k n", n=n_cand)
        outT = sb("outT", [C, H2, T])
        cnt = sb("cnt", [P, 8])
        ps = [ctx.enter_context(nc.psum_tensor(f"ps{i}", [128, 512], fp32)) for i in range(8)]

        def W(name, lo=0, n=None):
            a, b = p64[name]
            return w64_sb[:, a + lo:(a + lo + n if n else b)]

        def V(name):
            a, b = p128[name]
            return w128_sb[:, a:b]

        def R(name):
            a, b = prow[name]
            return rows_sb[:, a:b]

        def K(name, parts=P):
            a, b = pconst[name]
            return const_sb[0:parts, a:b]

        def two(row):
            return row.unsqueeze(1).broadcast_to([P, 2, row.shape[1]])

        def tile(t):
            return slice(t * P, (t + 1) * P)

        def sem(name):
            return ctx.enter_context(nc.semaphore(name))

        s_x_loaded = sem("x_loaded")
        s_dve = sem("dve")
        s_act = sem("act")
        s_ln_var = sem("ln_var")
        s_ln_std = sem("ln_std")
        s_ln_y = sem("ln_y")
        s_ln_yT = sem("ln_yT")
        s_yT_ready = sem("yT_ready")
        s_tok_z = sem("tok_z")
        s_tok_tanh = sem("tok_tanh")
        s_tok_score = sem("tok_score")
        s_tok_shift = sem("tok_shift")
        s_tok_exp = sem("tok_exp")
        s_h_ready = sem("h_ready")
        s_att_gT = sem("att_gT")
        s_att_qk = sem("att_qk")
        s_att_sim = sem("att_sim")
        s_att_max = sem("att_max")
        s_att_exp = sem("att_exp")
        s_att_pT = sem("att_pT")
        s_att_pTc = sem("att_pTc")
        s_att_out = sem("att_out")
        s_att_done = sem("att_done")
        s_l0_logit = sem("l0_logit")
        s_l0_shift = sem("l0_shift")
        s_l0_e = sem("l0_e")
        s_l0_xw = sem("l0_xw")
        s_l0_prod = sem("l0_prod")
        s_l0_sum = sem("l0_sum")
        s_l1_qkv = sem("l1_qkv")
        s_l1_q = sem("l1_q")
        s_l1_var = sem("l1_var")
        s_l1_std = sem("l1_std")
        s_l1_kvn = sem("l1_kvn")
        s_l1_kv = sem("l1_kv")
        s_l1_m = sem("l1_m")
        s_l1_attT = sem("l1_attT")
        s_l1_ret = sem("l1_ret")
        s_l1_proj = sem("l1_proj")
        s_l1_pre = sem("l1_pre")
        s_l1_gelu = sem("l1_gelu")
        s_e_hT = sem("e_hT")
        s_e_act = sem("e_act")
        s_e_gate = sem("e_gate")
        s_e_shift = sem("e_shift")
        s_e_exp = sem("e_exp")
        s_e_y = sem("e_y")
        s_e_used = sem("e_used")
        s_l2_qkv = sem("l2_qkv")
        s_l2_rope = sem("l2_rope")
        s_l2_v = sem("l2_v")
        s_pk_sim = sem("pk_sim")
        s_pk_copied = sem("pk_copied")
        s_pk_shift = sem("pk_shift")
        s_pk_exp = sem("pk_exp")
        s_m_prep = sem("m_prep")
        s_m_copied = sem("m_copied")
        s_m_sim = sem("m_sim")
        s_m_max = sem("m_max")
        s_m_exp = sem("m_exp")
        s_m_norm = sem("m_norm")
        s_m_pT = sem("m_pT")
        s_m_pTc = sem("m_pTc")
        s_m_oT = sem("m_oT")
        s_m_oTc = sem("m_oTc")
        s_m_out = sem("m_out")
        s_l3_q = sem("l3_q")
        s_l3_kv = sem("l3_kv")
        s_l3_pre = sem("l3_pre")
        s_l3_exp = sem("l3_exp")
        s_l3_elu = sem("l3_elu")
        s_l3_kvs = sem("l3_kvs")
        s_l3_m = sem("l3_m")
        s_l3_num = sem("l3_num")
        s_l3_msg = sem("l3_msg")
        s_l3_msgT = sem("l3_msgT")
        s_l3_msgTc = sem("l3_msgTc")
        s_l3_mm = sem("l3_mm")
        s_l3_msg2 = sem("l3_msg2")
        s_l3_hT = sem("l3_hT")
        s_l3_relu = sem("l3_relu")
        s_l3_h = sem("l3_h")
        s_c_w = sem("c_w")
        s_c_hT = sem("c_hT")
        s_c_act = sem("c_act")
        s_c_y = sem("c_y")
        s_c_out = sem("c_out")
        s_kv_summed = sem("kv_summed")
        s_stored = sem("stored")
        s_setup = sem("setup")
        fetched = [ctx.enter_context(nc.semaphore(f"fetched{i}")) for i in range(SLOTS)]
        cleared = range(s_x_loaded.num, s_setup.num + 1)

        def ln_vector(dve, seen, h, dst):
            for t in range(2):
                nc.vector.bn_stats(stat[:, t], h[:, t]).then_inc(s_dve, seen.one())
            dve.wait_ge(s_dve, seen.steps)
            nc.vector.bn_aggr(mv[:, 0], stat[:, 0])
            nc.vector.bn_aggr(mv[:, 1], stat[:, 1]).then_inc(s_ln_var, 1)
            dve.wait_ge(s_ln_std, seen(s_ln_std))
            nc.vector.reciprocal(rstd[:], std[:]).then_inc(s_dve, seen.one())
            dve.wait_ge(s_dve, seen.steps)
            for t in range(2):
                last = nc.vector.tensor_scalar(dst[:, t], h[:, t], mv[:, t, 0:1], rstd[:, t:t + 1], ALU.subtract, ALU.mult)
            last.then_inc(s_ln_y, 1)
            dve.wait_ge(s_ln_y, seen(s_ln_y))

        def ln_scalar(act, seen, dst=None):
            act.wait_ge(s_ln_var, seen(s_ln_var))
            nc.scalar.activation(std[:], mv[:, :, 1], ACT.Sqrt, bias=eps[:]).then_inc(s_ln_std, 1)
            if dst is not None:
                act.wait_ge(s_ln_yT, seen(s_ln_yT))
                nc.scalar.activation(dst[:], ps[4][0:64, 0:T], ACT.Copy).then_inc(s_yT_ready, 1)

        def ln_tensor(pe, seen, src):
            pe.wait_ge(s_ln_y, seen(s_ln_y))
            for t in range(2):
                last = nc.tensor.transpose(ps[4][0:64, tile(t)], src[:, t], K("ident")[:, 0:P])
            last.then_inc(s_ln_yT, 1)
            pe.wait_ge(s_yT_ready, seen(s_yT_ready))

        def att_vector(dve, seen, h, scale, causal):
            dve.wait_ge(s_att_sim, seen(s_att_sim))
            if causal:
                nc.vector.tensor_tensor(sm[:], ps[6][0:P, 0:2 * T].rearrange("p (t j) -> p t j", t=2),
                                        K("causal").rearrange("p (t j) -> p t j", t=2), ALU.add)\
                    .then_inc(s_dve, seen.one())
                dve.wait_ge(s_dve, seen.steps)
                s = sm[:]
            else:
                s = ps[6][0:P, 0:2 * T].rearrange("p (t j) -> p t j", t=2)
            nc.vector.tensor_reduce(nmax[:, 0], s, AX.X, ALU.max).then_inc(s_dve, seen.one())
            dve.wait_ge(s_dve, seen.steps)
            nc.vector.tensor_scalar(nmax[:, 1], nmax[:, 0], -scale, None, ALU.mult).then_inc(s_att_max, 1)
            dve.wait_ge(s_att_exp, seen(s_att_exp))
            nc.vector.reciprocal(rinv[:, 0], rsum[:, 0]).then_inc(s_dve, seen.one())
            dve.wait_ge(s_dve, seen.steps)
            dve.wait_ge(s_att_out, seen(s_att_out))
            for t in range(2):
                nc.vector.scalar_tensor_tensor(h[:, t], ps[3][0:P, t * C:(t + 1) * C], rinv[:, 0, t:t + 1],
                                               h[:, t], ALU.mult, ALU.add).then_inc(s_dve, seen.one())
            dve.wait_ge(s_dve, seen.steps)

        def att_scalar(act, seen, scale, causal):
            act.wait_ge(s_att_max, seen(s_att_max))
            for t in range(2):
                src = sm[:, t] if causal else ps[6][0:P, t * T:(t + 1) * T]
                last = nc.scalar.activation(pr[:, 0, t * T:(t + 1) * T], src, ACT.Exp, bias=nmax[:, 1, t:t + 1],
                                            scale=scale, accum_out=rsum[:, 0, t:t + 1])
            last.then_inc(s_att_exp, 1)
            act.wait_ge(s_att_pT, seen(s_att_pT))
            nc.scalar.activation(prT[:, 0], ps[7][0:P, 0:2 * T], ACT.Copy).then_inc(s_att_pTc, 1)

        def att_tensor(pe, seen, q, k, val):
            for t in range(2):
                last = nc.tensor.matmul(ps[6][0:P, t * T:(t + 1) * T], q[:, tile(t)], k, start=True, stop=True)
            last.then_inc(s_att_sim, 1)
            pe.wait_ge(s_att_exp, seen(s_att_exp))
            for t in range(2):
                for j in range(2):
                    last = nc.tensor.transpose(ps[7][0:P, j * T + t * P:j * T + (t + 1) * P],
                                               pr[:, 0, t * T + j * P:t * T + (j + 1) * P], K("ident")[:, 0:P])
            last.then_inc(s_att_pT, 1)
            pe.wait_ge(s_att_pTc, seen(s_att_pTc))
            for t in range(2):
                for j in range(2):
                    last = nc.tensor.matmul(ps[3][0:P, t * C:(t + 1) * C], prT[:, 0, j * T + t * P:j * T + (t + 1) * P],
                                            val(j), start=j == 0, stop=j == 1)
            last.then_inc(s_att_out, 1)

        def front_sync(sp, seen, b):
            sp.dma_start(xT_sb[:], xT[bass.ds(b, 1)].rearrange("a c t -> (a c) t")).then_inc(s_x_loaded, 16)
            for t in range(2):
                src = bass.AP(x.tensor, b * (T_IN * C) + t * P * C, [[C, P], [1, WIN * C]])
                sp.dma_start(xwin[:, t], src).then_inc(s_x_loaded, 16)

        def front_vector(dve, seen):
            h = hF
            dve.wait_ge(s_tok_score, seen(s_tok_score))
            score = ps[3][0:P, 0:2 * WIN].rearrange("p (t s) -> p t s", t=2)
            nc.vector.tensor_reduce(s2[:, 0], score, AX.X, ALU.max).then_inc(s_dve, seen.one())
            dve.wait_ge(s_dve, seen.steps)
            nc.vector.tensor_tensor(e9[:], score, s2[:, 0].unsqueeze(2).broadcast_to([P, 2, WIN]),
                                    ALU.subtract).then_inc(s_tok_shift, 1)
            dve.wait_ge(s_tok_exp, seen(s_tok_exp))
            nc.vector.tensor_reduce(s2[:, 1], e9[:], AX.X, ALU.add).then_inc(s_dve, seen.one())
            dve.wait_ge(s_dve, seen.steps)
            nc.vector.reciprocal(s2[:, 2], s2[:, 1]).then_inc(s_dve, seen.one())
            dve.wait_ge(s_dve, seen.steps)
            nc.vector.tensor_tensor(e9[:], e9[:], s2[:, 2].unsqueeze(2).broadcast_to([P, 2, WIN]), ALU.mult)\
                .then_inc(s_dve, seen.one())
            dve.wait_ge(s_dve, seen.steps)
            dve.wait_ge(s_x_loaded, seen(s_x_loaded, 48))
            for t in range(2):
                win = xwin[:, t].rearrange("p (s c) -> p s c", s=WIN)
                nc.vector.tensor_tensor(win, win, e9[:, t].unsqueeze(2).broadcast_to([P, WIN, C]), ALU.mult)\
                    .then_inc(s_dve, seen.one())
            dve.wait_ge(s_dve, seen.steps)
            for t in range(2):
                nc.vector.tensor_reduce(h[:, t], xwin[:, t].rearrange("p (s c) -> p c s", s=WIN), AX.X, ALU.add)\
                    .then_inc(s_dve, seen.one())
            dve.wait_ge(s_dve, seen.steps)

            ln_vector(dve, seen, h, y)
            att_vector(dve, seen, h, C ** -0.5, False)

            ln_vector(dve, seen, h, y)
            dve.wait_ge(s_l0_logit, seen(s_l0_logit))
            nc.vector.tensor_copy(lg[:], ps[3][0:P, 0:128].rearrange("p (t e) -> p t e", t=2)).then_inc(s_dve, seen.one())
            dve.wait_ge(s_dve, seen.steps)
            for t in range(2):
                nc.vector.max(m8[:, t], lg[:, t]).then_inc(s_dve, seen.one())
            dve.wait_ge(s_dve, seen.steps)
            nc.vector.tensor_scalar(s2[:, 0], m8[:, :, 0], 1.0, None, ALU.mult).then_inc(s_dve, seen.one())
            dve.wait_ge(s_dve, seen.steps)
            nc.vector.memset(m8[:, :, TOPK_E:8], NEG).then_inc(s_dve, seen.one())
            nc.vector.tensor_tensor(sc[:], lg[:], s2[:, 0].unsqueeze(2).broadcast_to([P, 2, 64]),
                                    ALU.subtract).then_inc(s_l0_shift, 1)
            dve.wait_ge(s_dve, seen.steps)
            for t in range(2):
                nc.vector.match_replace(rep[:, t], m8[:, t], lg[:, t], NEG).then_inc(s_dve, seen.one())
            dve.wait_ge(s_dve, seen.steps)
            dve.wait_ge(s_l0_e, seen(s_l0_e))
            for t in range(2):
                nc.vector.scalar_tensor_tensor(sc[:, t], rep[:, t], -1.0e38, sc[:, t], ALU.is_lt, ALU.mult)\
                    .then_inc(s_dve, seen.one())
            dve.wait_ge(s_dve, seen.steps)
            nc.vector.tensor_reduce(s2[:, 1], sc[:], AX.X, ALU.add).then_inc(s_dve, seen.one())
            dve.wait_ge(s_dve, seen.steps)
            nc.vector.reciprocal(s2[:, 2], s2[:, 1]).then_inc(s_dve, seen.one())
            dve.wait_ge(s_dve, seen.steps)
            nc.vector.tensor_tensor(sc[:], sc[:], s2[:, 2].unsqueeze(2).broadcast_to([P, 2, 64]), ALU.mult)\
                .then_inc(s_dve, seen.one())
            dve.wait_ge(s_dve, seen.steps)
            for n in range(16):
                t, c = divmod(n, 8)
                dve.wait_ge(s_l0_xw, seen(s_l0_xw))
                if n >= 4:
                    dve.wait_ge(s_l0_sum, seen(s_l0_sum))
                nc.vector.tensor_tensor(lw[:, n % 4].rearrange("p (e d) -> p e d", e=8),
                                        ps[n % 3][0:P, :].rearrange("p (e d) -> p e d", e=8),
                                        sc[:, t, 8 * c:8 * c + 8].unsqueeze(2).broadcast_to([P, 8, C]),
                                        ALU.mult).then_inc(s_l0_prod, 1)
            dve.wait_ge(s_l0_sum, seen(s_l0_sum, 4))
            nc.vector.tensor_tensor(t64[:, :, 0:C], ps[6][0:P, 0:128].rearrange("p (t c) -> p t c", t=2), y[:], ALU.add)\
                .then_inc(s_dve, seen.one())
            dve.wait_ge(s_dve, seen.steps)
            nc.vector.tensor_tensor(t64[:, :, 0:C], t64[:, :, 0:C], two(R("out_b")), ALU.add).then_inc(s_dve, seen.one())
            dve.wait_ge(s_dve, seen.steps)
            ln_vector(dve, seen, t64[:, :, 0:C], u64[:, :, 0:C])
            nc.vector.tensor_tensor(u64[:, :, 0:C], u64[:, :, 0:C], two(R("ln_g")), ALU.mult).then_inc(s_dve, seen.one())
            dve.wait_ge(s_dve, seen.steps)
            nc.vector.tensor_tensor(u64[:, :, 0:C], u64[:, :, 0:C], two(R("ln_b")), ALU.add).then_inc(s_dve, seen.one())
            dve.wait_ge(s_dve, seen.steps)
            nc.vector.tensor_tensor(h[:], h[:], u64[:, :, 0:C], ALU.add).then_inc(s_dve, seen.one())
            dve.wait_ge(s_dve, seen.steps)

            ln_vector(dve, seen, h, y)
            dve.wait_ge(s_l1_qkv, seen(s_l1_qkv))
            G = 2 * H1
            nc.vector.tensor_tensor(t64[:], ps[3][0:P, 0:256].rearrange("p (t c) -> p t c", t=2),
                                    two(R("l1_bkv")), ALU.add).then_inc(s_dve, seen.one())
            dve.wait_ge(s_dve, seen.steps)
            quad = t64[:].rearrange("p t (g d) -> p t g d", d=D1)
            nc.vector.tensor_reduce(g64[:], quad, AX.X, ALU.add).then_inc(s_dve, seen.one())
            dve.wait_ge(s_dve, seen.steps)
            nc.vector.tensor_scalar(g64[:], g64[:], 1.0 / D1, None, ALU.mult).then_inc(s_dve, seen.one())
            dve.wait_ge(s_dve, seen.steps)
            nc.vector.tensor_tensor(quad, quad, g64[:].unsqueeze(3).broadcast_to([P, 2, G, D1]), ALU.subtract)\
                .then_inc(s_dve, seen.one())
            dve.wait_ge(s_dve, seen.steps)
            nc.vector.tensor_tensor(u64[:], t64[:], t64[:], ALU.mult).then_inc(s_dve, seen.one())
            dve.wait_ge(s_dve, seen.steps)
            nc.vector.tensor_reduce(g64[:], u64[:].rearrange("p t (g d) -> p t g d", d=D1), AX.X,
                                    ALU.add).then_inc(s_l1_var, 1)
            dve.wait_ge(s_l1_std, seen(s_l1_std))
            nc.vector.tensor_scalar(g64[:], g64[:], 1e-5, None, ALU.add).then_inc(s_dve, seen.one())
            dve.wait_ge(s_dve, seen.steps)
            nc.vector.reciprocal(g64[:], g64[:]).then_inc(s_dve, seen.one())
            dve.wait_ge(s_dve, seen.steps)
            nc.vector.tensor_tensor(quad, quad, g64[:].unsqueeze(3).broadcast_to([P, 2, G, D1]), ALU.mult)\
                .then_inc(s_dve, seen.one())
            dve.wait_ge(s_dve, seen.steps)
            nc.vector.tensor_tensor(t64[:], t64[:], two(R("l1_w")), ALU.mult).then_inc(s_dve, seen.one())
            dve.wait_ge(s_dve, seen.steps)
            nc.vector.tensor_tensor(kvn[:], t64[:], two(R("l1_b")), ALU.add).then_inc(s_l1_kvn, 1)
            dve.wait_ge(s_l1_kv, seen(s_l1_kv))
            nc.vector.tensor_tensor(m64[:, 0:64], ps[5][0:64, 0:64], K("mask1", 64), ALU.mult).then_inc(s_l1_m, 1)
            dve.wait_ge(s_l1_attT, seen(s_l1_attT))
            nc.vector.tensor_tensor(qT[:, 1], ps[5][0:64, 128:128 + T], yT[:], ALU.add).then_inc(s_l1_ret, 1)
            dve.wait_ge(s_l1_proj, seen(s_l1_proj))
            nc.vector.tensor_tensor(t64[:, :, 0:C], ps[3][0:P, 0:128].rearrange("p (t c) -> p t c", t=2),
                                    two(R("l1_bproj")), ALU.add).then_inc(s_l1_pre, 1)
            dve.wait_ge(s_l1_gelu, seen(s_l1_gelu))
            nc.vector.tensor_tensor(u64[:, :, 0:C], u64[:, :, 0:C], y[:], ALU.add).then_inc(s_dve, seen.one())
            dve.wait_ge(s_dve, seen.steps)
            nc.vector.tensor_tensor(h[:], h[:], u64[:, :, 0:C], ALU.add).then_inc(s_dve, seen.one())
            dve.wait_ge(s_dve, seen.steps)

            ln_vector(dve, seen, h, y)
            dve.wait_ge(s_e_gate, seen(s_e_gate))
            gl = t64[:, :, 0:E1]
            nc.vector.tensor_tensor(gl, ps[3][0:P, 0:2 * E1].rearrange("p (t e) -> p t e", t=2),
                                    two(R("l1_bg")), ALU.add).then_inc(s_dve, seen.one())
            dve.wait_ge(s_dve, seen.steps)
            nc.vector.tensor_reduce(s2[:, 0], gl, AX.X, ALU.max).then_inc(s_dve, seen.one())
            dve.wait_ge(s_dve, seen.steps)
            nc.vector.tensor_tensor(gl, gl, s2[:, 0].unsqueeze(2).broadcast_to([P, 2, E1]),
                                    ALU.subtract).then_inc(s_e_shift, 1)
            dve.wait_ge(s_e_exp, seen(s_e_exp))
            nc.vector.tensor_reduce(s2[:, 1], gl, AX.X, ALU.add).then_inc(s_dve, seen.one())
            dve.wait_ge(s_dve, seen.steps)
            nc.vector.reciprocal(s2[:, 2], s2[:, 1]).then_inc(s_dve, seen.one())
            dve.wait_ge(s_dve, seen.steps)
            nc.vector.tensor_tensor(gl, gl, s2[:, 2].unsqueeze(2).broadcast_to([P, 2, E1]), ALU.mult)\
                .then_inc(s_dve, seen.one())
            dve.wait_ge(s_dve, seen.steps)
            for t in range(2):
                nc.vector.max(m8[:, t], gl[:, t]).then_inc(s_dve, seen.one())
            dve.wait_ge(s_dve, seen.steps)
            nc.vector.memset(m8[:, :, 1:8], NEG).then_inc(s_dve, seen.one())
            dve.wait_ge(s_dve, seen.steps)
            for t in range(2):
                nc.vector.match_replace(rep[:, t, 0:E1], m8[:, t], gl[:, t], NEG).then_inc(s_dve, seen.one())
            dve.wait_ge(s_dve, seen.steps)
            for t in range(2):
                nc.vector.scalar_tensor_tensor(sc[:, t, 0:E1], rep[:, t, 0:E1], -1.0e38, gl[:, t], ALU.is_lt, ALU.mult)\
                    .then_inc(s_dve, seen.one())
            dve.wait_ge(s_dve, seen.steps)
            for t in range(2):
                dve.wait_ge(s_e_y, seen(s_e_y))
                nc.vector.tensor_tensor(lw[:, t].rearrange("p (e d) -> p e d", e=E1),
                                        ps[1 + t][0:P, :].rearrange("p (e d) -> p e d", e=E1),
                                        sc[:, t, 0:E1].unsqueeze(2).broadcast_to([P, E1, C]), ALU.mult)\
                    .then_inc(s_dve, seen.one())
                dve.wait_ge(s_dve, seen.steps)
            nc.vector.tensor_reduce(u64[:, :, 0:C], lw[:, 0:2].rearrange("p t (e c) -> p t c e", e=E1), AX.X, ALU.add)\
                .then_inc(s_dve, seen.one())
            dve.wait_ge(s_dve, seen.steps)
            nc.vector.tensor_tensor(h[:], h[:], u64[:, :, 0:C], ALU.add).then_inc(s_dve, seen.one())
            dve.wait_ge(s_dve, seen.steps)

            ln_vector(dve, seen, h, y)
            dve.wait_ge(s_l2_qkv, seen(s_l2_qkv))
            qk = ps[0][0:C, 0:2 * T].rearrange("p (n j) -> p n j", n=2)
            swapped = ps[1][0:ROPE, 0:2 * T].rearrange("p (n j) -> p n j", n=2)
            cos = K("cos", C).unsqueeze(1).broadcast_to([C, 2, T])
            sin = K("sin", ROPE).unsqueeze(1).broadcast_to([ROPE, 2, T])
            nc.vector.tensor_tensor(qT[:], qk, cos, ALU.mult).then_inc(s_dve, seen.one())
            nc.vector.tensor_tensor(rope2[:], swapped, sin, ALU.mult).then_inc(s_dve, seen.one())
            dve.wait_ge(s_dve, seen.steps)
            nc.vector.tensor_tensor(qT[0:ROPE], qT[0:ROPE], rope2[:], ALU.add).then_inc(s_l2_rope, 1)
            att_vector(dve, seen, h, 64 ** -0.5, True)

            ln_vector(dve, seen, h, y)
            dve.wait_ge(s_pk_copied, seen(s_pk_copied))
            for t in range(2):
                pick_vector(dve, seen, t)
            dve.wait_ge(s_pk_exp, seen(s_pk_exp))
            nc.vector.tensor_reduce(s16(0), wgtF[:].rearrange("p t h k -> p (t h) k"), AX.X, ALU.add)\
                .then_inc(s_dve, seen.one())
            dve.wait_ge(s_dve, seen.steps)
            nc.vector.reciprocal(s16(1), s16(0)).then_inc(s_dve, seen.one())
            dve.wait_ge(s_dve, seen.steps)
            nc.vector.tensor_tensor(wgtF[:].rearrange("p t h k -> p (t h) k"),
                                    wgtF[:].rearrange("p t h k -> p (t h) k"),
                                    s16(1).unsqueeze(2).broadcast_to([P, 16, PK]), ALU.mult)\
                .then_inc(s_dve, seen.one())
            dve.wait_ge(s_dve, seen.steps)

        def s16(n):
            return g64[:].rearrange("p t g -> p (t g)")[:, 16 * n:16 * n + 16]

        def top16(dve, seen, n, values, work, best, best_i, size):
            for g in range(n):
                nc.vector.max(best[:, g, 0:8], values(g)).then_inc(s_dve, seen.one())
            dve.wait_ge(s_dve, seen.steps)
            for g in range(n):
                nc.vector.max_index(best_i[:, g, 0:8], best[:, g, 0:8], values(g)).then_inc(s_dve, seen.one())
                nc.vector.match_replace(work(g), best[:, g, 0:8], values(g), NEG).then_inc(s_dve, seen.one())
            dve.wait_ge(s_dve, seen.steps)
            for g in range(n):
                nc.vector.max(best[:, g, 8:16], work(g)).then_inc(s_dve, seen.one())
            dve.wait_ge(s_dve, seen.steps)
            for g in range(n):
                nc.vector.max_index(best_i[:, g, 8:16], best[:, g, 8:16], work(g)).then_inc(s_dve, seen.one())
            dve.wait_ge(s_dve, seen.steps)

        def pick_vector(dve, seen, t):
            top16(dve, seen, 16, lambda g: pks[:, t, NK * g:NK * (g + 1)], lambda g: pkr[:, NK * g:NK * (g + 1)], v16, i16, NK)
            nc.vector.tensor_copy(f16[:], i16[:]).then_inc(s_dve, seen.one())
            dve.wait_ge(s_dve, seen.steps)
            nc.vector.tensor_scalar(f16[:, H2:16], f16[:, H2:16], float(NK), None, ALU.mult).then_inc(s_dve, seen.one())
            dve.wait_ge(s_dve, seen.steps)
            for src, dst in ((v16, cs), (f16, ci)):
                for i0, i1, nj, at in CAND:
                    ni = i1 - i0
                    nc.vector.tensor_tensor(
                   dst[:, :, at:at + ni * nj].rearrange("p h (i j) -> p h i j", j=nj),
                   src[:, 0:H2, i0:i1].unsqueeze(3).broadcast_to([P, H2, ni, nj]),
                   src[:, H2:16, 0:nj].unsqueeze(2).broadcast_to([P, H2, ni, nj]), ALU.add)\
                        .then_inc(s_dve, seen.one())
            dve.wait_ge(s_dve, seen.steps)
            top16(dve, seen, H2, lambda h: cs[:, h], lambda h: cr[:, h], bv, bi, n_cand)
            last = nc.vector.tensor_tensor(wgtF[:, t], bv[:], bv[:, :, 0:1].broadcast_to([P, H2, PK]), ALU.subtract)
            last.then_inc(s_pk_shift, 1)
            nc.vector.tensor_copy(bf[:], bi[:]).then_inc(s_dve, seen.one())
            dve.wait_ge(s_dve, seen.steps)
            for h in range(0, H2, 2):
                shape = [P, 2, PK, n_cand]
                mask = hot[:].rearrange("p (h k) n -> p h k n", h=2)
                nc.vector.tensor_tensor(mask, K("iota").unsqueeze(1).unsqueeze(1).broadcast_to(shape),
                                        bf[:, h:h + 2].unsqueeze(3).broadcast_to(shape), ALU.is_equal)\
                    .then_inc(s_dve, seen.one())
                dve.wait_ge(s_dve, seen.steps)
                nc.vector.tensor_tensor(mask, mask, ci[:, h:h + 2].unsqueeze(2).broadcast_to(shape), ALU.mult)\
                    .then_inc(s_dve, seen.one())
                dve.wait_ge(s_dve, seen.steps)
                nc.vector.tensor_reduce(cr[:, h:h + 2, 0:PK], mask, AX.X, ALU.add).then_inc(s_dve, seen.one())
                dve.wait_ge(s_dve, seen.steps)
            nc.vector.tensor_tensor(idxF[:, t], cr[:, :, 0:PK],
                                    K("head_base").unsqueeze(2).broadcast_to([P, H2, PK]), ALU.add)\
                .then_inc(s_dve, seen.one())
            dve.wait_ge(s_dve, seen.steps)

        def front_scalar(act, seen):
            for n in range(3):
                act.wait_ge(s_tok_z, seen(s_tok_z))
                parts, pairs = (128, 2) if n < 2 else (64, 1)
                nc.scalar.activation(th[0:parts, 2 * n:2 * n + pairs].rearrange("p a t -> p (a t)"),
                                     ps[n][0:parts, 0:pairs * T], ACT.Tanh,
                                     bias=V("tok_b")[0:parts]).then_inc(s_tok_tanh, 1)
            act.wait_ge(s_tok_shift, seen(s_tok_shift))
            nc.scalar.activation(e9[:], e9[:], ACT.Exp).then_inc(s_tok_exp, 1)
            ln_scalar(act, seen, yT)
            act.wait_ge(s_att_gT, seen(s_att_gT))
            nc.scalar.activation(qT[:, 0], ps[5][0:64, 0:T], ACT.Copy).then_inc(s_att_qk, 1)
            att_scalar(act, seen, C ** -0.5, False)
            ln_scalar(act, seen, yT)
            act.wait_ge(s_l0_shift, seen(s_l0_shift))
            nc.scalar.activation(sc[:], sc[:], ACT.Exp).then_inc(s_l0_e, 1)
            ln_scalar(act, seen)
            ln_scalar(act, seen, yT)
            act.wait_ge(s_l1_q, seen(s_l1_q))
            nc.scalar.activation(qT[:, 0], ps[0][0:64, 0:T], ACT.Identity, bias=V("l1_bq")[0:64]).then_inc(s_l1_q, 1)
            act.wait_ge(s_l1_var, seen(s_l1_var))
            nc.scalar.activation(g64[:], g64[:], ACT.Sqrt, scale=1.0 / (D1 - 1)).then_inc(s_l1_std, 1)
            act.wait_ge(s_l1_pre, seen(s_l1_pre))
            nc.scalar.activation(u64[:, :, 0:C], t64[:, :, 0:C], ACT.Gelu).then_inc(s_l1_gelu, 1)
            ln_scalar(act, seen, yT)
            act.wait_ge(s_e_hT, seen(s_e_hT))
            for c in range(2):
                last = nc.scalar.activation(actT[:, c], ps[0][:, c * T:(c + 1) * T], ACT.Gelu, bias=V("l1_b1")[:, c:c + 1])
            last.then_inc(s_e_act, 1)
            act.wait_ge(s_e_shift, seen(s_e_shift))
            nc.scalar.activation(t64[:, :, 0:E1], t64[:, :, 0:E1], ACT.Exp).then_inc(s_e_exp, 1)
            ln_scalar(act, seen, yT)
            act.wait_ge(s_l2_v, seen(s_l2_v))
            nc.scalar.activation(v_sb[:, :, 0:C], ps[5][0:P, 0:128].rearrange("p (t c) -> p t c", t=2),
                                 ACT.Copy).then_inc(s_l2_v, 1)
            att_scalar(act, seen, 64 ** -0.5, True)
            ln_scalar(act, seen, yTF)
            act.wait_ge(s_pk_sim, seen(s_pk_sim))
            for k in range(4):
                last = nc.scalar.activation(pks[:, k // 2, 512 * (k % 2):512 * (k % 2) + 512], ps[(0, 1, 2, 5)[k]][0:P, :],
                                            ACT.Copy)
            last.then_inc(s_pk_copied, 1)
            act.wait_ge(s_pk_shift, seen(s_pk_shift, 2))
            nc.scalar.activation(wgtF[:], wgtF[:], ACT.Exp).then_inc(s_pk_exp, 1)

        def front_tensor(pe, seen):
            pe.wait_ge(s_x_loaded, seen(s_x_loaded, 48))
            for n in range(5):
                z = ps[n // 2][:, (n % 2) * T:(n % 2 + 1) * T]
                m = 128 if n < 4 else 64
                last = nc.tensor.matmul(z[0:m], W("tok_qry2", 0, m), xT_sb[:, WIN // 2:WIN // 2 + T], start=True, stop=False,
                                        skip_group_check=True)
                for half in range(m // 64):
                    s = 2 * n + half
                    last = nc.tensor.matmul(z[64 * half:64 * half + 64], W("tok_key"), xT_sb[:, s:s + T], start=False,
                                            stop=True, skip_group_check=True)
                if n % 2 or n == 4:
                    last.then_inc(s_tok_z, 1)
            pe.wait_ge(s_tok_tanh, seen(s_tok_tanh, 3))
            for t in range(2):
                for n in range(5):
                    k, cols = (128, 2) if n < 4 else (64, 1)
                    at = t * WIN + 2 * n
                    last = nc.tensor.matmul(ps[3][0:P, at:at + cols], th[0:k, n, tile(t)], V("tok_v")[0:k, 0:cols],
                                            start=True, stop=True)
            last.then_inc(s_tok_score, 1)
            ln_tensor(pe, seen, y)
            nc.tensor.matmul(ps[5][0:64, 0:T], l0_a[:], yT[:], start=True, stop=True).then_inc(s_att_gT, 1)
            pe.wait_ge(s_att_qk, seen(s_att_qk))
            att_tensor(pe, seen, qT[:, 0], yT[:], lambda j: y[:, j])
            ln_tensor(pe, seen, y)
            for t in range(2):
                last = nc.tensor.matmul(ps[3][0:P, 64 * t:64 * t + 64], yT[:, tile(t)], W("gate"), start=True, stop=True)
            last.then_inc(s_l0_logit, 1)
            for n in range(16 + 2):
                if n < 16:
                    t, c = divmod(n, 8)
                    if n >= 3:
                        pe.wait_ge(s_l0_prod, seen(s_l0_prod))
                    nc.tensor.matmul(ps[n % 3][0:P, :], yT[:, tile(t)], latt[:, 512 * c:512 * c + 512], start=True,
                                     stop=True).then_inc(s_l0_xw, 1)
                if n >= 16:
                    pe.wait_ge(s_l0_prod, seen(s_l0_prod, 1 if n == 16 else 2))
                if n >= 3 or n >= 16:
                    for m in ([n - 3] if n < 16 else ([13] if n == 16 else [14, 15])):
                        t, c = divmod(m, 8)
                        for e in range(8):
                            last = nc.tensor.matmul(ps[6][0:P, C * t:C * t + C], K("ident")[:, 0:P],
                                                    lw[:, m % 4, C * e:C * e + C], start=c == 0 and e == 0, stop=c == 7 and e == 7)
                        last.then_inc(s_l0_sum, 1)
            pe.wait_ge(s_ln_y, seen(s_ln_y))
            ln_tensor(pe, seen, y)
            for t in range(2):
                last = nc.tensor.matmul(ps[3][0:P, 128 * t:128 * t + 128], yT[:, tile(t)], W("l1_kv"), start=True, stop=True)
            last.then_inc(s_l1_qkv, 1)
            nc.tensor.matmul(ps[0][0:64, 0:T], W("l1_q"), yT[:], start=True, stop=True).then_inc(s_l1_q, 1)
            pe.wait_ge(s_l1_kvn, seen(s_l1_kvn))
            for t in range(2):
                last = nc.tensor.matmul(ps[5][0:64, 0:64], kvn[:, t, 0:64], kvn[:, t, 64:128], start=t == 0, stop=t == 1)
            last.then_inc(s_l1_kv, 1)
            pe.wait_ge(s_l1_q, seen(s_l1_q, 2))
            pe.wait_ge(s_l1_m, seen(s_l1_m))
            nc.tensor.matmul(ps[5][0:64, 128:128 + T], m64[:, 0:64], qT[:, 0], start=True, stop=True).then_inc(s_l1_attT, 1)
            pe.wait_ge(s_l1_ret, seen(s_l1_ret))
            for t in range(2):
                last = nc.tensor.matmul(ps[3][0:P, C * t:C * t + C], qT[:, 1, tile(t)], W("l1_proj"), start=True, stop=True)
            last.then_inc(s_l1_proj, 1)
            ln_tensor(pe, seen, y)
            for c in range(2):
                last = nc.tensor.matmul(ps[0][:, c * T:(c + 1) * T], W("l1_w1", 128 * c, 128), yT[:], start=True, stop=True)
            last.then_inc(s_e_hT, 1)
            pe.wait_ge(s_e_act, seen(s_e_act))
            for t in range(2):
                for c in range(2):
                    last = nc.tensor.matmul(ps[3][0:P, E1 * t:E1 * t + E1], actT[:, c, tile(t)],
                                            V("l1_wg")[:, E1 * c:E1 * c + E1], start=c == 0, stop=c == 1)
            last.then_inc(s_e_gate, 1)
            for t in range(2):
                for c in range(2):
                    nc.tensor.matmul(ps[1 + t][0:P, :], actT[:, c, tile(t)], V("l1_wd")[:, 512 * c:512 * c + 512],
                                     start=c == 0, stop=False)
                nc.tensor.matmul(ps[1 + t][0:P, :], K("ones")[0:1], R("bd")[0:1], start=False, stop=True)\
                    .then_inc(s_e_y, 1)
            ln_tensor(pe, seen, y)
            for n, w in enumerate((l2_qw, l2_kvw)):
                nc.tensor.matmul(ps[0][0:64, n * T:(n + 1) * T], w[:, 0:64], yT[:], start=True, stop=True)
                last = nc.tensor.matmul(ps[1][0:ROPE, n * T:(n + 1) * T], w[:, 64:80], yT[:], start=True, stop=True)
            last.then_inc(s_l2_qkv, 1)
            for t in range(2):
                last = nc.tensor.matmul(ps[5][0:P, C * t:C * t + C], yT[:, tile(t)], l2_kvw[:, 80:144], start=True, stop=True)
            last.then_inc(s_l2_v, 1)
            pe.wait_ge(s_l2_v, seen(s_l2_v, 2))
            pe.wait_ge(s_l2_rope, seen(s_l2_rope))
            att_tensor(pe, seen, qT[:, 0], qT[:, 1], lambda j: v_sb[:, j, 0:C])
            ln_tensor(pe, seen, y)
            for k in range(4):
                last = nc.tensor.matmul(ps[(0, 1, 2, 5)[k]][0:P, :], yTF[:, tile(k // 2)],
                                        pk_w[:, 512 * (k % 2):512 * (k % 2) + 512], start=True, stop=True)
            last.then_inc(s_pk_sim, 1)

        def gather_pool(pool, seen):
            for u in range(2 * H2):
                t, h = divmod(u, H2)
                if u >= SLOTS:
                    pool.wait_ge(s_kv_summed, seen(s_kv_summed))
                for k in range(PK):
                    pool.indirect_dma_start(rowbuf[:, u % SLOTS, k], None, table,
                                                bass.IndirectOffsetOnAxis(ap=idxG[:, t, h, k:k + 1], axis=0))\
                        .then_inc(fetched[u % SLOTS], 16)

        def gather_vector(dve, seen, before):
            for u in range(2 * H2):
                t, h = divmod(u, H2)
                dve.wait_ge(fetched[u % SLOTS], (before + u // SLOTS + 1) * (16 * PK))
                row, w = rowbuf[:, u % SLOTS], wgtG[:, t, h]
                for k in range(PK):
                    acc = odd[:] if k % 2 else kv[:, t, h]
                    if k < 2:
                        nc.vector.tensor_scalar(acc, row[:, k], w[:, k:k + 1], None, ALU.mult).then_inc(s_dve, seen.one())
                    else:
                        dve.wait_ge(s_dve, seen.steps - 1)
                        nc.vector.scalar_tensor_tensor(acc, row[:, k], w[:, k:k + 1], acc, ALU.mult, ALU.add)\
                            .then_inc(s_dve, seen.one())
                dve.wait_ge(s_dve, seen.steps)
                nc.vector.tensor_tensor(kv[:, t, h], kv[:, t, h], odd[:], ALU.add).then_inc(s_kv_summed, 1)
                dve.wait_ge(s_kv_summed, seen(s_kv_summed))

        def back_vector(dve, seen):
            h = hB
            for n in range(H2):
                i = n % 2
                dve.wait_ge(s_m_sim, seen(s_m_sim))
                sim = ps[2 + i][0:P, 0:2 * T].rearrange("p (t j) -> p t j", t=2)
                nc.vector.scalar_tensor_tensor(sm[:].rearrange("p t j -> p (t j)"), ps[2 + i][0:P, 0:2 * T],
                                               C ** -0.5, K("causal"), ALU.mult, ALU.add)\
                    .then_inc(s_dve, seen.one())
                dve.wait_ge(s_dve, seen.steps)
                nc.vector.tensor_reduce(nmax[:, 0], sm[:], AX.X, ALU.max).then_inc(s_dve, seen.one())
                dve.wait_ge(s_dve, seen.steps)
                nc.vector.tensor_scalar(nmax[:, 1], nmax[:, 0], -1.0, None, ALU.mult).then_inc(s_m_max, 1)
                dve.wait_ge(s_m_exp, seen(s_m_exp))
                nc.vector.reciprocal(rinv[:, 0], rsum[:, 0]).then_inc(s_dve, seen.one())
                dve.wait_ge(s_dve, seen.steps)
                pi = pr[:, i].rearrange("p (t j) -> p t j", t=2)
                nc.vector.tensor_tensor(pi, pi, rinv[:, 0].unsqueeze(2).broadcast_to([P, 2, T]),
                                        ALU.mult).then_inc(s_m_norm, 1)
            dve.wait_ge(s_m_out, seen(s_m_out))
            nc.vector.tensor_tensor(h[:], h[:], ps[7][0:P, 0:128].rearrange("p (t c) -> p t c", t=2), ALU.add)\
                .then_inc(s_dve, seen.one())
            dve.wait_ge(s_dve, seen.steps)

            ln_vector(dve, seen, h, y)
            dve.wait_ge(s_l3_q, seen(s_l3_q))
            nc.vector.tensor_scalar(qT[:, 0], ps[0][0:64, 0:T], 0.0, None, ALU.min).then_inc(s_dve, seen.one())
            nc.vector.tensor_scalar(kT[:, 0], ps[0][0:64, 0:T], 0.0, None, ALU.max).then_inc(s_dve, seen.one())
            dve.wait_ge(s_l3_kv, seen(s_l3_kv))
            kx = ps[1][0:P, 0:256].rearrange("p (t c) -> p t c", t=2)
            nc.vector.tensor_scalar(v_sb[:, :, 0:C], kx[:, :, C:2 * C], 1.0 / T, None, ALU.mult)\
                .then_inc(s_dve, seen.one())
            nc.vector.memset(v_sb[:, :, C:C + H3], 1.0).then_inc(s_dve, seen.one())
            nc.vector.tensor_scalar(u64[:, :, 0:C], kx[:, :, 0:C], 0.0, None, ALU.max).then_inc(s_dve, seen.one())
            nc.vector.tensor_scalar(t64[:, :, 0:C], kx[:, :, 0:C], 0.0, None, ALU.min).then_inc(s_l3_pre, 1)
            dve.wait_ge(s_dve, seen.steps)
            dve.wait_ge(s_l3_exp, seen(s_l3_exp))
            nc.vector.tensor_tensor(t64[:, :, 0:C], t64[:, :, 0:C], u64[:, :, 0:C], ALU.add)
            nc.vector.tensor_tensor(qT[:, 0], qT[:, 0], kT[:, 0], ALU.add).then_inc(s_l3_elu, 1)
            dve.wait_ge(s_l3_kvs, seen(s_l3_kvs))
            nc.vector.tensor_tensor(m64[:], ps[5][0:64, 0:72], K("mask3", 64), ALU.mult).then_inc(s_l3_m, 1)
            dve.wait_ge(s_l3_num, seen(s_l3_num))
            num = ps[3][0:P, 0:144].rearrange("p (t c) -> p t c", t=2)
            nc.vector.tensor_scalar(g64[:, :, 0:H3], num[:, :, C:C + H3], 1e-6, None, ALU.add).then_inc(s_dve, seen.one())
            dve.wait_ge(s_dve, seen.steps)
            nc.vector.reciprocal(g64[:, :, 0:H3], g64[:, :, 0:H3]).then_inc(s_dve, seen.one())
            dve.wait_ge(s_dve, seen.steps)
            nc.vector.tensor_scalar(g64[:, :, 0:H3], g64[:, :, 0:H3], float(T), None, ALU.mult)\
                .then_inc(s_dve, seen.one())
            dve.wait_ge(s_dve, seen.steps)
            for t in range(2):
                last = nc.vector.tensor_tensor(
                    t64[:, t, 0:C].rearrange("p (h d) -> p h d", h=H3), num[:, t, 0:C].rearrange("p (h d) -> p h d", h=H3),
                    g64[:, t, 0:H3].unsqueeze(2).broadcast_to([P, H3, D3]), ALU.mult)
            last.then_inc(s_l3_msg, 1)
            dve.wait_ge(s_l3_mm, seen(s_l3_mm))
            nc.vector.tensor_copy(t64[:, :, 0:C], ps[3][0:P, 0:128].rearrange("p (t c) -> p t c", t=2))\
                .then_inc(s_dve, seen.one())
            dve.wait_ge(s_dve, seen.steps)
            ln_vector(dve, seen, t64[:, :, 0:C], u64[:, :, 0:C])
            nc.vector.tensor_tensor(u64[:, :, 0:C], u64[:, :, 0:C], two(R("g1")), ALU.mult).then_inc(s_dve, seen.one())
            dve.wait_ge(s_dve, seen.steps)
            nc.vector.tensor_tensor(u64[:, :, 0:C], u64[:, :, 0:C], two(R("b1")), ALU.add).then_inc(s_l3_msg2, 1)
            dve.wait_ge(s_l3_h, seen(s_l3_h))
            nc.vector.tensor_copy(t64[:, :, 0:C], ps[3][0:P, 0:128].rearrange("p (t c) -> p t c", t=2))\
                .then_inc(s_dve, seen.one())
            dve.wait_ge(s_dve, seen.steps)
            ln_vector(dve, seen, t64[:, :, 0:C], u64[:, :, 0:C])
            nc.vector.tensor_tensor(u64[:, :, 0:C], u64[:, :, 0:C], two(R("g2")), ALU.mult).then_inc(s_dve, seen.one())
            dve.wait_ge(s_dve, seen.steps)
            nc.vector.tensor_tensor(u64[:, :, 0:C], u64[:, :, 0:C], two(R("b2")), ALU.add).then_inc(s_dve, seen.one())
            dve.wait_ge(s_dve, seen.steps)
            nc.vector.tensor_tensor(u64[:, :, 0:C], u64[:, :, 0:C], y[:], ALU.add).then_inc(s_dve, seen.one())
            dve.wait_ge(s_dve, seen.steps)
            nc.vector.tensor_tensor(h[:], h[:], u64[:, :, 0:C], ALU.add).then_inc(s_dve, seen.one())
            dve.wait_ge(s_dve, seen.steps)

            ln_vector(dve, seen, h, y)
            dve.wait_ge(s_c_w, seen(s_c_w))
            nc.vector.tensor_scalar(sm[:, 0], ps[5][0:P, 0:T], R("cap_br"), None, ALU.add).then_inc(s_dve, seen.one())
            dve.wait_ge(s_dve, seen.steps)
            for t in range(2):
                own = K("own")[:, t * T:(t + 1) * T]
                tri = K("tri")[:, t * T:(t + 1) * T]
                nc.vector.tensor_tensor(sm[:, 1], sm[:, 0], own, ALU.mult).then_inc(s_dve, seen.one())
                dve.wait_ge(s_dve, seen.steps)
                nc.vector.tensor_reduce(cnt[:, t:t + 1], sm[:, 1], AX.X, ALU.add).then_inc(s_dve, seen.one())
                dve.wait_ge(s_dve, seen.steps)
                nc.vector.scalar_tensor_tensor(sm[:, 1], sm[:, 0], cnt[:, t:t + 1], tri, ALU.is_equal, ALU.mult)\
                    .then_inc(s_dve, seen.one())
                dve.wait_ge(s_dve, seen.steps)
                nc.vector.scalar_tensor_tensor(sm[:, 1], sm[:, 0], cnt[:, t:t + 1], sm[:, 1], ALU.is_gt, ALU.add)\
                    .then_inc(s_dve, seen.one())
                dve.wait_ge(s_dve, seen.steps)
                nc.vector.tensor_reduce(cnt[:, 2 + t:3 + t], sm[:, 1], AX.X, ALU.add).then_inc(s_dve, seen.one())
                dve.wait_ge(s_dve, seen.steps)
            nc.vector.scalar_tensor_tensor(cnt[:, 4:6], cnt[:, 2:4], float(CAP), cnt[:, 0:2], ALU.is_lt, ALU.mult)\
                .then_inc(s_dve, seen.one())
            dve.wait_ge(s_dve, seen.steps)
            dve.wait_ge(s_c_y, seen(s_c_y))
            nc.vector.tensor_tensor(t64[:, :, 0:C], ps[3][0:P, 0:128].rearrange("p (t c) -> p t c", t=2),
                                    two(R("cap_b2")), ALU.add).then_inc(s_dve, seen.one())
            dve.wait_ge(s_dve, seen.steps)
            nc.vector.tensor_tensor(h[:], h[:], y[:], ALU.add).then_inc(s_dve, seen.one())
            dve.wait_ge(s_dve, seen.steps)
            for t in range(2):
                last = nc.vector.scalar_tensor_tensor(h[:, t], t64[:, t, 0:C], cnt[:, 4 + t:5 + t], h[:, t], ALU.mult, ALU.add)
            last.then_inc(s_c_out, 1)
            dve.wait_ge(s_c_out, seen(s_c_out))

        def back_scalar(act, seen):
            for n in range(H2 + 1):
                if n < H2:
                    i = n % 2
                    act.wait_ge(s_m_prep, seen(s_m_prep))
                    nc.scalar.activation(kT[:, i], ps[i][0:64, 0:T], ACT.Copy)
                    nc.scalar.activation(qT[:, i], ps[i][0:64, T:2 * T], ACT.Copy).then_inc(s_m_copied, 1)
                if n:
                    j = (n - 1) % 2
                    act.wait_ge(s_m_pT, seen(s_m_pT))
                    nc.scalar.activation(prT[:, j], ps[4 + j][0:P, 0:2 * T], ACT.Copy).then_inc(s_m_pTc, 1)
                    act.wait_ge(s_m_oT, seen(s_m_oT))
                    nc.scalar.activation(outT[:, n - 1], ps[6][0:64, 0:T], ACT.Copy).then_inc(s_m_oTc, 1)
                if n < H2:
                    act.wait_ge(s_m_max, seen(s_m_max))
                    for t in range(2):
                        last = nc.scalar.activation(pr[:, i, t * T:(t + 1) * T], sm[:, t], ACT.Exp,
                                                    bias=nmax[:, 1, t:t + 1], accum_out=rsum[:, 0, t:t + 1])
                    last.then_inc(s_m_exp, 1)
            ln_scalar(act, seen, yT)
            act.wait_ge(s_l3_pre, seen(s_l3_pre))
            nc.scalar.activation(t64[:, :, 0:C], t64[:, :, 0:C], ACT.Exp)
            nc.scalar.activation(qT[:, 0], qT[:, 0], ACT.Exp).then_inc(s_l3_exp, 1)
            act.wait_ge(s_l3_msgT, seen(s_l3_msgT))
            nc.scalar.activation(kT[:, 0], ps[4][0:64, 0:T], ACT.Copy).then_inc(s_l3_msgTc, 1)
            ln_scalar(act, seen)
            act.wait_ge(s_l3_msgT, seen(s_l3_msgT))
            nc.scalar.activation(kT[:, 0], ps[4][0:64, 0:T], ACT.Copy).then_inc(s_l3_msgTc, 1)
            act.wait_ge(s_l3_hT, seen(s_l3_hT))
            nc.scalar.activation(actT[:, 0], ps[0][:, 0:T], ACT.Relu).then_inc(s_l3_relu, 1)
            ln_scalar(act, seen)
            ln_scalar(act, seen, yT)
            act.wait_ge(s_c_hT, seen(s_c_hT))
            for c in range(2):
                last = nc.scalar.activation(actT[:, c], ps[0][:, c * T:(c + 1) * T], ACT.Gelu_apprx_tanh,
                                            bias=V("cap_b1")[:, c:c + 1])
            last.then_inc(s_c_act, 1)

        def back_tensor(pe, seen):
            for n in range(H2 + 1):
                if n < H2:
                    i = n % 2
                    for t in range(2):
                        nc.tensor.transpose(ps[i][0:64, tile(t)], kv[:, t, n, 0:C], K("ident")[:, 0:P])
                    nc.tensor.matmul(ps[i][0:64, T:2 * T], W("l2f_q", C * n, C), yTB[:], start=True,
                                     stop=True).then_inc(s_m_prep, 1)
                    pe.wait_ge(s_m_copied, seen(s_m_copied))
                    for t in range(2):
                        last = nc.tensor.matmul(ps[2 + i][0:P, t * T:(t + 1) * T], qT[:, i, tile(t)], kT[:, i],
                                                start=True, stop=True)
                    last.then_inc(s_m_sim, 1)
                if n:
                    j = (n - 1) % 2
                    pe.wait_ge(s_m_norm, seen(s_m_norm))
                    for t in range(2):
                        for k in range(2):
                            last = nc.tensor.transpose(ps[4 + j][0:P, k * T + t * P:k * T + (t + 1) * P],
                                                       pr[:, j, t * T + k * P:t * T + (k + 1) * P], K("ident")[:, 0:P])
                    last.then_inc(s_m_pT, 1)
                    pe.wait_ge(s_m_pTc, seen(s_m_pTc))
                    if n > 1:
                        pe.wait_ge(s_m_oTc, seen(s_m_oTc))
                    for k in range(2):
                        last = nc.tensor.matmul(ps[6][0:64, 0:T], kv[:, k, n - 1, C:2 * C], prT[:, j, k * T:(k + 1) * T],
                                                start=k == 0, stop=k == 1)
                    last.then_inc(s_m_oT, 1)
            pe.wait_ge(s_m_oTc, seen(s_m_oTc))
            for t in range(2):
                for n in range(H2):
                    last = nc.tensor.matmul(ps[7][0:P, C * t:C * t + C], outT[:, n, tile(t)], W("l2f_o", C * n, C),
                                            start=n == 0, stop=n == H2 - 1)
            last.then_inc(s_m_out, 1)
            ln_tensor(pe, seen, y)
            nc.tensor.matmul(ps[0][0:64, 0:T], W("l3_q"), yT[:], start=True, stop=True).then_inc(s_l3_q, 1)
            for t in range(2):
                nc.tensor.matmul(ps[1][0:P, 128 * t:128 * t + C], yT[:, tile(t)], W("l3_k"), start=True, stop=True)
                last = nc.tensor.matmul(ps[1][0:P, 128 * t + C:128 * t + 2 * C], yT[:, tile(t)], W("l3_v"), start=True, stop=True)
            last.then_inc(s_l3_kv, 1)
            pe.wait_ge(s_l3_elu, seen(s_l3_elu))
            for t in range(2):
                last = nc.tensor.matmul(ps[5][0:64, 0:72], t64[:, t, 0:C], v_sb[:, t], start=t == 0, stop=t == 1)
            last.then_inc(s_l3_kvs, 1)
            pe.wait_ge(s_l3_m, seen(s_l3_m))
            for t in range(2):
                last = nc.tensor.matmul(ps[3][0:P, 72 * t:72 * t + 72], qT[:, 0, tile(t)], m64[:], start=True, stop=True)
            last.then_inc(s_l3_num, 1)
            pe.wait_ge(s_l3_msg, seen(s_l3_msg))
            for t in range(2):
                last = nc.tensor.transpose(ps[4][0:64, tile(t)], t64[:, t, 0:C], K("ident")[:, 0:P])
            last.then_inc(s_l3_msgT, 1)
            pe.wait_ge(s_l3_msgTc, seen(s_l3_msgTc))
            for t in range(2):
                last = nc.tensor.matmul(ps[3][0:P, C * t:C * t + C], kT[:, 0, tile(t)], W("l3_m"), start=True, stop=True)
            last.then_inc(s_l3_mm, 1)
            pe.wait_ge(s_l3_msg2, seen(s_l3_msg2))
            for t in range(2):
                last = nc.tensor.transpose(ps[4][0:64, tile(t)], u64[:, t, 0:C], K("ident")[:, 0:P])
            last.then_inc(s_l3_msgT, 1)
            nc.tensor.matmul(ps[0][:, 0:T], W("l3_w1x"), yT[:], start=True, stop=False)
            pe.wait_ge(s_l3_msgTc, seen(s_l3_msgTc))
            nc.tensor.matmul(ps[0][:, 0:T], W("l3_w1m"), kT[:, 0], start=False, stop=True).then_inc(s_l3_hT, 1)
            pe.wait_ge(s_l3_relu, seen(s_l3_relu))
            for t in range(2):
                last = nc.tensor.matmul(ps[3][0:P, C * t:C * t + C], actT[:, 0, tile(t)], V("l3_w2"), start=True, stop=True)
            last.then_inc(s_l3_h, 1)
            pe.wait_ge(s_ln_y, seen(s_ln_y, 2))
            ln_tensor(pe, seen, y)
            nc.tensor.matmul(ps[5][0:P, 0:T], W("cap_wr"), yT[:], start=True, stop=True).then_inc(s_c_w, 1)
            for c in range(2):
                last = nc.tensor.matmul(ps[0][:, c * T:(c + 1) * T], W("cap_w1", 128 * c, 128), yT[:], start=True, stop=True)
            last.then_inc(s_c_hT, 1)
            pe.wait_ge(s_c_act, seen(s_c_act))
            for t in range(2):
                for c in range(2):
                    last = nc.tensor.matmul(ps[3][0:P, C * t:C * t + C], actT[:, c, tile(t)],
                                            V("cap_w2")[:, C * c:C * c + C], start=c == 0, stop=c == 1)
            last.then_inc(s_c_y, 1)

        def back_sync(sp, seen, b):
            sp.wait_ge(s_c_out, seen(s_c_out))
            sp.dma_start(out[bass.ds(b, 1)].rearrange("a (t p) c -> p (a t) c", p=P), hB[:])\
                .then_inc(s_stored, 16)
            sp.wait_ge(s_stored, seen(s_stored, 16))

        def turn(b, front, gather, back):
            with nc.Block() as block:
                @block.sync
                def _(sp):
                    seen = Count()
                    if front:
                        front_sync(sp, seen, b)
                    if back:
                        back_sync(sp, seen, b - 2)

                @block.vector
                def _(dve):
                    seen = Count()
                    if back:
                        back_vector(dve, seen)
                    if front:
                        front_vector(dve, seen)
                    if gather:
                        gather_vector(dve, seen, (b - 1) * (2 * H2 // SLOTS))
                    if back:
                        dve.wait_ge(s_stored, seen(s_stored, 16))
                    if gather:
                        nc.vector.tensor_copy(hB[:], hG[:]).then_inc(s_dve, seen.one())
                        nc.vector.tensor_copy(yTB[:], yTG[:]).then_inc(s_dve, seen.one())
                        dve.wait_ge(s_dve, seen.steps)
                    if front:
                        nc.vector.tensor_copy(hG[:], hF[:]).then_inc(s_dve, seen.one())
                        nc.vector.tensor_copy(yTG[:], yTF[:]).then_inc(s_dve, seen.one())
                        nc.vector.tensor_copy(idxG[:], idxF[:]).then_inc(s_dve, seen.one())
                        nc.vector.tensor_copy(wgtG[:], wgtF[:]).then_inc(s_dve, seen.one())
                        dve.wait_ge(s_dve, seen.steps)

                @block.scalar
                def _(act):
                    seen = Count()
                    if back:
                        back_scalar(act, seen)
                    if front:
                        front_scalar(act, seen)

                @block.tensor
                def _(pe):
                    seen = Count()
                    if back:
                        back_tensor(pe, seen)
                        pe.wait_ge(s_c_out, seen(s_c_out))
                    if front:
                        front_tensor(pe, seen)

                @block.gpsimd
                def _(pool):
                    if gather:
                        gather_pool(pool, Count())
            nc.all_engine_barrier(sems_to_clear=cleared)

        eps = sb("eps", [P, 1])
        lattice_raw = rowbuf[0:64].rearrange("p s k c -> p (s k c)")[:, 0:EXPERTS0 * C]
        with nc.Block() as block:
            @block.sync
            def _(sp):
                for dst, src in ((w64_sb[:], w64), (w128_sb[:], w128), (rows_sb[:], rows.partition_broadcast(P)),
                                 (const_sb[:], const), (pk_sb[:, 0], pk_q), (pk_sb[:, 1], pk_k), (lattice_raw, lattice)):
                    sp.dma_start(dst, src).then_inc(s_x_loaded, 16)

            @block.vector
            def _(dve):
                nc.vector.memset(eps[:], 1e-5).then_inc(s_dve, 1)
                dve.wait_ge(s_dve, 1)

            @block.tensor
            def _(pe):
                pe.wait_ge(s_x_loaded, 7 * 16)
                nc.tensor.matmul(ps[0][0:64, 0:64], W("l0_wq"), W("l0_wk"), start=True, stop=True)
                nc.tensor.matmul(ps[0][0:64, 64:144], W("qcomp"), W("q_rcs"), start=True, stop=True)
                nc.tensor.matmul(ps[0][0:64, 144:288], W("kvcomp"), W("kv_rcsv"), start=True, stop=True)\
                    .then_inc(s_setup, 1)
                for g in range(16):
                    last = nc.tensor.matmul(ps[1 + g // 8][0:64, 64 * (g % 8):64 * (g % 8) + 64], pk_sb[:, 0, 64 * g:64 * g + 64],
                                            pk_sb[:, 1, 64 * g:64 * g + 64], start=True, stop=True)
                last.then_inc(s_setup, 1)
                for c in range(8):
                    if c >= 4:
                        pe.wait_ge(s_act, c - 3)
                    for e in range(8):
                        last = nc.tensor.matmul(ps[3 + c % 4][0:64, 64 * e:64 * e + 64],
                                                lattice_raw[:, 64 * (8 * c + e):64 * (8 * c + e) + 64], W("out_w"),
                                                start=True, stop=True)
                    last.then_inc(s_l0_xw, 1)

            @block.scalar
            def _(act):
                for c in range(8):
                    act.wait_ge(s_l0_xw, c + 1)
                    nc.scalar.activation(latt[:, 512 * c:512 * c + 512], ps[3 + c % 4][0:64, :], ACT.Copy)\
                        .then_inc(s_act, 1)
                act.wait_ge(s_setup, 2)
                nc.scalar.activation(l0_a[:], ps[0][0:64, 0:64], ACT.Copy)
                nc.scalar.activation(l2_qw[:], ps[0][0:64, 64:144], ACT.Copy)
                nc.scalar.activation(l2_kvw[:], ps[0][0:64, 144:288], ACT.Copy)
                for c in range(2):
                    last = nc.scalar.activation(pk_w[:, 512 * c:512 * c + 512], ps[1 + c][0:64, :], ACT.Copy)
                last.then_inc(s_act, 1)
                act.wait_ge(s_act, 9)
        nc.all_engine_barrier(sems_to_clear=cleared)

        turn(0, True, False, False)
        turn(1, True, True, False)
        with nc.Fori(2, B) as b:
            turn(b, True, True, True)
        turn(B, False, True, True)
        turn(B + 1, False, False, True)


def kernel(**inputs):
    import concourse.bacc as bacc
    from concourse.bass_utils import run_bass_kernel_spmd

    f = {k: np.asarray(v) for k, v in inputs.items()}

    def pack(table, parts, have):
        cols = []
        for name, n in table:
            a = np.asarray(have[name]).reshape(-1, n)
            cols.append(np.pad(a, ((0, parts - a.shape[0]), (0, 0))))
        return np.ascontiguousarray(np.concatenate(cols, axis=1), dtype=np.float32)

    qkv = f["L1_attn_W_qkv"].reshape(H1, 3, D1, C)
    bqkv = f["L1_attn_b_qkv"].reshape(H1, 3, D1)
    swap = np.arange(ROPE) ^ 1
    halves = lambda a: np.concatenate([a[:128], a[128:]], axis=1)
    w64 = pack(W64, 64, {
        "tok_key": f["L0_tok_W_key"], "tok_qry2": np.concatenate([f["L0_tok_W_qry"]] * 2, axis=1),
        "l0_wq": f["L0_attn_Wq"], "l0_wk": f["L0_attn_Wk"], "gate": f["L0_ffn_gate_w"].T, "out_w": f["L0_ffn_out_w"].T,
        "l1_q": qkv[:, 0].reshape(C, C).T,
        "l1_kv": np.concatenate([qkv[:, 1].reshape(C, C).T, qkv[:, 2].reshape(C, C).T], axis=1),
        "l1_proj": f["L1_attn_W_proj"].T, "l1_w1": f["L1_ffn_W1"],
        "qcomp": f["L2_attn_Wq_comp"].T, "kvcomp": f["L2_attn_Wkv_comp"].T,
        "q_rcs": np.concatenate([f["L2_attn_Wqr"], f["L2_attn_Wqc"], f["L2_attn_Wqr"][:, swap]], axis=1),
        "kv_rcsv": np.concatenate([f["L2_attn_Wkr"], f["L2_attn_Wkc"], f["L2_attn_Wkr"][:, swap], f["L2_attn_Wv"]], axis=1),
        "l2f_q": f["L2_ffn_Wq"], "l2f_o": f["L2_ffn_Wo"].reshape(H2, C, C).transpose(1, 0, 2).reshape(C, H2 * C),
        "l3_q": f["L3_attn_Wq"], "l3_k": f["L3_attn_Wk"], "l3_v": f["L3_attn_Wv"], "l3_m": f["L3_attn_Wm"],
        "l3_w1x": f["L3_attn_W1"][:C], "l3_w1m": f["L3_attn_W1"][C:], "cap_w1": f["L3_ffn_w1"],
        "cap_wr": np.repeat(f["L3_ffn_wr"], P, axis=1)})
    zero = np.zeros((C, 1), np.float32)
    tv, tb = f["L0_tok_v"].reshape(C, 1), f["L0_tok_b"].reshape(C, 1)
    w128 = pack(W128, 128, {
        "tok_v": np.concatenate([np.concatenate([tv, zero], 1), np.concatenate([zero, tv], 1)]),
        "tok_b": np.concatenate([tb, tb]), "l1_bq": bqkv[:, 0].reshape(C, 1),
        "l1_b1": f["L1_ffn_b1"].reshape(2, 128).T, "cap_b1": f["L3_ffn_b1"].reshape(2, 128).T,
        "l1_wg": halves(f["L1_ffn_Wg"]), "l1_wd": halves(f["L1_ffn_Wd"].transpose(1, 0, 2).reshape(HID, E1 * C)),
        "l3_w2": f["L3_attn_W2"], "cap_w2": halves(f["L3_ffn_w2"])})
    kvw = lambda a, b: np.concatenate([a.reshape(-1), b.reshape(-1)])
    rows = {
        "out_b": f["L0_ffn_out_b"], "ln_g": f["L0_ffn_ln_g"], "ln_b": f["L0_ffn_ln_b"],
        "l1_bkv": kvw(bqkv[:, 1], bqkv[:, 2]), "l1_w": kvw(f["L1_attn_kln_w"], f["L1_attn_vln_w"]),
        "l1_b": kvw(f["L1_attn_kln_b"], f["L1_attn_vln_b"]), "l1_bproj": f["L1_attn_b_proj"], "l1_bg": f["L1_ffn_bg"],
        "g1": f["L3_attn_g1"], "b1": f["L3_attn_b1"], "g2": f["L3_attn_g2"], "b2": f["L3_attn_b2"],
        "cap_b2": f["L3_ffn_b2"], "cap_br": f["L3_ffn_br"], "bd": f["L1_ffn_bd"].reshape(-1)}
    rows = np.concatenate([np.asarray(rows[n], np.float32) for n, _ in ROWS])

    i, j = np.arange(T)[:, None], np.arange(T)[None, :]
    tiles = lambda m: m.reshape(2, P, T).transpose(1, 0, 2).reshape(P, 2 * T)
    half = ROPE // 2
    theta = (1.0 / np.float32(10000.0) ** (np.arange(half, dtype=np.float32) / np.float32(half))).astype(np.float32)
    angle = (np.arange(T, dtype=np.float32)[:, None] * theta[None, :]).T
    cos = np.ones((C, T), np.float32)
    cos[:ROPE] = np.repeat(np.cos(angle), 2, axis=0)
    sin = np.repeat(np.sin(angle), 2, axis=0)
    sin[0::2] *= -1
    block = lambda n, d: np.kron(np.eye(n), np.ones((d, d)))
    const = pack(CONST, 128, {
        "ident": np.eye(128), "causal": tiles(np.where(j <= i, 0.0, -1.0e38)), "tri": tiles((j < i) * 1.0),
        "own": tiles((i == j) * 1.0), "iota": np.broadcast_to(np.arange(n_cand), (P, n_cand)),
        "head_base": np.broadcast_to(np.arange(H2) * NKV, (P, H2)), "cos": cos, "sin": sin,
        "mask1": block(H1, D1) / T, "mask3": np.concatenate([block(H3, D3), np.kron(np.eye(H3), np.ones((D3, 1)))], axis=1),
        "ones": np.ones((1, P))})
    arrays = {
        "x": f["x"], "xT": np.ascontiguousarray(f["x"].transpose(0, 2, 1)), "w64": w64, "w128": w128,
        "lattice": np.ascontiguousarray(f["L0_ffn_lattice_weights"].transpose(2, 0, 1).reshape(C, EXPERTS0 * C)),
        "pk_q": np.ascontiguousarray(f["L2_ffn_Wq_pk"].reshape(C, 16, 32).transpose(2, 1, 0).reshape(32, 16 * C)),
        "pk_k": np.ascontiguousarray(f["L2_ffn_pk_keys"].transpose(3, 0, 2, 1).reshape(32, 16 * NK)),
        "rows": rows, "const": const,
        "table": np.concatenate([f["L2_ffn_keys_table"], f["L2_ffn_values_table"]], axis=1)}
    nc = bacc.Bacc("TRN2", target_bir_lowering=False, num_devices=1)
    args = [nc.dram_tensor(n, a.shape, mybir.dt.from_np(a.dtype), kind="ExternalInput").ap() for n, a in arrays.items()]
    out = nc.dram_tensor("out", (B, T, C), mybir.dt.float32, kind="ExternalOutput").ap()
    tower(nc, *args, out)
    r = run_bass_kernel_spmd(nc, [arrays], core_ids=[0])
    return r.results[0]["out"]
```

```python
from contextlib import ExitStack

import numpy as np
import concourse.bass as bass
from concourse import mybir

B, T_IN, C = 16, 250, 64
WIN = 9
T = T_IN - WIN + 1
P = T // 2
TOPK_E, EXPERTS0 = 6, 64
H1, D1 = 16, 4
HID, E1 = 256, 8
ROPE = 16
H2, NK, PK = 8, 64, 16
NKV = NK * NK
H3, D3 = 8, 8
CAP = T // 2 - 1
SLOTS = 6
ROWS_BITS = H2 * NKV
NEG = -3.0e38

CAND, n_cand = [], 0
for i0, i1 in ((0, 1), (1, 2), (2, 3), (3, 4), (4, 5), (5, 8), (8, 16)):
    CAND.append((i0, i1, PK // (i0 + 1), n_cand))
    n_cand += (i1 - i0) * (PK // (i0 + 1))

W64 = [("tok_key", 64), ("tok_qry2", 128), ("l0_wq", 64), ("l0_wk", 64), ("gate", 64), ("out_w", 64),
       ("l1_q", 64), ("l1_kv", 128), ("l1_proj", 64), ("l1_w1", HID), ("qcomp", 64), ("kvcomp", 64),
       ("q_rcs", 80), ("kv_rcsv", 144), ("l2f_q", 512), ("l2f_o", 512), ("l3_q", 64), ("l3_k", 64),
       ("l3_v", 64), ("l3_m", 64), ("l3_w1x", 128), ("l3_w1m", 128), ("cap_w1", HID), ("cap_wr", P)]
W128 = [("tok_v", 2), ("tok_b", 1), ("l1_bq", 1), ("l1_b1", 2), ("cap_b1", 2), ("l1_wg", 2 * E1),
        ("l1_wd", 2 * E1 * C), ("l3_w2", C), ("cap_w2", 2 * C)]
ROWS = [("out_b", 64), ("ln_g", 64), ("ln_b", 64), ("l1_bkv", 128), ("l1_w", 128), ("l1_b", 128),
        ("l1_bproj", 64), ("l1_bg", E1), ("g1", 64), ("b1", 64), ("g2", 64), ("b2", 64),
        ("cap_b2", 64), ("cap_br", 1), ("bd", E1 * C)]
CONST = [("ident", 128), ("causal", 2 * T), ("tri", 2 * T), ("own", 2 * T), ("row_base", H2 * n_cand),
         ("bit_base", H2 * n_cand), ("cos", T), ("sin", T), ("mask1", 64), ("mask3", 72), ("ones", P)]


def places(table):
    out, at = {}, 0
    for name, n in table:
        out[name] = (at, at + n)
        at += n
    return out, at


class Count:

    def __init__(self, gathers=False, before=0, heads=False):
        self.values, self.steps = {}, 0
        self.gathers, self.before = gathers, before
        self.heads, self.head_steps = heads, 0
        self.units = 0

    def __call__(self, sem, n=1):
        self.values[sem.name] = self.values.get(sem.name, 0) + n
        return self.values[sem.name]

    def one(self):
        self.steps += 1
        return 1

    def unit(self):
        if not self.gathers or self.units == 2 * H2:
            return None
        self.units += 1
        return self.units - 1

    def left(self):
        return range(2 * H2 - self.units if self.gathers else 0)


def tower(nc, x, xT, w64, w128, lattice, pk_q, pk_k, rows, const, table, out):
    fp32, u32 = mybir.dt.float32, mybir.dt.uint32
    ALU, ACT, AX = mybir.AluOpType, mybir.ActivationFunctionType, mybir.AxisListType
    p64, n64 = places(W64)
    p128, n128 = places(W128)
    prow, nrow = places(ROWS)
    pconst, nconst = places(CONST)
    ctx = ExitStack()

    def sb(name, shape, dt=fp32):
        return ctx.enter_context(nc.sbuf_tensor(name, shape, dt))

    with ctx:
        w64_sb, w128_sb = sb("w64_sb", [64, n64]), sb("w128_sb", [128, n128])
        rows_sb, const_sb = sb("rows_sb", [P, nrow]), sb("const_sb", [128, nconst])
        pk_sb = sb("pk_sb", [32, 2, 16 * 64])
        l0_a = sb("l0_a", [64, 64])
        latt = sb("latt", [64, EXPERTS0 * C])
        l2_qw, l2_kvw = sb("l2_qw", [64, 80]), sb("l2_kvw", [64, 144])
        pk_w = sb("pk_w", [64, 16 * NK])
        hF, hG, hB = sb("hF", [P, 2, C]), sb("hG", [P, 2, C]), sb("hB", [P, 2, C])
        yTF, yTG, yTB = sb("yTF", [C, T]), sb("yTG", [C, T]), sb("yTB", [C, T])
        idxF, idxG = sb("idxF", [P, 2, H2, PK], u32), sb("idxG", [P, 2, H2, PK], u32)
        wgtF, wgtG = sb("wgtF", [P, 2, H2, PK]), sb("wgtG", [P, 2, H2, PK])
        rowbuf = sb("rowbuf", [P, SLOTS, PK, 2 * C])
        kvG, kvB = sb("kvG", [P, 2, H2, 2 * C]), sb("kvB", [P, 2, H2, 2 * C])
        xT_sb, xwin = sb("xT_sb", [C, T_IN]), sb("xwin", [P, 2, WIN * C])
        e9, s2 = sb("e9", [P, 2, WIN]), sb("s2", [P, 4, 2])
        y, yT = sb("y", [P, 2, C]), sb("yT", [C, T])
        stat, mv, std, rstd = sb("stat", [P, 2, 6]), sb("mv", [P, 2, 2]), sb("std", [P, 2]), sb("rstd", [P, 2])
        qT, kT = sb("qT", [C, 2, T]), sb("kT", [C, 2, T])
        sm, pr, prT = sb("sm", [P, 2, T]), sb("pr", [P, 2, 2 * T]), sb("prT", [P, 2, 2 * T])
        nmax, rsum, rinv = sb("nmax", [P, 2, 2]), sb("rsum", [P, 2, 2]), sb("rinv", [P, 2, 2])
        lg, m8, rep, sc = sb("lg", [P, 2, 64]), sb("m8", [P, 2, 8]), sb("rep", [P, 2, 64]), sb("sc", [P, 2, 64])
        lw = sb("lw", [P, 4, 512])
        t64, u64 = sb("t64", [P, 2, 2 * C]), sb("u64", [P, 2, 2 * C])
        kvn = sb("kvn", [P, 2, 2 * C])
        g64 = sb("g64", [P, 2, 32])
        m64 = sb("m64", [64, 72])
        actT = sb("actT", [128, 2, T])
        rope2 = sb("rope2", [ROPE, 2, T])
        v_sb = sb("v_sb", [P, 2, 72])
        pks_all = sb("pks_all", [128, 2 * 16 * NK])
        pks = pks_all[0:P].rearrange("p (t n) -> p t n", t=2)
        th = pks_all[:, 0:5 * T].rearrange("p (n t) -> p n t", n=5)
        pkr = xwin[:].rearrange("p t n -> p (t n)")[:, 0:16 * NK]
        v16, i16, f16 = sb("v16", [P, 16, PK]), sb("i16", [P, 16, PK], u32), sb("f16", [P, 16, PK])
        cs, cr, ci = sb("cs", [P, H2, n_cand]), sb("cr", [P, H2, n_cand]), sb("ci", [P, H2, n_cand])
        bv = sb("bv", [P, H2, PK])
        key_all = lw[:].rearrange("p a b -> p (a b)")[:, 0:3 * H2 * n_cand]
        key = key_all.rearrange("p (m h n) -> p m h n", m=3, h=H2)
        kbits = key_all.bitcast(u32).rearrange("p (m h n) -> p m h n", m=3, h=H2)
        best, ibest = sb("best", [P, 3, H2, PK]), sb("ibest", [P, 3, H2, PK], u32)
        outT = sb("outT", [C, H2, T])
        cnt = sb("cnt", [P, 8])
        ps = [ctx.enter_context(nc.psum_tensor(f"ps{i}", [128, 512], fp32)) for i in range(8)]

        def W(name, lo=0, n=None):
            a, b = p64[name]
            return w64_sb[:, a + lo:(a + lo + n if n else b)]

        def V(name):
            a, b = p128[name]
            return w128_sb[:, a:b]

        def R(name):
            a, b = prow[name]
            return rows_sb[:, a:b]

        def K(name, parts=P):
            a, b = pconst[name]
            return const_sb[0:parts, a:b]

        def two(row):
            return row.unsqueeze(1).broadcast_to([P, 2, row.shape[1]])

        def tile(t):
            return slice(t * P, (t + 1) * P)

        def sem(name):
            return ctx.enter_context(nc.semaphore(name))

        s_x_loaded = sem("x_loaded")
        s_dve = sem("dve")
        s_act = sem("act")
        s_ln_var = sem("ln_var")
        s_ln_std = sem("ln_std")
        s_ln_y = sem("ln_y")
        s_ln_yT = sem("ln_yT")
        s_yT_ready = sem("yT_ready")
        s_tok_z = sem("tok_z")
        s_tok_tanh = sem("tok_tanh")
        s_tok_score = sem("tok_score")
        s_tok_shift = sem("tok_shift")
        s_tok_exp = sem("tok_exp")
        s_h_ready = sem("h_ready")
        s_att_gT = sem("att_gT")
        s_att_qk = sem("att_qk")
        s_att_sim = sem("att_sim")
        s_att_max = sem("att_max")
        s_att_exp = sem("att_exp")
        s_att_pT = sem("att_pT")
        s_att_pTc = sem("att_pTc")
        s_att_out = sem("att_out")
        s_att_done = sem("att_done")
        s_l0_logit = sem("l0_logit")
        s_l0_shift = sem("l0_shift")
        s_l0_e = sem("l0_e")
        s_l0_xw = sem("l0_xw")
        s_l0_prod = sem("l0_prod")
        s_l1_qkv = sem("l1_qkv")
        s_l1_q = sem("l1_q")
        s_l1_var = sem("l1_var")
        s_l1_std = sem("l1_std")
        s_l1_kvn = sem("l1_kvn")
        s_l1_kv = sem("l1_kv")
        s_l1_m = sem("l1_m")
        s_l1_attT = sem("l1_attT")
        s_l1_ret = sem("l1_ret")
        s_l1_proj = sem("l1_proj")
        s_l1_pre = sem("l1_pre")
        s_l1_gelu = sem("l1_gelu")
        s_e_hT = sem("e_hT")
        s_e_act = sem("e_act")
        s_e_gate = sem("e_gate")
        s_e_shift = sem("e_shift")
        s_e_exp = sem("e_exp")
        s_e_y = sem("e_y")
        s_e_used = sem("e_used")
        s_l2_qkv = sem("l2_qkv")
        s_l2_rope = sem("l2_rope")
        s_l2_v = sem("l2_v")
        s_pk_sim = sem("pk_sim")
        s_pk_copied = sem("pk_copied")
        s_pk_shift = sem("pk_shift")
        s_pk_exp = sem("pk_exp")
        s_m_prep = sem("m_prep")
        s_m_copied = sem("m_copied")
        s_m_sim = sem("m_sim")
        s_m_max = sem("m_max")
        s_m_exp = sem("m_exp")
        s_m_rinv = sem("m_rinv")
        s_m_norm = sem("m_norm")
        s_m_pT = sem("m_pT")
        s_m_pTc = sem("m_pTc")
        s_m_oT = sem("m_oT")
        s_m_oTc = sem("m_oTc")
        s_m_out = sem("m_out")
        s_l3_q = sem("l3_q")
        s_l3_kv = sem("l3_kv")
        s_l3_pre = sem("l3_pre")
        s_l3_exp = sem("l3_exp")
        s_l3_elu = sem("l3_elu")
        s_l3_kvs = sem("l3_kvs")
        s_l3_m = sem("l3_m")
        s_l3_num = sem("l3_num")
        s_l3_msg = sem("l3_msg")
        s_l3_msgT = sem("l3_msgT")
        s_l3_msgTc = sem("l3_msgTc")
        s_l3_mm = sem("l3_mm")
        s_l3_msg2 = sem("l3_msg2")
        s_l3_hT = sem("l3_hT")
        s_l3_relu = sem("l3_relu")
        s_l3_h = sem("l3_h")
        s_c_w = sem("c_w")
        s_c_hT = sem("c_hT")
        s_c_act = sem("c_act")
        s_c_y = sem("c_y")
        s_c_out = sem("c_out")
        s_weighed = sem("weighed")
        s_summed = sem("summed")
        s_kept = sem("kept")
        s_stored = sem("stored")
        s_setup = sem("setup")
        fetched = [ctx.enter_context(nc.semaphore(f"fetched{i}")) for i in range(SLOTS)]
        cleared = range(s_x_loaded.num, s_setup.num + 1)

        def ln_vector(dve, seen, h, dst, unit=False):
            for t in range(2):
                nc.vector.bn_stats(stat[:, t], h[:, t]).then_inc(s_dve, seen.one())
            dve.wait_ge(s_dve, seen.steps)
            nc.vector.bn_aggr(mv[:, 0], stat[:, 0])
            nc.vector.bn_aggr(mv[:, 1], stat[:, 1]).then_inc(s_ln_var, 1)
            if unit:
                weigh_rows(dve, seen)
            dve.wait_ge(s_ln_std, seen(s_ln_std))
            nc.vector.reciprocal(rstd[:], std[:]).then_inc(s_dve, seen.one())
            dve.wait_ge(s_dve, seen.steps)
            for t in range(2):
                last = nc.vector.tensor_scalar(dst[:, t], h[:, t], mv[:, t, 0:1], rstd[:, t:t + 1], ALU.subtract, ALU.mult)
            last.then_inc(s_ln_y, 1)
            dve.wait_ge(s_ln_y, seen(s_ln_y))

        def ln_scalar(act, seen, dst=None, unit=False):
            act.wait_ge(s_ln_var, seen(s_ln_var))
            nc.scalar.activation(std[:], mv[:, :, 1], ACT.Sqrt, bias=eps[:]).then_inc(s_ln_std, 1)
            if unit:
                keep_sum(act, seen)
            if dst is not None:
                act.wait_ge(s_ln_yT, seen(s_ln_yT))
                nc.scalar.activation(dst[:], ps[4][0:64, 0:T], ACT.Copy).then_inc(s_yT_ready, 1)

        def ln_tensor(pe, seen, src, unit=False):
            if unit:
                sum_rows(pe, seen)
            pe.wait_ge(s_ln_y, seen(s_ln_y))
            for t in range(2):
                last = nc.tensor.transpose(ps[4][0:64, tile(t)], src[:, t], K("ident")[:, 0:P])
            last.then_inc(s_ln_yT, 1)
            pe.wait_ge(s_yT_ready, seen(s_yT_ready))

        def att_vector(dve, seen, h, scale, causal):
            dve.wait_ge(s_att_sim, seen(s_att_sim))
            if causal:
                nc.vector.tensor_tensor(sm[:], ps[6][0:P, 0:2 * T].rearrange("p (t j) -> p t j", t=2),
                                        K("causal").rearrange("p (t j) -> p t j", t=2), ALU.add)\
                    .then_inc(s_dve, seen.one())
                dve.wait_ge(s_dve, seen.steps)
                s = sm[:]
            else:
                s = ps[6][0:P, 0:2 * T].rearrange("p (t j) -> p t j", t=2)
            nc.vector.tensor_reduce(nmax[:, 0], s, AX.X, ALU.max).then_inc(s_dve, seen.one())
            dve.wait_ge(s_dve, seen.steps)
            nc.vector.tensor_scalar(nmax[:, 1], nmax[:, 0], -scale, None, ALU.mult).then_inc(s_att_max, 1)
            dve.wait_ge(s_att_exp, seen(s_att_exp))
            nc.vector.reciprocal(rinv[:, 0], rsum[:, 0]).then_inc(s_dve, seen.one())
            dve.wait_ge(s_dve, seen.steps)
            dve.wait_ge(s_att_out, seen(s_att_out))
            for t in range(2):
                nc.vector.scalar_tensor_tensor(h[:, t], ps[3][0:P, t * C:(t + 1) * C], rinv[:, 0, t:t + 1],
                                               h[:, t], ALU.mult, ALU.add).then_inc(s_dve, seen.one())
            dve.wait_ge(s_dve, seen.steps)

        def att_scalar(act, seen, scale, causal):
            act.wait_ge(s_att_max, seen(s_att_max))
            for t in range(2):
                src = sm[:, t] if causal else ps[6][0:P, t * T:(t + 1) * T]
                last = nc.scalar.activation(pr[:, 0, t * T:(t + 1) * T], src, ACT.Exp, bias=nmax[:, 1, t:t + 1],
                                            scale=scale, accum_out=rsum[:, 0, t:t + 1])
            last.then_inc(s_att_exp, 1)
            act.wait_ge(s_att_pT, seen(s_att_pT))
            nc.scalar.activation(prT[:, 0], ps[2][0:P, 0:2 * T], ACT.Copy).then_inc(s_att_pTc, 1)

        def att_tensor(pe, seen, q, k, val):
            for t in range(2):
                last = nc.tensor.matmul(ps[6][0:P, t * T:(t + 1) * T], q[:, tile(t)], k, start=True, stop=True)
            last.then_inc(s_att_sim, 1)
            pe.wait_ge(s_att_exp, seen(s_att_exp))
            for t in range(2):
                for j in range(2):
                    last = nc.tensor.transpose(ps[2][0:P, j * T + t * P:j * T + (t + 1) * P],
                                               pr[:, 0, t * T + j * P:t * T + (j + 1) * P], K("ident")[:, 0:P])
            last.then_inc(s_att_pT, 1)
            pe.wait_ge(s_att_pTc, seen(s_att_pTc))
            for t in range(2):
                for j in range(2):
                    last = nc.tensor.matmul(ps[3][0:P, t * C:(t + 1) * C], prT[:, 0, j * T + t * P:j * T + (t + 1) * P],
                                            val(j), start=j == 0, stop=j == 1)
            last.then_inc(s_att_out, 1)

        def front_sync(sp, seen, b):
            sp.dma_start(xT_sb[:], xT[bass.ds(b, 1)].rearrange("a c t -> (a c) t")).then_inc(s_x_loaded, 16)
            for t in range(2):
                src = bass.AP(x.tensor, b * (T_IN * C) + t * P * C, [[C, P], [1, WIN * C]])
                sp.dma_start(xwin[:, t], src).then_inc(s_x_loaded, 16)

        def front_vector(dve, seen):
            h = hF
            dve.wait_ge(s_tok_score, seen(s_tok_score))
            score = ps[3][0:P, 0:2 * WIN].rearrange("p (t s) -> p t s", t=2)
            nc.vector.tensor_reduce(s2[:, 0], score, AX.X, ALU.max).then_inc(s_dve, seen.one())
            dve.wait_ge(s_dve, seen.steps)
            nc.vector.tensor_tensor(e9[:], score, s2[:, 0].unsqueeze(2).broadcast_to([P, 2, WIN]),
                                    ALU.subtract).then_inc(s_tok_shift, 1)
            dve.wait_ge(s_tok_exp, seen(s_tok_exp))
            nc.vector.tensor_reduce(s2[:, 1], e9[:], AX.X, ALU.add).then_inc(s_dve, seen.one())
            dve.wait_ge(s_dve, seen.steps)
            nc.vector.reciprocal(s2[:, 2], s2[:, 1]).then_inc(s_dve, seen.one())
            dve.wait_ge(s_dve, seen.steps)
            nc.vector.tensor_tensor(e9[:], e9[:], s2[:, 2].unsqueeze(2).broadcast_to([P, 2, WIN]), ALU.mult)\
                .then_inc(s_dve, seen.one())
            dve.wait_ge(s_dve, seen.steps)
            dve.wait_ge(s_x_loaded, seen(s_x_loaded, 48))
            for t in range(2):
                win = xwin[:, t].rearrange("p (s c) -> p s c", s=WIN)
                nc.vector.tensor_tensor(win, win, e9[:, t].unsqueeze(2).broadcast_to([P, WIN, C]), ALU.mult)\
                    .then_inc(s_dve, seen.one())
            dve.wait_ge(s_dve, seen.steps)
            for t in range(2):
                nc.vector.tensor_reduce(h[:, t], xwin[:, t].rearrange("p (s c) -> p c s", s=WIN), AX.X, ALU.add)\
                    .then_inc(s_dve, seen.one())
            dve.wait_ge(s_dve, seen.steps)

            ln_vector(dve, seen, h, y)
            att_vector(dve, seen, h, C ** -0.5, False)

            ln_vector(dve, seen, h, y, unit=True)
            dve.wait_ge(s_l0_logit, seen(s_l0_logit))
            nc.vector.tensor_copy(lg[:], ps[3][0:P, 0:128].rearrange("p (t e) -> p t e", t=2)).then_inc(s_dve, seen.one())
            dve.wait_ge(s_dve, seen.steps)
            for t in range(2):
                nc.vector.max(m8[:, t], lg[:, t]).then_inc(s_dve, seen.one())
            dve.wait_ge(s_dve, seen.steps)
            nc.vector.tensor_scalar(s2[:, 0], m8[:, :, 0], 1.0, None, ALU.mult).then_inc(s_dve, seen.one())
            dve.wait_ge(s_dve, seen.steps)
            nc.vector.memset(m8[:, :, TOPK_E:8], NEG).then_inc(s_dve, seen.one())
            nc.vector.tensor_tensor(sc[:], lg[:], s2[:, 0].unsqueeze(2).broadcast_to([P, 2, 64]),
                                    ALU.subtract).then_inc(s_l0_shift, 1)
            dve.wait_ge(s_dve, seen.steps)
            for t in range(2):
                nc.vector.match_replace(rep[:, t], m8[:, t], lg[:, t], NEG).then_inc(s_dve, seen.one())
            dve.wait_ge(s_dve, seen.steps)
            dve.wait_ge(s_l0_e, seen(s_l0_e))
            for t in range(2):
                nc.vector.scalar_tensor_tensor(sc[:, t], rep[:, t], -1.0e38, sc[:, t], ALU.is_lt, ALU.mult)\
                    .then_inc(s_dve, seen.one())
            dve.wait_ge(s_dve, seen.steps)
            nc.vector.tensor_reduce(s2[:, 1], sc[:], AX.X, ALU.add).then_inc(s_dve, seen.one())
            dve.wait_ge(s_dve, seen.steps)
            nc.vector.reciprocal(s2[:, 2], s2[:, 1]).then_inc(s_dve, seen.one())
            dve.wait_ge(s_dve, seen.steps)
            nc.vector.tensor_tensor(sc[:], sc[:], s2[:, 2].unsqueeze(2).broadcast_to([P, 2, 64]), ALU.mult)\
                .then_inc(s_dve, seen.one())
            dve.wait_ge(s_dve, seen.steps)
            parts = kvn[:].rearrange("p t (b c) -> p t b c", b=2)
            for n in range(16):
                t, c = divmod(n, 8)
                dve.wait_ge(s_l0_xw, seen(s_l0_xw))
                nc.vector.tensor_tensor(lw[:, n % 4].rearrange("p (e d) -> p e d", e=8),
                                        ps[(0, 1, 2, 5)[n % 4]][0:P, :].rearrange("p (e d) -> p e d", e=8),
                                        sc[:, t, 8 * c:8 * c + 8].unsqueeze(2).broadcast_to([P, 8, C]),
                                        ALU.mult).then_inc(s_l0_prod, 1)
                if n % 4 == 3:
                    dve.wait_ge(s_l0_prod, seen(s_l0_prod, 4))
                    nc.vector.tensor_reduce(parts[:, t, n // 4 % 2], lw[:].rearrange("p b (e d) -> p d (b e)", e=8), AX.X,
                                            ALU.add).then_inc(s_dve, seen.one())
                    dve.wait_ge(s_dve, seen.steps)
            nc.vector.tensor_tensor(parts[:, :, 0], parts[:, :, 0], parts[:, :, 1], ALU.add).then_inc(s_dve, seen.one())
            dve.wait_ge(s_dve, seen.steps)
            nc.vector.tensor_tensor(t64[:, :, 0:C], parts[:, :, 0], y[:], ALU.add).then_inc(s_dve, seen.one())
            dve.wait_ge(s_dve, seen.steps)
            nc.vector.tensor_tensor(t64[:, :, 0:C], t64[:, :, 0:C], two(R("out_b")), ALU.add).then_inc(s_dve, seen.one())
            dve.wait_ge(s_dve, seen.steps)
            ln_vector(dve, seen, t64[:, :, 0:C], u64[:, :, 0:C], unit=True)
            nc.vector.tensor_tensor(u64[:, :, 0:C], u64[:, :, 0:C], two(R("ln_g")), ALU.mult).then_inc(s_dve, seen.one())
            dve.wait_ge(s_dve, seen.steps)
            nc.vector.tensor_tensor(u64[:, :, 0:C], u64[:, :, 0:C], two(R("ln_b")), ALU.add).then_inc(s_dve, seen.one())
            dve.wait_ge(s_dve, seen.steps)
            nc.vector.tensor_tensor(h[:], h[:], u64[:, :, 0:C], ALU.add).then_inc(s_dve, seen.one())
            dve.wait_ge(s_dve, seen.steps)

            ln_vector(dve, seen, h, y, unit=True)
            dve.wait_ge(s_l1_qkv, seen(s_l1_qkv))
            G = 2 * H1
            nc.vector.tensor_tensor(t64[:], ps[3][0:P, 0:256].rearrange("p (t c) -> p t c", t=2),
                                    two(R("l1_bkv")), ALU.add).then_inc(s_dve, seen.one())
            dve.wait_ge(s_dve, seen.steps)
            quad = t64[:].rearrange("p t (g d) -> p t g d", d=D1)
            nc.vector.tensor_reduce(g64[:], quad, AX.X, ALU.add).then_inc(s_dve, seen.one())
            dve.wait_ge(s_dve, seen.steps)
            nc.vector.tensor_scalar(g64[:], g64[:], 1.0 / D1, None, ALU.mult).then_inc(s_dve, seen.one())
            dve.wait_ge(s_dve, seen.steps)
            nc.vector.tensor_tensor(quad, quad, g64[:].unsqueeze(3).broadcast_to([P, 2, G, D1]), ALU.subtract)\
                .then_inc(s_dve, seen.one())
            dve.wait_ge(s_dve, seen.steps)
            nc.vector.tensor_tensor(u64[:], t64[:], t64[:], ALU.mult).then_inc(s_dve, seen.one())
            dve.wait_ge(s_dve, seen.steps)
            nc.vector.tensor_reduce(g64[:], u64[:].rearrange("p t (g d) -> p t g d", d=D1), AX.X,
                                    ALU.add).then_inc(s_l1_var, 1)
            dve.wait_ge(s_l1_std, seen(s_l1_std))
            nc.vector.tensor_scalar(g64[:], g64[:], 1e-5, None, ALU.add).then_inc(s_dve, seen.one())
            dve.wait_ge(s_dve, seen.steps)
            nc.vector.reciprocal(g64[:], g64[:]).then_inc(s_dve, seen.one())
            dve.wait_ge(s_dve, seen.steps)
            nc.vector.tensor_tensor(quad, quad, g64[:].unsqueeze(3).broadcast_to([P, 2, G, D1]), ALU.mult)\
                .then_inc(s_dve, seen.one())
            dve.wait_ge(s_dve, seen.steps)
            nc.vector.tensor_tensor(t64[:], t64[:], two(R("l1_w")), ALU.mult).then_inc(s_dve, seen.one())
            dve.wait_ge(s_dve, seen.steps)
            nc.vector.tensor_tensor(kvn[:], t64[:], two(R("l1_b")), ALU.add).then_inc(s_l1_kvn, 1)
            dve.wait_ge(s_l1_kv, seen(s_l1_kv))
            nc.vector.tensor_tensor(m64[:, 0:64], ps[5][0:64, 0:64], K("mask1", 64), ALU.mult).then_inc(s_l1_m, 1)
            dve.wait_ge(s_l1_attT, seen(s_l1_attT))
            nc.vector.tensor_tensor(qT[:, 1], ps[5][0:64, 128:128 + T], yT[:], ALU.add).then_inc(s_l1_ret, 1)
            dve.wait_ge(s_l1_proj, seen(s_l1_proj))
            nc.vector.tensor_tensor(t64[:, :, 0:C], ps[3][0:P, 0:128].rearrange("p (t c) -> p t c", t=2),
                                    two(R("l1_bproj")), ALU.add).then_inc(s_l1_pre, 1)
            dve.wait_ge(s_l1_gelu, seen(s_l1_gelu))
            nc.vector.tensor_tensor(u64[:, :, 0:C], u64[:, :, 0:C], y[:], ALU.add).then_inc(s_dve, seen.one())
            dve.wait_ge(s_dve, seen.steps)
            nc.vector.tensor_tensor(h[:], h[:], u64[:, :, 0:C], ALU.add).then_inc(s_dve, seen.one())
            dve.wait_ge(s_dve, seen.steps)

            ln_vector(dve, seen, h, y, unit=True)
            dve.wait_ge(s_e_gate, seen(s_e_gate))
            gl = t64[:, :, 0:E1]
            nc.vector.tensor_tensor(gl, ps[3][0:P, 0:2 * E1].rearrange("p (t e) -> p t e", t=2),
                                    two(R("l1_bg")), ALU.add).then_inc(s_dve, seen.one())
            dve.wait_ge(s_dve, seen.steps)
            nc.vector.tensor_reduce(s2[:, 0], gl, AX.X, ALU.max).then_inc(s_dve, seen.one())
            dve.wait_ge(s_dve, seen.steps)
            nc.vector.tensor_tensor(gl, gl, s2[:, 0].unsqueeze(2).broadcast_to([P, 2, E1]),
                                    ALU.subtract).then_inc(s_e_shift, 1)
            dve.wait_ge(s_e_exp, seen(s_e_exp))
            nc.vector.tensor_reduce(s2[:, 1], gl, AX.X, ALU.add).then_inc(s_dve, seen.one())
            dve.wait_ge(s_dve, seen.steps)
            nc.vector.reciprocal(s2[:, 2], s2[:, 1]).then_inc(s_dve, seen.one())
            dve.wait_ge(s_dve, seen.steps)
            nc.vector.tensor_tensor(gl, gl, s2[:, 2].unsqueeze(2).broadcast_to([P, 2, E1]), ALU.mult)\
                .then_inc(s_dve, seen.one())
            dve.wait_ge(s_dve, seen.steps)
            for t in range(2):
                nc.vector.max(m8[:, t], gl[:, t]).then_inc(s_dve, seen.one())
            dve.wait_ge(s_dve, seen.steps)
            nc.vector.memset(m8[:, :, 1:8], NEG).then_inc(s_dve, seen.one())
            dve.wait_ge(s_dve, seen.steps)
            for t in range(2):
                nc.vector.match_replace(rep[:, t, 0:E1], m8[:, t], gl[:, t], NEG).then_inc(s_dve, seen.one())
            dve.wait_ge(s_dve, seen.steps)
            for t in range(2):
                nc.vector.scalar_tensor_tensor(sc[:, t, 0:E1], rep[:, t, 0:E1], -1.0e38, gl[:, t], ALU.is_lt, ALU.mult)\
                    .then_inc(s_dve, seen.one())
            dve.wait_ge(s_dve, seen.steps)
            for t in range(2):
                dve.wait_ge(s_e_y, seen(s_e_y))
                nc.vector.tensor_tensor(lw[:, t].rearrange("p (e d) -> p e d", e=E1),
                                        ps[1 + t][0:P, :].rearrange("p (e d) -> p e d", e=E1),
                                        sc[:, t, 0:E1].unsqueeze(2).broadcast_to([P, E1, C]), ALU.mult)\
                    .then_inc(s_dve, seen.one())
                dve.wait_ge(s_dve, seen.steps)
            nc.vector.tensor_reduce(u64[:, :, 0:C], lw[:, 0:2].rearrange("p t (e c) -> p t c e", e=E1), AX.X, ALU.add)\
                .then_inc(s_dve, seen.one())
            dve.wait_ge(s_dve, seen.steps)
            nc.vector.tensor_tensor(h[:], h[:], u64[:, :, 0:C], ALU.add).then_inc(s_dve, seen.one())
            dve.wait_ge(s_dve, seen.steps)

            ln_vector(dve, seen, h, y, unit=True)
            dve.wait_ge(s_l2_qkv, seen(s_l2_qkv))
            qk = ps[0][0:C, 0:2 * T].rearrange("p (n j) -> p n j", n=2)
            swapped = ps[1][0:ROPE, 0:2 * T].rearrange("p (n j) -> p n j", n=2)
            cos = K("cos", C).unsqueeze(1).broadcast_to([C, 2, T])
            sin = K("sin", ROPE).unsqueeze(1).broadcast_to([ROPE, 2, T])
            nc.vector.tensor_tensor(qT[:], qk, cos, ALU.mult).then_inc(s_dve, seen.one())
            nc.vector.tensor_tensor(rope2[:], swapped, sin, ALU.mult).then_inc(s_dve, seen.one())
            dve.wait_ge(s_dve, seen.steps)
            nc.vector.tensor_tensor(qT[0:ROPE], qT[0:ROPE], rope2[:], ALU.add).then_inc(s_l2_rope, 1)
            att_vector(dve, seen, h, 64 ** -0.5, True)

            ln_vector(dve, seen, h, y, unit=True)
            dve.wait_ge(s_pk_copied, seen(s_pk_copied))
            for t in range(2):
                weigh_rows(dve, seen)
                weigh_rows(dve, seen)
                pick_vector(dve, seen, t)
            heads_vector(dve, seen)
            dve.wait_ge(s_pk_exp, seen(s_pk_exp))
            nc.vector.tensor_reduce(s16(0), wgtF[:].rearrange("p t h k -> p (t h) k"), AX.X, ALU.add)\
                .then_inc(s_dve, seen.one())
            dve.wait_ge(s_dve, seen.steps)
            nc.vector.reciprocal(s16(1), s16(0)).then_inc(s_dve, seen.one())
            dve.wait_ge(s_dve, seen.steps)
            nc.vector.tensor_tensor(wgtF[:].rearrange("p t h k -> p (t h) k"),
                                    wgtF[:].rearrange("p t h k -> p (t h) k"),
                                    s16(1).unsqueeze(2).broadcast_to([P, 16, PK]), ALU.mult)\
                .then_inc(s_dve, seen.one())
            dve.wait_ge(s_dve, seen.steps)

        def s16(n):
            return g64[:].rearrange("p t g -> p (t g)")[:, 16 * n:16 * n + 16]

        def top16(dve, seen, n, values, work, best, best_i, size):
            for g in range(n):
                nc.vector.max(best[:, g, 0:8], values(g)).then_inc(s_dve, seen.one())
            head_vector(dve, seen)
            dve.wait_ge(s_dve, seen.steps)
            for g in range(n):
                nc.vector.max_index(best_i[:, g, 0:8], best[:, g, 0:8], values(g)).then_inc(s_dve, seen.one())
            head_vector(dve, seen)
            for g in range(n):
                nc.vector.match_replace(work(g), best[:, g, 0:8], values(g), NEG).then_inc(s_dve, seen.one())
            head_vector(dve, seen)
            dve.wait_ge(s_dve, seen.steps)
            for g in range(n):
                nc.vector.max(best[:, g, 8:16], work(g)).then_inc(s_dve, seen.one())
            head_vector(dve, seen)
            dve.wait_ge(s_dve, seen.steps)
            for g in range(n):
                nc.vector.max_index(best_i[:, g, 8:16], best[:, g, 8:16], work(g)).then_inc(s_dve, seen.one())
            head_vector(dve, seen)
            dve.wait_ge(s_dve, seen.steps)

        def pick_vector(dve, seen, t):
            top16(dve, seen, 16, lambda g: pks[:, t, NK * g:NK * (g + 1)], lambda g: pkr[:, NK * g:NK * (g + 1)], v16, i16, NK)
            nc.vector.tensor_copy(f16[:], i16[:]).then_inc(s_dve, seen.one())
            dve.wait_ge(s_dve, seen.steps)
            nc.vector.tensor_scalar(f16[:, H2:16], f16[:, H2:16], float(NK), None, ALU.mult).then_inc(s_dve, seen.one())
            dve.wait_ge(s_dve, seen.steps)
            for src, dst in ((v16, cs), (f16, ci)):
                for i0, i1, nj, at in CAND:
                    ni = i1 - i0
                    nc.vector.tensor_tensor(
                   dst[:, :, at:at + ni * nj].rearrange("p h (i j) -> p h i j", j=nj),
                   src[:, 0:H2, i0:i1].unsqueeze(3).broadcast_to([P, H2, ni, nj]),
                   src[:, H2:16, 0:nj].unsqueeze(2).broadcast_to([P, H2, ni, nj]), ALU.add)\
                        .then_inc(s_dve, seen.one())
            dve.wait_ge(s_dve, seen.steps)
            for rank in (0, 8):
                src = cr if rank else cs
                for h in range(H2):
                    nc.vector.max(bv[:, h, rank:rank + 8], src[:, h]).then_inc(s_dve, seen.one())
                dve.wait_ge(s_dve, seen.steps)
                for h in range(H2):
                    nc.vector.match_replace(cr[:, h], bv[:, h, rank:rank + 8], src[:, h], NEG).then_inc(s_dve, seen.one())
                head_vector(dve, seen)
                dve.wait_ge(s_dve, seen.steps)
            bits = cs[:].bitcast(u32)
            nc.vector.tensor_tensor(key[:, 0], ci[:], K("row_base").rearrange("p (h n) -> p h n", h=H2), ALU.add)\
                .then_inc(s_dve, seen.one())
            nc.vector.tensor_scalar(kbits[:, 1], bits, 16, None, ALU.logical_shift_right).then_inc(s_dve, seen.one())
            nc.vector.tensor_scalar(kbits[:, 2], bits, 0xFFFF, None, ALU.bitwise_and).then_inc(s_dve, seen.one())
            dve.wait_ge(s_dve, seen.steps)
            for m in (1, 2):
                nc.vector.tensor_tensor(key[:, m], kbits[:, m], K("bit_base").rearrange("p (h n) -> p h n", h=H2), ALU.add)\
                    .then_inc(s_dve, seen.one())
            dve.wait_ge(s_dve, seen.steps)
            for m in range(3):
                nc.vector.scalar_tensor_tensor(key[:, m], cr[:], -1.0e38, key[:, m], ALU.is_lt, ALU.mult)\
                    .then_inc(s_dve, seen.one())
            dve.wait_ge(s_dve, seen.steps)
            for m in range(3):
                for h in range(H2):
                    nc.vector.max(best[:, m, h, 0:8], key[:, m, h]).then_inc(s_dve, seen.one())
            head_vector(dve, seen)
            dve.wait_ge(s_dve, seen.steps)
            for m in range(3):
                for h in range(H2):
                    nc.vector.match_replace(key[:, m, h], best[:, m, h, 0:8], key[:, m, h], 0.0).then_inc(s_dve, seen.one())
            dve.wait_ge(s_dve, seen.steps)
            for m in range(3):
                for h in range(H2):
                    nc.vector.max(best[:, m, h, 8:16], key[:, m, h]).then_inc(s_dve, seen.one())
            dve.wait_ge(s_dve, seen.steps)
            nc.vector.tensor_scalar(ibest[:], best[:], -1.0, None, ALU.add).then_inc(s_dve, seen.one())
            dve.wait_ge(s_dve, seen.steps)
            nc.vector.tensor_scalar(idxF[:, t], ibest[:, 0], ROWS_BITS - 1, None, ALU.bitwise_and).then_inc(s_dve, seen.one())
            nc.vector.tensor_scalar(ibest[:, 2], ibest[:, 2], 0xFFFF, None, ALU.bitwise_and).then_inc(s_dve, seen.one())
            dve.wait_ge(s_dve, seen.steps)
            nc.vector.scalar_tensor_tensor(ibest[:, 1], ibest[:, 1], 16, ibest[:, 2], ALU.logical_shift_left,
                                           ALU.bitwise_or).then_inc(s_dve, seen.one())
            dve.wait_ge(s_dve, seen.steps)
            nc.vector.tensor_tensor(wgtF[:, t], ibest[:, 1].bitcast(fp32), bv[:, :, 0:1].broadcast_to([P, H2, PK]),
                                    ALU.subtract).then_inc(s_pk_shift, 1)

        def front_scalar(act, seen):
            for n in range(3):
                act.wait_ge(s_tok_z, seen(s_tok_z))
                parts, pairs = (128, 2) if n < 2 else (64, 1)
                nc.scalar.activation(th[0:parts, 2 * n:2 * n + pairs].rearrange("p a t -> p (a t)"),
                                     ps[n][0:parts, 0:pairs * T], ACT.Tanh,
                                     bias=V("tok_b")[0:parts]).then_inc(s_tok_tanh, 1)
            act.wait_ge(s_tok_shift, seen(s_tok_shift))
            nc.scalar.activation(e9[:], e9[:], ACT.Exp).then_inc(s_tok_exp, 1)
            ln_scalar(act, seen, yT)
            act.wait_ge(s_att_gT, seen(s_att_gT))
            nc.scalar.activation(qT[:, 0], ps[5][0:64, 0:T], ACT.Copy).then_inc(s_att_qk, 1)
            att_scalar(act, seen, C ** -0.5, False)
            ln_scalar(act, seen, yT)
            act.wait_ge(s_l0_shift, seen(s_l0_shift))
            nc.scalar.activation(sc[:], sc[:], ACT.Exp).then_inc(s_l0_e, 1)
            ln_scalar(act, seen, unit=True)
            ln_scalar(act, seen, yT, unit=True)
            act.wait_ge(s_l1_q, seen(s_l1_q))
            nc.scalar.activation(qT[:, 0], ps[0][0:64, 0:T], ACT.Identity, bias=V("l1_bq")[0:64]).then_inc(s_l1_q, 1)
            act.wait_ge(s_l1_var, seen(s_l1_var))
            nc.scalar.activation(g64[:], g64[:], ACT.Sqrt, scale=1.0 / (D1 - 1)).then_inc(s_l1_std, 1)
            act.wait_ge(s_l1_pre, seen(s_l1_pre))
            nc.scalar.activation(u64[:, :, 0:C], t64[:, :, 0:C], ACT.Gelu).then_inc(s_l1_gelu, 1)
            ln_scalar(act, seen, yT, unit=True)
            act.wait_ge(s_e_hT, seen(s_e_hT))
            for c in range(2):
                last = nc.scalar.activation(actT[:, c], ps[0][:, c * T:(c + 1) * T], ACT.Gelu, bias=V("l1_b1")[:, c:c + 1])
            last.then_inc(s_e_act, 1)
            act.wait_ge(s_e_shift, seen(s_e_shift))
            nc.scalar.activation(t64[:, :, 0:E1], t64[:, :, 0:E1], ACT.Exp).then_inc(s_e_exp, 1)
            ln_scalar(act, seen, yT, unit=True)
            act.wait_ge(s_l2_v, seen(s_l2_v))
            nc.scalar.activation(v_sb[:, :, 0:C], ps[5][0:P, 0:128].rearrange("p (t c) -> p t c", t=2),
                                 ACT.Copy).then_inc(s_l2_v, 1)
            att_scalar(act, seen, 64 ** -0.5, True)
            ln_scalar(act, seen, yTF, unit=True)
            act.wait_ge(s_pk_sim, seen(s_pk_sim))
            for k in range(4):
                last = nc.scalar.activation(pks[:, k // 2, 512 * (k % 2):512 * (k % 2) + 512], ps[(0, 1, 2, 5)[k]][0:P, :],
                                            ACT.Copy)
            last.then_inc(s_pk_copied, 1)
            if seen.heads:
                heads_scalar(act, seen)
            act.wait_ge(s_pk_shift, seen(s_pk_shift, 2))
            nc.scalar.activation(wgtF[:], wgtF[:], ACT.Exp).then_inc(s_pk_exp, 1)

        def front_tensor(pe, seen):
            pe.wait_ge(s_x_loaded, seen(s_x_loaded, 48))
            for n in range(5):
                z = ps[n // 2][:, (n % 2) * T:(n % 2 + 1) * T]
                m = 128 if n < 4 else 64
                last = nc.tensor.matmul(z[0:m], W("tok_qry2", 0, m), xT_sb[:, WIN // 2:WIN // 2 + T], start=True, stop=False,
                                        skip_group_check=True)
                for half in range(m // 64):
                    s = 2 * n + half
                    last = nc.tensor.matmul(z[64 * half:64 * half + 64], W("tok_key"), xT_sb[:, s:s + T], start=False,
                                            stop=True, skip_group_check=True)
                if n % 2 or n == 4:
                    last.then_inc(s_tok_z, 1)
            pe.wait_ge(s_tok_tanh, seen(s_tok_tanh, 3))
            for t in range(2):
                for n in range(5):
                    k, cols = (128, 2) if n < 4 else (64, 1)
                    at = t * WIN + 2 * n
                    last = nc.tensor.matmul(ps[3][0:P, at:at + cols], th[0:k, n, tile(t)], V("tok_v")[0:k, 0:cols],
                                            start=True, stop=True)
            last.then_inc(s_tok_score, 1)
            ln_tensor(pe, seen, y)
            nc.tensor.matmul(ps[5][0:64, 0:T], l0_a[:], yT[:], start=True, stop=True).then_inc(s_att_gT, 1)
            pe.wait_ge(s_att_qk, seen(s_att_qk))
            att_tensor(pe, seen, qT[:, 0], yT[:], lambda j: y[:, j])
            ln_tensor(pe, seen, y)
            for t in range(2):
                last = nc.tensor.matmul(ps[3][0:P, 64 * t:64 * t + 64], yT[:, tile(t)], W("gate"), start=True, stop=True)
            last.then_inc(s_l0_logit, 1)
            for n in range(16):
                t, c = divmod(n, 8)
                if n >= 4:
                    pe.wait_ge(s_l0_prod, seen(s_l0_prod))
                nc.tensor.matmul(ps[(0, 1, 2, 5)[n % 4]][0:P, :], yT[:, tile(t)], latt[:, 512 * c:512 * c + 512], start=True,
                                 stop=True).then_inc(s_l0_xw, 1)
            sum_rows(pe, seen)
            pe.wait_ge(s_ln_y, seen(s_ln_y))
            ln_tensor(pe, seen, y, unit=True)
            for t in range(2):
                last = nc.tensor.matmul(ps[3][0:P, 128 * t:128 * t + 128], yT[:, tile(t)], W("l1_kv"), start=True, stop=True)
            last.then_inc(s_l1_qkv, 1)
            nc.tensor.matmul(ps[0][0:64, 0:T], W("l1_q"), yT[:], start=True, stop=True).then_inc(s_l1_q, 1)
            pe.wait_ge(s_l1_kvn, seen(s_l1_kvn))
            for t in range(2):
                last = nc.tensor.matmul(ps[5][0:64, 0:64], kvn[:, t, 0:64], kvn[:, t, 64:128], start=t == 0, stop=t == 1)
            last.then_inc(s_l1_kv, 1)
            pe.wait_ge(s_l1_q, seen(s_l1_q, 2))
            pe.wait_ge(s_l1_m, seen(s_l1_m))
            nc.tensor.matmul(ps[5][0:64, 128:128 + T], m64[:, 0:64], qT[:, 0], start=True, stop=True).then_inc(s_l1_attT, 1)
            pe.wait_ge(s_l1_ret, seen(s_l1_ret))
            for t in range(2):
                last = nc.tensor.matmul(ps[3][0:P, C * t:C * t + C], qT[:, 1, tile(t)], W("l1_proj"), start=True, stop=True)
            last.then_inc(s_l1_proj, 1)
            ln_tensor(pe, seen, y, unit=True)
            for c in range(2):
                last = nc.tensor.matmul(ps[0][:, c * T:(c + 1) * T], W("l1_w1", 128 * c, 128), yT[:], start=True, stop=True)
            last.then_inc(s_e_hT, 1)
            pe.wait_ge(s_e_act, seen(s_e_act))
            for t in range(2):
                for c in range(2):
                    last = nc.tensor.matmul(ps[3][0:P, E1 * t:E1 * t + E1], actT[:, c, tile(t)],
                                            V("l1_wg")[:, E1 * c:E1 * c + E1], start=c == 0, stop=c == 1)
            last.then_inc(s_e_gate, 1)
            for t in range(2):
                for c in range(2):
                    nc.tensor.matmul(ps[1 + t][0:P, :], actT[:, c, tile(t)], V("l1_wd")[:, 512 * c:512 * c + 512],
                                     start=c == 0, stop=False)
                nc.tensor.matmul(ps[1 + t][0:P, :], K("ones")[0:1], R("bd")[0:1], start=False, stop=True)\
                    .then_inc(s_e_y, 1)
            ln_tensor(pe, seen, y, unit=True)
            for n, w in enumerate((l2_qw, l2_kvw)):
                nc.tensor.matmul(ps[0][0:64, n * T:(n + 1) * T], w[:, 0:64], yT[:], start=True, stop=True)
                last = nc.tensor.matmul(ps[1][0:ROPE, n * T:(n + 1) * T], w[:, 64:80], yT[:], start=True, stop=True)
            last.then_inc(s_l2_qkv, 1)
            for t in range(2):
                last = nc.tensor.matmul(ps[5][0:P, C * t:C * t + C], yT[:, tile(t)], l2_kvw[:, 80:144], start=True, stop=True)
            last.then_inc(s_l2_v, 1)
            pe.wait_ge(s_l2_v, seen(s_l2_v, 2))
            pe.wait_ge(s_l2_rope, seen(s_l2_rope))
            att_tensor(pe, seen, qT[:, 0], qT[:, 1], lambda j: v_sb[:, j, 0:C])
            ln_tensor(pe, seen, y, unit=True)
            for k in range(4):
                last = nc.tensor.matmul(ps[(0, 1, 2, 5)[k]][0:P, :], yTF[:, tile(k // 2)],
                                        pk_w[:, 512 * (k % 2):512 * (k % 2) + 512], start=True, stop=True)
            last.then_inc(s_pk_sim, 1)
            pe.wait_ge(s_pk_copied, seen(s_pk_copied))

        def gather_pool(pool, seen):
            for u in range(2 * H2):
                t, h = divmod(u, H2)
                if u >= SLOTS:
                    pool.wait_ge(s_summed, seen(s_summed))
                for k in range(PK):
                    pool.indirect_dma_start(rowbuf[:, u % SLOTS, k], None, table,
                                                bass.IndirectOffsetOnAxis(ap=idxG[:, t, h, k:k + 1], axis=0))\
                        .then_inc(fetched[u % SLOTS], 16)

        def weigh_rows(dve, seen):
            u = seen.unit()
            if u is not None:
                t, h = divmod(u, H2)
                row = rowbuf[:, u % SLOTS]
                dve.wait_ge(fetched[u % SLOTS], (seen.before * len(range(u % SLOTS, 2 * H2, SLOTS)) + u // SLOTS + 1) * (16 * PK))
                nc.vector.tensor_tensor(row, row, wgtG[:, t, h].unsqueeze(2).broadcast_to([P, PK, 2 * C]),
                                        ALU.mult).then_inc(s_weighed, 1)

        def sum_rows(pe, seen):
            u = seen.unit()
            if u is not None:
                if u:
                    pe.wait_ge(s_kept, seen(s_kept))
                pe.wait_ge(s_weighed, seen(s_weighed))
                for k in range(PK):
                    last = nc.tensor.matmul(ps[7][0:P, 0:2 * C], K("ident")[:, 0:P], rowbuf[:, u % SLOTS, k],
                                            start=k == 0, stop=k == PK - 1)
                last.then_inc(s_summed, 1)

        def keep_sum(act, seen):
            u = seen.unit()
            if u is not None:
                t, h = divmod(u, H2)
                act.wait_ge(s_summed, seen(s_summed))
                nc.scalar.activation(kvG[:, t, h], ps[7][0:P, 0:2 * C], ACT.Copy).then_inc(s_kept, 1)

        def head_vector(dve, seen):
            if not seen.heads or seen.head_steps == 2 * H2:
                return
            n, step = divmod(seen.head_steps, 2)
            seen.head_steps += 1
            if step == 0:
                dve.wait_ge(s_m_sim, seen(s_m_sim))
                nc.vector.scalar_tensor_tensor(sm[:].rearrange("p t j -> p (t j)"), ps[2 + n % 2][0:P, 0:2 * T],
                                               C ** -0.5, K("causal"), ALU.mult, ALU.add)\
                    .then_inc(s_dve, seen.one())
                dve.wait_ge(s_dve, seen.steps)
                nc.vector.tensor_reduce(nmax[:, 0], sm[:], AX.X, ALU.max).then_inc(s_dve, seen.one())
                dve.wait_ge(s_dve, seen.steps)
                nc.vector.tensor_scalar(nmax[:, 1], nmax[:, 0], -1.0, None, ALU.mult).then_inc(s_m_max, 1)
            else:
                dve.wait_ge(s_m_exp, seen(s_m_exp))
                nc.vector.reciprocal(rinv[:, n % 2], rsum[:, n % 2]).then_inc(s_m_rinv, 1)

        def heads_vector(dve, seen, units=False):
            while seen.heads and seen.head_steps < 2 * H2:
                head_vector(dve, seen)
                if units and seen.head_steps % 4 == 0:
                    weigh_rows(dve, seen)

        def back_vector(dve, seen):
            h = hB
            dve.wait_ge(s_m_out, seen(s_m_out))
            nc.vector.tensor_tensor(h[:], h[:], ps[5][0:P, 0:128].rearrange("p (t c) -> p t c", t=2), ALU.add)\
                .then_inc(s_dve, seen.one())
            dve.wait_ge(s_dve, seen.steps)

            ln_vector(dve, seen, h, y, unit=True)
            dve.wait_ge(s_l3_q, seen(s_l3_q))
            nc.vector.tensor_scalar(qT[:, 0], ps[0][0:64, 0:T], 0.0, None, ALU.min).then_inc(s_dve, seen.one())
            nc.vector.tensor_scalar(kT[:, 0], ps[0][0:64, 0:T], 0.0, None, ALU.max).then_inc(s_dve, seen.one())
            dve.wait_ge(s_l3_kv, seen(s_l3_kv))
            kx = ps[1][0:P, 0:256].rearrange("p (t c) -> p t c", t=2)
            nc.vector.tensor_scalar(v_sb[:, :, 0:C], kx[:, :, C:2 * C], 1.0 / T, None, ALU.mult)\
                .then_inc(s_dve, seen.one())
            nc.vector.memset(v_sb[:, :, C:C + H3], 1.0).then_inc(s_dve, seen.one())
            nc.vector.tensor_scalar(u64[:, :, 0:C], kx[:, :, 0:C], 0.0, None, ALU.max).then_inc(s_dve, seen.one())
            nc.vector.tensor_scalar(t64[:, :, 0:C], kx[:, :, 0:C], 0.0, None, ALU.min).then_inc(s_l3_pre, 1)
            dve.wait_ge(s_dve, seen.steps)
            dve.wait_ge(s_l3_exp, seen(s_l3_exp))
            nc.vector.tensor_tensor(t64[:, :, 0:C], t64[:, :, 0:C], u64[:, :, 0:C], ALU.add)
            nc.vector.tensor_tensor(qT[:, 0], qT[:, 0], kT[:, 0], ALU.add).then_inc(s_l3_elu, 1)
            dve.wait_ge(s_l3_kvs, seen(s_l3_kvs))
            nc.vector.tensor_tensor(m64[:], ps[5][0:64, 0:72], K("mask3", 64), ALU.mult).then_inc(s_l3_m, 1)
            dve.wait_ge(s_l3_num, seen(s_l3_num))
            num = ps[3][0:P, 0:144].rearrange("p (t c) -> p t c", t=2)
            nc.vector.tensor_scalar(g64[:, :, 0:H3], num[:, :, C:C + H3], 1e-6, None, ALU.add).then_inc(s_dve, seen.one())
            dve.wait_ge(s_dve, seen.steps)
            nc.vector.reciprocal(g64[:, :, 0:H3], g64[:, :, 0:H3]).then_inc(s_dve, seen.one())
            dve.wait_ge(s_dve, seen.steps)
            nc.vector.tensor_scalar(g64[:, :, 0:H3], g64[:, :, 0:H3], float(T), None, ALU.mult)\
                .then_inc(s_dve, seen.one())
            dve.wait_ge(s_dve, seen.steps)
            for t in range(2):
                last = nc.vector.tensor_tensor(
                    t64[:, t, 0:C].rearrange("p (h d) -> p h d", h=H3), num[:, t, 0:C].rearrange("p (h d) -> p h d", h=H3),
                    g64[:, t, 0:H3].unsqueeze(2).broadcast_to([P, H3, D3]), ALU.mult)
            last.then_inc(s_l3_msg, 1)
            dve.wait_ge(s_l3_mm, seen(s_l3_mm))
            nc.vector.tensor_copy(t64[:, :, 0:C], ps[3][0:P, 0:128].rearrange("p (t c) -> p t c", t=2))\
                .then_inc(s_dve, seen.one())
            dve.wait_ge(s_dve, seen.steps)
            ln_vector(dve, seen, t64[:, :, 0:C], u64[:, :, 0:C], unit=True)
            nc.vector.tensor_tensor(u64[:, :, 0:C], u64[:, :, 0:C], two(R("g1")), ALU.mult).then_inc(s_dve, seen.one())
            dve.wait_ge(s_dve, seen.steps)
            nc.vector.tensor_tensor(u64[:, :, 0:C], u64[:, :, 0:C], two(R("b1")), ALU.add).then_inc(s_l3_msg2, 1)
            dve.wait_ge(s_l3_h, seen(s_l3_h))
            nc.vector.tensor_copy(t64[:, :, 0:C], ps[3][0:P, 0:128].rearrange("p (t c) -> p t c", t=2))\
                .then_inc(s_dve, seen.one())
            dve.wait_ge(s_dve, seen.steps)
            ln_vector(dve, seen, t64[:, :, 0:C], u64[:, :, 0:C], unit=True)
            nc.vector.tensor_tensor(u64[:, :, 0:C], u64[:, :, 0:C], two(R("g2")), ALU.mult).then_inc(s_dve, seen.one())
            dve.wait_ge(s_dve, seen.steps)
            nc.vector.tensor_tensor(u64[:, :, 0:C], u64[:, :, 0:C], two(R("b2")), ALU.add).then_inc(s_dve, seen.one())
            dve.wait_ge(s_dve, seen.steps)
            nc.vector.tensor_tensor(u64[:, :, 0:C], u64[:, :, 0:C], y[:], ALU.add).then_inc(s_dve, seen.one())
            dve.wait_ge(s_dve, seen.steps)
            nc.vector.tensor_tensor(h[:], h[:], u64[:, :, 0:C], ALU.add).then_inc(s_dve, seen.one())
            dve.wait_ge(s_dve, seen.steps)

            ln_vector(dve, seen, h, y, unit=True)
            dve.wait_ge(s_c_w, seen(s_c_w))
            nc.vector.tensor_scalar(sm[:, 0], ps[5][0:P, 0:T], R("cap_br"), None, ALU.add).then_inc(s_dve, seen.one())
            dve.wait_ge(s_dve, seen.steps)
            for t in range(2):
                own = K("own")[:, t * T:(t + 1) * T]
                tri = K("tri")[:, t * T:(t + 1) * T]
                nc.vector.tensor_tensor(sm[:, 1], sm[:, 0], own, ALU.mult).then_inc(s_dve, seen.one())
                dve.wait_ge(s_dve, seen.steps)
                nc.vector.tensor_reduce(cnt[:, t:t + 1], sm[:, 1], AX.X, ALU.add).then_inc(s_dve, seen.one())
                dve.wait_ge(s_dve, seen.steps)
                nc.vector.scalar_tensor_tensor(sm[:, 1], sm[:, 0], cnt[:, t:t + 1], tri, ALU.is_equal, ALU.mult)\
                    .then_inc(s_dve, seen.one())
                dve.wait_ge(s_dve, seen.steps)
                nc.vector.scalar_tensor_tensor(sm[:, 1], sm[:, 0], cnt[:, t:t + 1], sm[:, 1], ALU.is_gt, ALU.add)\
                    .then_inc(s_dve, seen.one())
                dve.wait_ge(s_dve, seen.steps)
                nc.vector.tensor_reduce(cnt[:, 2 + t:3 + t], sm[:, 1], AX.X, ALU.add).then_inc(s_dve, seen.one())
                dve.wait_ge(s_dve, seen.steps)
            nc.vector.scalar_tensor_tensor(cnt[:, 4:6], cnt[:, 2:4], float(CAP), cnt[:, 0:2], ALU.is_lt, ALU.mult)\
                .then_inc(s_dve, seen.one())
            dve.wait_ge(s_dve, seen.steps)
            dve.wait_ge(s_c_y, seen(s_c_y))
            nc.vector.tensor_tensor(t64[:, :, 0:C], ps[3][0:P, 0:128].rearrange("p (t c) -> p t c", t=2),
                                    two(R("cap_b2")), ALU.add).then_inc(s_dve, seen.one())
            dve.wait_ge(s_dve, seen.steps)
            nc.vector.tensor_tensor(h[:], h[:], y[:], ALU.add).then_inc(s_dve, seen.one())
            dve.wait_ge(s_dve, seen.steps)
            for t in range(2):
                last = nc.vector.scalar_tensor_tensor(h[:, t], t64[:, t, 0:C], cnt[:, 4 + t:5 + t], h[:, t], ALU.mult, ALU.add)
            last.then_inc(s_c_out, 1)
            dve.wait_ge(s_c_out, seen(s_c_out))

        def heads_scalar(act, seen):
            for n in range(H2 + 1):
                if n < H2:
                    i = n % 2
                    act.wait_ge(s_m_prep, seen(s_m_prep))
                    nc.scalar.activation(kT[:, i], ps[i][0:64, 0:T], ACT.Copy)
                    nc.scalar.activation(qT[:, i], ps[i][0:64, T:2 * T], ACT.Copy).then_inc(s_m_copied, 1)
                if n:
                    j = (n - 1) % 2
                    act.wait_ge(s_m_pT, seen(s_m_pT))
                    nc.scalar.activation(prT[:, j], ps[4 + j][0:P, 0:2 * T], ACT.Copy).then_inc(s_m_pTc, 1)
                    act.wait_ge(s_m_oT, seen(s_m_oT))
                    nc.scalar.activation(outT[:, n - 1], ps[6][0:64, 0:T], ACT.Copy).then_inc(s_m_oTc, 1)
                if n < H2:
                    act.wait_ge(s_m_max, seen(s_m_max))
                    for t in range(2):
                        last = nc.scalar.activation(pr[:, i, t * T:(t + 1) * T], sm[:, t], ACT.Exp,
                                                    bias=nmax[:, 1, t:t + 1], accum_out=rsum[:, i, t:t + 1])
                    last.then_inc(s_m_exp, 1)
                    act.wait_ge(s_m_rinv, seen(s_m_rinv))
                    for t in range(2):
                        last = nc.scalar.activation(pr[:, i, t * T:(t + 1) * T], pr[:, i, t * T:(t + 1) * T], ACT.Copy,
                                                    scale=rinv[:, i, t:t + 1])
                    last.then_inc(s_m_norm, 1)
                if n in (2, 3, 6, 7):
                    keep_sum(act, seen)

        def back_scalar(act, seen):
            ln_scalar(act, seen, yT, unit=True)
            act.wait_ge(s_l3_pre, seen(s_l3_pre))
            nc.scalar.activation(t64[:, :, 0:C], t64[:, :, 0:C], ACT.Exp)
            nc.scalar.activation(qT[:, 0], qT[:, 0], ACT.Exp).then_inc(s_l3_exp, 1)
            act.wait_ge(s_l3_msgT, seen(s_l3_msgT))
            nc.scalar.activation(kT[:, 0], ps[4][0:64, 0:T], ACT.Copy).then_inc(s_l3_msgTc, 1)
            ln_scalar(act, seen, unit=True)
            act.wait_ge(s_l3_msgT, seen(s_l3_msgT))
            nc.scalar.activation(kT[:, 0], ps[4][0:64, 0:T], ACT.Copy).then_inc(s_l3_msgTc, 1)
            act.wait_ge(s_l3_hT, seen(s_l3_hT))
            nc.scalar.activation(actT[:, 0], ps[0][:, 0:T], ACT.Relu).then_inc(s_l3_relu, 1)
            ln_scalar(act, seen, unit=True)
            ln_scalar(act, seen, yT, unit=True)
            act.wait_ge(s_c_hT, seen(s_c_hT))
            for c in range(2):
                last = nc.scalar.activation(actT[:, c], ps[0][:, c * T:(c + 1) * T], ACT.Gelu_apprx_tanh,
                                            bias=V("cap_b1")[:, c:c + 1])
            last.then_inc(s_c_act, 1)

        def heads_tensor(pe, seen):
            for n in range(H2 + 1):
                if n < H2:
                    i = n % 2
                    for t in range(2):
                        nc.tensor.transpose(ps[i][0:64, tile(t)], kvB[:, t, n, 0:C], K("ident")[:, 0:P])
                    nc.tensor.matmul(ps[i][0:64, T:2 * T], W("l2f_q", C * n, C), yTB[:], start=True,
                                     stop=True).then_inc(s_m_prep, 1)
                    pe.wait_ge(s_m_copied, seen(s_m_copied))
                    for t in range(2):
                        last = nc.tensor.matmul(ps[2 + i][0:P, t * T:(t + 1) * T], qT[:, i, tile(t)], kT[:, i],
                                                start=True, stop=True)
                    last.then_inc(s_m_sim, 1)
                if n:
                    j = (n - 1) % 2
                    pe.wait_ge(s_m_norm, seen(s_m_norm))
                    for t in range(2):
                        for k in range(2):
                            last = nc.tensor.transpose(ps[4 + j][0:P, k * T + t * P:k * T + (t + 1) * P],
                                                       pr[:, j, t * T + k * P:t * T + (k + 1) * P], K("ident")[:, 0:P])
                    last.then_inc(s_m_pT, 1)
                    pe.wait_ge(s_m_pTc, seen(s_m_pTc))
                    if n > 1:
                        pe.wait_ge(s_m_oTc, seen(s_m_oTc))
                    for k in range(2):
                        last = nc.tensor.matmul(ps[6][0:64, 0:T], kvB[:, k, n - 1, C:2 * C], prT[:, j, k * T:(k + 1) * T],
                                                start=k == 0, stop=k == 1)
                    last.then_inc(s_m_oT, 1)
                if n in (2, 3, 6, 7):
                    sum_rows(pe, seen)
            pe.wait_ge(s_m_oTc, seen(s_m_oTc))
            for t in range(2):
                for n in range(H2):
                    last = nc.tensor.matmul(ps[5][0:P, C * t:C * t + C], outT[:, n, tile(t)], W("l2f_o", C * n, C),
                                            start=n == 0, stop=n == H2 - 1)
            last.then_inc(s_m_out, 1)

        def back_tensor(pe, seen):
            ln_tensor(pe, seen, y, unit=True)
            nc.tensor.matmul(ps[0][0:64, 0:T], W("l3_q"), yT[:], start=True, stop=True).then_inc(s_l3_q, 1)
            for t in range(2):
                nc.tensor.matmul(ps[1][0:P, 128 * t:128 * t + C], yT[:, tile(t)], W("l3_k"), start=True, stop=True)
                last = nc.tensor.matmul(ps[1][0:P, 128 * t + C:128 * t + 2 * C], yT[:, tile(t)], W("l3_v"), start=True, stop=True)
            last.then_inc(s_l3_kv, 1)
            pe.wait_ge(s_l3_elu, seen(s_l3_elu))
            for t in range(2):
                last = nc.tensor.matmul(ps[5][0:64, 0:72], t64[:, t, 0:C], v_sb[:, t], start=t == 0, stop=t == 1)
            last.then_inc(s_l3_kvs, 1)
            pe.wait_ge(s_l3_m, seen(s_l3_m))
            for t in range(2):
                last = nc.tensor.matmul(ps[3][0:P, 72 * t:72 * t + 72], qT[:, 0, tile(t)], m64[:], start=True, stop=True)
            last.then_inc(s_l3_num, 1)
            pe.wait_ge(s_l3_msg, seen(s_l3_msg))
            for t in range(2):
                last = nc.tensor.transpose(ps[4][0:64, tile(t)], t64[:, t, 0:C], K("ident")[:, 0:P])
            last.then_inc(s_l3_msgT, 1)
            pe.wait_ge(s_l3_msgTc, seen(s_l3_msgTc))
            for t in range(2):
                last = nc.tensor.matmul(ps[3][0:P, C * t:C * t + C], kT[:, 0, tile(t)], W("l3_m"), start=True, stop=True)
            last.then_inc(s_l3_mm, 1)
            sum_rows(pe, seen)
            pe.wait_ge(s_l3_msg2, seen(s_l3_msg2))
            for t in range(2):
                last = nc.tensor.transpose(ps[4][0:64, tile(t)], u64[:, t, 0:C], K("ident")[:, 0:P])
            last.then_inc(s_l3_msgT, 1)
            nc.tensor.matmul(ps[0][:, 0:T], W("l3_w1x"), yT[:], start=True, stop=False)
            pe.wait_ge(s_l3_msgTc, seen(s_l3_msgTc))
            nc.tensor.matmul(ps[0][:, 0:T], W("l3_w1m"), kT[:, 0], start=False, stop=True).then_inc(s_l3_hT, 1)
            pe.wait_ge(s_l3_relu, seen(s_l3_relu))
            for t in range(2):
                last = nc.tensor.matmul(ps[3][0:P, C * t:C * t + C], actT[:, 0, tile(t)], V("l3_w2"), start=True, stop=True)
            last.then_inc(s_l3_h, 1)
            sum_rows(pe, seen)
            pe.wait_ge(s_ln_y, seen(s_ln_y, 2))
            ln_tensor(pe, seen, y, unit=True)
            nc.tensor.matmul(ps[5][0:P, 0:T], W("cap_wr"), yT[:], start=True, stop=True).then_inc(s_c_w, 1)
            for c in range(2):
                last = nc.tensor.matmul(ps[0][:, c * T:(c + 1) * T], W("cap_w1", 128 * c, 128), yT[:], start=True, stop=True)
            last.then_inc(s_c_hT, 1)
            pe.wait_ge(s_c_act, seen(s_c_act))
            for t in range(2):
                for c in range(2):
                    last = nc.tensor.matmul(ps[3][0:P, C * t:C * t + C], actT[:, c, tile(t)],
                                            V("cap_w2")[:, C * c:C * c + C], start=c == 0, stop=c == 1)
            last.then_inc(s_c_y, 1)

        def back_sync(sp, seen, b):
            sp.wait_ge(s_c_out, seen(s_c_out))
            sp.dma_start(out[bass.ds(b, 1)].rearrange("a (t p) c -> p (a t) c", p=P), hB[:])\
                .then_inc(s_stored, 16)
            sp.wait_ge(s_stored, seen(s_stored, 16))

        def turn(b, front, gather, back):
            with nc.Block() as block:
                @block.sync
                def _(sp):
                    seen = Count()
                    if front:
                        front_sync(sp, seen, b)
                    if back:
                        back_sync(sp, seen, b - 2)

                @block.vector
                def _(dve):
                    seen = Count(gather, b - 1, back)
                    if front:
                        front_vector(dve, seen)
                    elif back:
                        heads_vector(dve, seen, units=True)
                    if back:
                        back_vector(dve, seen)
                    for _ in seen.left():
                        weigh_rows(dve, seen)
                    if back:
                        dve.wait_ge(s_stored, seen(s_stored, 16))
                    if gather:
                        nc.vector.tensor_copy(hB[:], hG[:]).then_inc(s_dve, seen.one())
                        nc.vector.tensor_copy(yTB[:], yTG[:]).then_inc(s_dve, seen.one())
                        dve.wait_ge(s_dve, seen.steps)
                    if front:
                        nc.vector.tensor_copy(hG[:], hF[:]).then_inc(s_dve, seen.one())
                        nc.vector.tensor_copy(yTG[:], yTF[:]).then_inc(s_dve, seen.one())
                        nc.vector.tensor_copy(idxG[:], idxF[:]).then_inc(s_dve, seen.one())
                        nc.vector.tensor_copy(wgtG[:], wgtF[:]).then_inc(s_dve, seen.one())
                        dve.wait_ge(s_dve, seen.steps)

                @block.scalar
                def _(act):
                    seen = Count(gather, heads=back)
                    if front:
                        front_scalar(act, seen)
                    elif back:
                        heads_scalar(act, seen)
                    if back:
                        back_scalar(act, seen)
                    for _ in seen.left():
                        keep_sum(act, seen)
                    if gather:
                        act.wait_ge(s_kept, 2 * H2)
                        if back:
                            act.wait_ge(s_m_oT, H2)
                        nc.scalar.activation(kvB[:], kvG[:], ACT.Copy).then_inc(s_act, 1)
                        act.wait_ge(s_act, 1)

                @block.tensor
                def _(pe):
                    seen = Count(gather)
                    if front:
                        front_tensor(pe, seen)
                    if back:
                        heads_tensor(pe, seen)
                        back_tensor(pe, seen)
                    for _ in seen.left():
                        sum_rows(pe, seen)

                @block.gpsimd
                def _(pool):
                    if gather:
                        gather_pool(pool, Count())
            nc.all_engine_barrier(sems_to_clear=cleared)

        eps = sb("eps", [P, 1])
        lattice_raw = rowbuf[0:64].rearrange("p s k c -> p (s k c)")[:, 0:EXPERTS0 * C]
        with nc.Block() as block:
            @block.sync
            def _(sp):
                for dst, src in ((w64_sb[:], w64), (w128_sb[:], w128), (rows_sb[:], rows.partition_broadcast(P)),
                                 (const_sb[:], const), (pk_sb[:, 0], pk_q), (pk_sb[:, 1], pk_k), (lattice_raw, lattice)):
                    sp.dma_start(dst, src).then_inc(s_x_loaded, 16)

            @block.vector
            def _(dve):
                nc.vector.memset(eps[:], 1e-5).then_inc(s_dve, 1)
                dve.wait_ge(s_dve, 1)

            @block.tensor
            def _(pe):
                pe.wait_ge(s_x_loaded, 7 * 16)
                nc.tensor.matmul(ps[0][0:64, 0:64], W("l0_wq"), W("l0_wk"), start=True, stop=True)
                nc.tensor.matmul(ps[0][0:64, 64:144], W("qcomp"), W("q_rcs"), start=True, stop=True)
                nc.tensor.matmul(ps[0][0:64, 144:288], W("kvcomp"), W("kv_rcsv"), start=True, stop=True)\
                    .then_inc(s_setup, 1)
                for g in range(16):
                    last = nc.tensor.matmul(ps[1 + g // 8][0:64, 64 * (g % 8):64 * (g % 8) + 64], pk_sb[:, 0, 64 * g:64 * g + 64],
                                            pk_sb[:, 1, 64 * g:64 * g + 64], start=True, stop=True)
                last.then_inc(s_setup, 1)
                for c in range(8):
                    if c >= 4:
                        pe.wait_ge(s_act, c - 3)
                    for e in range(8):
                        last = nc.tensor.matmul(ps[3 + c % 4][0:64, 64 * e:64 * e + 64],
                                                lattice_raw[:, 64 * (8 * c + e):64 * (8 * c + e) + 64], W("out_w"),
                                                start=True, stop=True)
                    last.then_inc(s_l0_xw, 1)

            @block.scalar
            def _(act):
                for c in range(8):
                    act.wait_ge(s_l0_xw, c + 1)
                    nc.scalar.activation(latt[:, 512 * c:512 * c + 512], ps[3 + c % 4][0:64, :], ACT.Copy)\
                        .then_inc(s_act, 1)
                act.wait_ge(s_setup, 2)
                nc.scalar.activation(l0_a[:], ps[0][0:64, 0:64], ACT.Copy)
                nc.scalar.activation(l2_qw[:], ps[0][0:64, 64:144], ACT.Copy)
                nc.scalar.activation(l2_kvw[:], ps[0][0:64, 144:288], ACT.Copy)
                for c in range(2):
                    last = nc.scalar.activation(pk_w[:, 512 * c:512 * c + 512], ps[1 + c][0:64, :], ACT.Copy)
                last.then_inc(s_act, 1)
                act.wait_ge(s_act, 9)
        nc.all_engine_barrier(sems_to_clear=cleared)

        turn(0, True, False, False)
        turn(1, True, True, False)
        with nc.Fori(2, B) as b:
            turn(b, True, True, True)
        turn(B, False, True, True)
        turn(B + 1, False, False, True)


def kernel(**inputs):
    import concourse.bacc as bacc
    from concourse.bass_utils import run_bass_kernel_spmd

    f = {k: np.asarray(v) for k, v in inputs.items()}

    def pack(table, parts, have):
        cols = []
        for name, n in table:
            a = np.asarray(have[name]).reshape(-1, n)
            cols.append(np.pad(a, ((0, parts - a.shape[0]), (0, 0))))
        return np.ascontiguousarray(np.concatenate(cols, axis=1), dtype=np.float32)

    qkv = f["L1_attn_W_qkv"].reshape(H1, 3, D1, C)
    bqkv = f["L1_attn_b_qkv"].reshape(H1, 3, D1)
    swap = np.arange(ROPE) ^ 1
    halves = lambda a: np.concatenate([a[:128], a[128:]], axis=1)
    w64 = pack(W64, 64, {
        "tok_key": f["L0_tok_W_key"], "tok_qry2": np.concatenate([f["L0_tok_W_qry"]] * 2, axis=1),
        "l0_wq": f["L0_attn_Wq"], "l0_wk": f["L0_attn_Wk"], "gate": f["L0_ffn_gate_w"].T, "out_w": f["L0_ffn_out_w"].T,
        "l1_q": qkv[:, 0].reshape(C, C).T,
        "l1_kv": np.concatenate([qkv[:, 1].reshape(C, C).T, qkv[:, 2].reshape(C, C).T], axis=1),
        "l1_proj": f["L1_attn_W_proj"].T, "l1_w1": f["L1_ffn_W1"],
        "qcomp": f["L2_attn_Wq_comp"].T, "kvcomp": f["L2_attn_Wkv_comp"].T,
        "q_rcs": np.concatenate([f["L2_attn_Wqr"], f["L2_attn_Wqc"], f["L2_attn_Wqr"][:, swap]], axis=1),
        "kv_rcsv": np.concatenate([f["L2_attn_Wkr"], f["L2_attn_Wkc"], f["L2_attn_Wkr"][:, swap], f["L2_attn_Wv"]], axis=1),
        "l2f_q": f["L2_ffn_Wq"], "l2f_o": f["L2_ffn_Wo"].reshape(H2, C, C).transpose(1, 0, 2).reshape(C, H2 * C),
        "l3_q": f["L3_attn_Wq"], "l3_k": f["L3_attn_Wk"], "l3_v": f["L3_attn_Wv"], "l3_m": f["L3_attn_Wm"],
        "l3_w1x": f["L3_attn_W1"][:C], "l3_w1m": f["L3_attn_W1"][C:], "cap_w1": f["L3_ffn_w1"],
        "cap_wr": np.repeat(f["L3_ffn_wr"], P, axis=1)})
    zero = np.zeros((C, 1), np.float32)
    tv, tb = f["L0_tok_v"].reshape(C, 1), f["L0_tok_b"].reshape(C, 1)
    w128 = pack(W128, 128, {
        "tok_v": np.concatenate([np.concatenate([tv, zero], 1), np.concatenate([zero, tv], 1)]),
        "tok_b": np.concatenate([tb, tb]), "l1_bq": bqkv[:, 0].reshape(C, 1),
        "l1_b1": f["L1_ffn_b1"].reshape(2, 128).T, "cap_b1": f["L3_ffn_b1"].reshape(2, 128).T,
        "l1_wg": halves(f["L1_ffn_Wg"]), "l1_wd": halves(f["L1_ffn_Wd"].transpose(1, 0, 2).reshape(HID, E1 * C)),
        "l3_w2": f["L3_attn_W2"], "cap_w2": halves(f["L3_ffn_w2"])})
    kvw = lambda a, b: np.concatenate([a.reshape(-1), b.reshape(-1)])
    rows = {
        "out_b": f["L0_ffn_out_b"], "ln_g": f["L0_ffn_ln_g"], "ln_b": f["L0_ffn_ln_b"],
        "l1_bkv": kvw(bqkv[:, 1], bqkv[:, 2]), "l1_w": kvw(f["L1_attn_kln_w"], f["L1_attn_vln_w"]),
        "l1_b": kvw(f["L1_attn_kln_b"], f["L1_attn_vln_b"]), "l1_bproj": f["L1_attn_b_proj"], "l1_bg": f["L1_ffn_bg"],
        "g1": f["L3_attn_g1"], "b1": f["L3_attn_b1"], "g2": f["L3_attn_g2"], "b2": f["L3_attn_b2"],
        "cap_b2": f["L3_ffn_b2"], "cap_br": f["L3_ffn_br"], "bd": f["L1_ffn_bd"].reshape(-1)}
    rows = np.concatenate([np.asarray(rows[n], np.float32) for n, _ in ROWS])

    i, j = np.arange(T)[:, None], np.arange(T)[None, :]
    tiles = lambda m: m.reshape(2, P, T).transpose(1, 0, 2).reshape(P, 2 * T)
    half = ROPE // 2
    theta = (1.0 / np.float32(10000.0) ** (np.arange(half, dtype=np.float32) / np.float32(half))).astype(np.float32)
    angle = (np.arange(T, dtype=np.float32)[:, None] * theta[None, :]).T
    cos = np.ones((C, T), np.float32)
    cos[:ROPE] = np.repeat(np.cos(angle), 2, axis=0)
    sin = np.repeat(np.sin(angle), 2, axis=0)
    sin[0::2] *= -1
    place = np.arange(n_cand)
    block = lambda n, d: np.kron(np.eye(n), np.ones((d, d)))
    const = pack(CONST, 128, {
        "ident": np.eye(128), "causal": tiles(np.where(j <= i, 0.0, -1.0e38)), "tri": tiles((j < i) * 1.0),
        "own": tiles((i == j) * 1.0), "row_base": np.broadcast_to(np.add.outer(np.arange(H2) * NKV, place * ROWS_BITS + 1).reshape(-1), (P, H2 * n_cand)),
        "bit_base": np.broadcast_to(np.tile(place * 65536 + 1, H2), (P, H2 * n_cand)), "cos": cos, "sin": sin,
        "mask1": block(H1, D1) / T, "mask3": np.concatenate([block(H3, D3), np.kron(np.eye(H3), np.ones((D3, 1)))], axis=1),
        "ones": np.ones((1, P))})
    arrays = {
        "x": f["x"], "xT": np.ascontiguousarray(f["x"].transpose(0, 2, 1)), "w64": w64, "w128": w128,
        "lattice": np.ascontiguousarray(f["L0_ffn_lattice_weights"].transpose(2, 0, 1).reshape(C, EXPERTS0 * C)),
        "pk_q": np.ascontiguousarray(f["L2_ffn_Wq_pk"].reshape(C, 16, 32).transpose(2, 1, 0).reshape(32, 16 * C)),
        "pk_k": np.ascontiguousarray(f["L2_ffn_pk_keys"].transpose(3, 0, 2, 1).reshape(32, 16 * NK)),
        "rows": rows, "const": const,
        "table": np.concatenate([f["L2_ffn_keys_table"], f["L2_ffn_values_table"]], axis=1)}
    nc = bacc.Bacc("TRN2", target_bir_lowering=False, num_devices=1)
    args = [nc.dram_tensor(n, a.shape, mybir.dt.from_np(a.dtype), kind="ExternalInput").ap() for n, a in arrays.items()]
    out = nc.dram_tensor("out", (B, T, C), mybir.dt.float32, kind="ExternalOutput").ap()
    tower(nc, *args, out)
    r = run_bass_kernel_spmd(nc, [arrays], core_ids=[0])
    return r.results[0]["out"]
```

```python
from contextlib import ExitStack

import numpy as np
import concourse.bass as bass
from concourse import mybir

B, T_IN, C = 16, 250, 64
WIN = 9
T = T_IN - WIN + 1
P = T // 2
TOPK_E, EXPERTS0 = 6, 64
H1, D1 = 16, 4
HID, E1 = 256, 8
ROPE = 16
H2, NK, PK = 8, 64, 16
NKV = NK * NK
H3, D3 = 8, 8
CAP = T // 2 - 1
UNITS = 2 * H2
HELD = 2
EARLY = 2
SHARED = 8
SLOTS = 6
ROWS_BITS = H2 * NKV
NEG = -3.0e38
MASKED = -1.0e30

CAND, n_cand = [], 0
for i0, i1 in ((0, 1), (1, 2), (2, 3), (3, 4), (4, 5), (5, 8), (8, 16)):
    CAND.append((i0, i1, PK // (i0 + 1), n_cand))
    n_cand += (i1 - i0) * (PK // (i0 + 1))

W64 = [("tok_key", 64), ("tok_qry2", 128), ("l0_wq", 64), ("l0_wk", 64), ("gate", 64), ("out_w", 64),
       ("l1_q", 64), ("l1_kv", 128), ("l1_proj", 64), ("l1_w1", HID), ("qcomp", 64), ("kvcomp", 64),
       ("q_rcs", 80), ("kv_rcsv", 144), ("l2f_q", 512), ("l2f_o", 512), ("l3_q", 64), ("l3_k", 64),
       ("l3_v", 64), ("l3_m", 64), ("l3_w1x", 128), ("l3_w1m", 128), ("cap_w1", HID), ("cap_wr", P)]
W128 = [("tok_v", 2), ("tok_b", 1), ("l1_bq", 1), ("l1_b1", 2), ("cap_b1", 2), ("l1_wg", 2 * E1),
        ("l1_wd", 2 * E1 * C), ("l3_w2", C), ("cap_w2", 2 * C)]
ROWS = [("out_b", 64), ("ln_g", 64), ("ln_b", 64), ("l1_bkv", 128), ("l1_w", 128), ("l1_b", 128),
        ("l1_bproj", 64), ("l1_bg", E1), ("g1", 64), ("b1", 64), ("g2", 64), ("b2", 64),
        ("cap_b2", 64), ("cap_br", 1), ("bd", E1 * C)]
CONST = [("ident", 128), ("causal", P), ("tri", 2 * T), ("own", 2 * T), ("high_key", H2 * n_cand),
         ("low_key", H2 * n_cand), ("cos", T), ("sin", T), ("mask1", 64), ("mask3", 72), ("ones", P)]


def places(table):
    out, at = {}, 0
    for name, n in table:
        out[name] = (at, at + n)
        at += n
    return out, at


class Count:

    def __init__(self, work=None, heads=False):
        self.values, self.steps = {}, 0
        self.work = work or Work(0)
        self.heads, self.head_steps = heads, 0
        self.units = 0

    def __call__(self, sem, n=1):
        self.values[sem.name] = self.values.get(sem.name, 0) + n
        return self.values[sem.name]

    def one(self):
        self.steps += 1
        return 1

    def unit(self):
        if self.units == len(self.work.sums):
            return None, False
        self.units += 1
        return self.work.sums[self.units - 1]

    def left(self):
        return range(len(self.work.sums) - self.units)


class Work:

    def __init__(self, batch, fetched=(), held=(), fresh=(), last=False, final=False):
        self.batch, self.fetched = batch, fetched
        self.held = held
        self.sums = [(u, True) for u in held] + [(u, False) for u in fresh]
        self.last = last
        self.final = final

    def place(self, u, held):
        return (u % 2, u // 2) if self.last and not held else divmod(u, H2)

    def freed(self, u):
        for n, (v, held) in enumerate(self.sums):
            if (v == u - SLOTS and not held) or (held and u < SLOTS and v % SLOTS == u):
                return n + 1
        return 0


def tower(nc, x, xT, w64, w128, lattice, pk_q, pk_k, rows, const, table, out):
    fp32, u32 = mybir.dt.float32, mybir.dt.uint32
    ALU, ACT, AX = mybir.AluOpType, mybir.ActivationFunctionType, mybir.AxisListType
    p64, n64 = places(W64)
    p128, n128 = places(W128)
    prow, nrow = places(ROWS)
    pconst, nconst = places(CONST)
    ctx = ExitStack()

    def sb(name, shape, dt=fp32):
        return ctx.enter_context(nc.sbuf_tensor(name, shape, dt))

    with ctx:
        w64_sb, w128_sb = sb("w64_sb", [64, n64]), sb("w128_sb", [128, n128])
        rows_sb, const_sb = sb("rows_sb", [P, nrow]), sb("const_sb", [128, nconst])
        pk_sb = sb("pk_sb", [32, 2, 16 * 64])
        l0_a = sb("l0_a", [64, 64])
        latt = sb("latt", [64, EXPERTS0 * C])
        l2_qw, l2_kvw = sb("l2_qw", [64, 80]), sb("l2_kvw", [64, 144])
        pk_w = sb("pk_w", [64, 16 * NK])
        hF, hG, hB = sb("hF", [P, 2, C]), sb("hG", [P, 2, C]), sb("hB", [P, 2, C])
        yTF, yTG, yTB = sb("yTF", [C, T]), sb("yTG", [C, T]), sb("yTB", [C, T])
        idxF, idxG = sb("idxF", [P, 2, H2, PK], u32), sb("idxG", [P, 2, H2, PK], u32)
        wgtF, wgtG = sb("wgtF", [P, 2, H2, PK]), sb("wgtG", [P, 2, H2, PK])
        wgtH = sb("wgtH", [P, HELD, PK])
        rowbuf = sb("rowbuf", [P, SLOTS, PK, 2 * C])
        kvG, kvB = sb("kvG", [P, 2, H2, 2 * C]), sb("kvB", [P, 2, H2, 2 * C])
        xT_sb, xwin = sb("xT_sb", [C, T_IN]), sb("xwin", [P, 2, WIN * C])
        e9, s2 = sb("e9", [P, 2, WIN]), sb("s2", [P, 4, 2])
        y, yT = sb("y", [P, 2, C]), sb("yT", [C, T])
        stat, mv, std, rstd = sb("stat", [P, 2, 6]), sb("mv", [P, 2, 2]), sb("std", [P, 2]), sb("rstd", [P, 2])
        qT, kT = sb("qT", [C, 2, T]), sb("kT", [C, 2, T])
        sm, pr, prT = sb("sm", [P, 2, T]), sb("pr", [P, 2, 2 * T]), sb("prT", [P, 2, 2 * T])
        nmax, rsum, rinv = sb("nmax", [P, 2]), sb("rsum", [P, 2, 2]), sb("rinv", [P, 2, 2])
        lg, m8, rep, sc = sb("lg", [P, 2, 64]), sb("m8", [P, 2, 8]), sb("rep", [P, 2, 64]), sb("sc", [P, 2, 64])
        lw = sb("lw", [P, 4, 512])
        t64, u64 = sb("t64", [P, 2, 2 * C]), sb("u64", [P, 2, 2 * C])
        kvn = sb("kvn", [P, 2, 2 * C])
        g64 = sb("g64", [P, 2, 32])
        m64 = sb("m64", [64, 72])
        actT = sb("actT", [128, 2, T])
        rope2 = sb("rope2", [ROPE, 2, T])
        v_sb = sb("v_sb", [P, 2, 72])
        pks_all = sb("pks_all", [128, 2 * 16 * NK])
        pks = pks_all[0:P].rearrange("p (t n) -> p t n", t=2)
        th = pks_all[:, 0:5 * T].rearrange("p (n t) -> p n t", n=5)
        pkr = xwin[:].rearrange("p t n -> p (t n)")[:, 0:16 * NK]
        v16, i16 = sb("v16", [P, 16, PK]), sb("i16", [P, 16, PK], u32)
        cs, cr, ci = sb("cs", [P, H2, n_cand]), sb("cr", [P, H2, n_cand]), sb("ci", [P, H2, n_cand], u32)
        bv = sb("bv", [P, H2, PK])
        key_all = lw[:].rearrange("p a b -> p (a b)")[:, 0:2 * H2 * n_cand]
        key = key_all.rearrange("p (m h n) -> p m h n", m=2, h=H2)
        kbits = key_all.bitcast(u32).rearrange("p (m h n) -> p m h n", m=2, h=H2)
        best, sbits = sb("best", [P, 2, H2, PK]), sb("sbits", [P, H2, PK], u32)
        outT = sb("outT", [C, 2, T])
        cnt = sb("cnt", [P, 8])
        ps = [ctx.enter_context(nc.psum_tensor(f"ps{i}", [128, 512], fp32)) for i in range(8)]

        def W(name, lo=0, n=None):
            a, b = p64[name]
            return w64_sb[:, a + lo:(a + lo + n if n else b)]

        def V(name):
            a, b = p128[name]
            return w128_sb[:, a:b]

        def R(name):
            a, b = prow[name]
            return rows_sb[:, a:b]

        def K(name, parts=P):
            a, b = pconst[name]
            return const_sb[0:parts, a:b]

        def two(row):
            return row.unsqueeze(1).broadcast_to([P, 2, row.shape[1]])

        def tile(t):
            return slice(t * P, (t + 1) * P)

        def sem(name):
            return ctx.enter_context(nc.semaphore(name))

        s_x_loaded = sem("x_loaded")
        s_dve = sem("dve")
        s_act = sem("act")
        s_ln_var = sem("ln_var")
        s_ln_std = sem("ln_std")
        s_ln_y = sem("ln_y")
        s_ln_yT = sem("ln_yT")
        s_yT_ready = sem("yT_ready")
        s_tok_z = sem("tok_z")
        s_tok_tanh = sem("tok_tanh")
        s_tok_score = sem("tok_score")
        s_tok_shift = sem("tok_shift")
        s_tok_exp = sem("tok_exp")
        s_att_gT = sem("att_gT")
        s_att_qk = sem("att_qk")
        s_att_sim = sem("att_sim")
        s_att_max = sem("att_max")
        s_att_exp = sem("att_exp")
        s_att_pT = sem("att_pT")
        s_att_pTc = sem("att_pTc")
        s_att_out = sem("att_out")
        s_l0_logit = sem("l0_logit")
        s_l0_shift = sem("l0_shift")
        s_l0_e = sem("l0_e")
        s_l0_xw = sem("l0_xw")
        s_l0_prod = sem("l0_prod")
        s_l1_qkv = sem("l1_qkv")
        s_l1_q = sem("l1_q")
        s_l1_var = sem("l1_var")
        s_l1_std = sem("l1_std")
        s_l1_kvn = sem("l1_kvn")
        s_l1_kv = sem("l1_kv")
        s_l1_m = sem("l1_m")
        s_l1_attT = sem("l1_attT")
        s_l1_ret = sem("l1_ret")
        s_l1_proj = sem("l1_proj")
        s_l1_pre = sem("l1_pre")
        s_l1_gelu = sem("l1_gelu")
        s_e_hT = sem("e_hT")
        s_e_act = sem("e_act")
        s_e_gate = sem("e_gate")
        s_e_shift = sem("e_shift")
        s_e_exp = sem("e_exp")
        s_e_y = sem("e_y")
        s_l2_qkv = sem("l2_qkv")
        s_l2_rope = sem("l2_rope")
        s_l2_v = sem("l2_v")
        s_pk_sim = sem("pk_sim")
        s_pk_copied = sem("pk_copied")
        s_handed = sem("handed")
        s_early = sem("early")
        s_lattice = sem("lattice")
        s_fold = sem("fold")
        s_folded = sem("folded")
        s_pk_shift = sem("pk_shift")
        s_pk_exp = sem("pk_exp")
        s_m_prep = sem("m_prep")
        s_m_copied = sem("m_copied")
        s_m_sim = sem("m_sim")
        s_m_max = sem("m_max")
        s_m_exp = sem("m_exp")
        s_m_rinv = sem("m_rinv")
        s_m_norm = sem("m_norm")
        s_m_pT = sem("m_pT")
        s_m_pTc = sem("m_pTc")
        s_m_oT = sem("m_oT")
        s_m_oTc = sem("m_oTc")
        s_m_out = sem("m_out")
        s_l3_q = sem("l3_q")
        s_l3_kv = sem("l3_kv")
        s_l3_pre = sem("l3_pre")
        s_l3_exp = sem("l3_exp")
        s_l3_elu = sem("l3_elu")
        s_l3_kvs = sem("l3_kvs")
        s_l3_m = sem("l3_m")
        s_l3_num = sem("l3_num")
        s_l3_msg = sem("l3_msg")
        s_l3_msgT = sem("l3_msgT")
        s_l3_msgTc = sem("l3_msgTc")
        s_l3_mm = sem("l3_mm")
        s_l3_msg2 = sem("l3_msg2")
        s_l3_hT = sem("l3_hT")
        s_l3_relu = sem("l3_relu")
        s_l3_h = sem("l3_h")
        s_c_w = sem("c_w")
        s_c_hT = sem("c_hT")
        s_c_act = sem("c_act")
        s_c_y = sem("c_y")
        s_c_out = sem("c_out")
        s_weighed = sem("weighed")
        s_summed = sem("summed")
        s_kept = sem("kept")
        s_stored = sem("stored")
        s_setup = sem("setup")
        fetched = [ctx.enter_context(nc.semaphore(f"fetched{i}")) for i in range(SLOTS)]
        cleared = range(s_x_loaded.num, s_setup.num + 1)

        def ln_vector(dve, seen, h, dst, unit=False):
            for t in range(2):
                nc.vector.bn_stats(stat[:, t], h[:, t]).then_inc(s_dve, seen.one())
            dve.wait_ge(s_dve, seen.steps)
            nc.vector.bn_aggr(mv[:, 0], stat[:, 0])
            nc.vector.bn_aggr(mv[:, 1], stat[:, 1]).then_inc(s_ln_var, 1)
            if unit:
                weigh_rows(dve, seen)
            dve.wait_ge(s_ln_std, seen(s_ln_std))
            nc.vector.reciprocal(rstd[:], std[:]).then_inc(s_dve, seen.one())
            dve.wait_ge(s_dve, seen.steps)
            for t in range(2):
                last = nc.vector.tensor_scalar(dst[:, t], h[:, t], mv[:, t, 0:1], rstd[:, t:t + 1], ALU.subtract, ALU.mult)
            last.then_inc(s_ln_y, 1)
            dve.wait_ge(s_ln_y, seen(s_ln_y))

        def ln_scalar(act, seen, dst=None, unit=False):
            act.wait_ge(s_ln_var, seen(s_ln_var))
            nc.scalar.activation(std[:], mv[:, :, 1], ACT.Sqrt, bias=eps[:]).then_inc(s_ln_std, 1)
            if unit:
                keep_sum(act, seen)
            if dst is not None:
                act.wait_ge(s_ln_yT, seen(s_ln_yT))
                nc.scalar.activation(dst[:], ps[4][0:64, 0:T], ACT.Copy).then_inc(s_yT_ready, 1)

        def ln_tensor(pe, seen, src, unit=False):
            if unit:
                sum_rows(pe, seen)
            pe.wait_ge(s_ln_y, seen(s_ln_y))
            for t in range(2):
                last = nc.tensor.transpose(ps[4][0:64, tile(t)], src[:, t], K("ident")[:, 0:P])
            last.then_inc(s_ln_yT, 1)
            pe.wait_ge(s_yT_ready, seen(s_yT_ready))

        def slot(j, t):
            return (t if j == 0 else 3 - t) * P

        def sims(bank, q, k, causal):
            for t in range(2):
                n = P if causal and t == 0 else T
                last = nc.tensor.matmul(bank[0:P, t * T:t * T + n], q[:, tile(t)], k[:, 0:n], start=True, stop=not causal,
                                        skip_group_check=True)
                if causal:
                    last = nc.tensor.matmul(bank[0:P, t * (T + P):t * (T + P) + P], K("ident")[:, 0:P], K("causal"),
                                            start=False, stop=True, skip_group_check=True)
            return last

        def maxima(bank, sem, causal):
            if causal:
                nc.vector.tensor_reduce(nmax[:, 0:1], bank[0:P, 0:P], AX.X, ALU.max, negate=True)
                nc.vector.tensor_reduce(nmax[:, 1:2], bank[0:P, T:2 * T], AX.X, ALU.max, negate=True).then_inc(sem, 1)
            else:
                nc.vector.tensor_reduce(nmax[:], bank[0:P, 0:2 * T].rearrange("p (t j) -> p t j", t=2), AX.X, ALU.max,
                                        negate=True).then_inc(sem, 1)

        def exps(bank, i, causal):
            for t in range(2):
                n = P if causal and t == 0 else T
                last = nc.scalar.activation(pr[:, i, t * T:t * T + n], bank[0:P, t * T:t * T + n], ACT.Exp,
                                            bias=nmax[:, t:t + 1], accum_out=rsum[:, i, t:t + 1])
            return last

        def prs_T(bank, i, causal):
            for j, t in ((0, 0), (0, 1), (1, 1)) if causal else ((0, 0), (0, 1), (1, 1), (1, 0)):
                last = nc.tensor.transpose(bank[0:P, slot(j, t):slot(j, t) + P], pr[:, i, t * T + j * P:t * T + (j + 1) * P],
                                           K("ident")[:, 0:P])
            return last

        def att_vector(dve, seen, h, causal):
            dve.wait_ge(s_att_sim, seen(s_att_sim))
            maxima(ps[6], s_att_max, causal)
            dve.wait_ge(s_att_exp, seen(s_att_exp))
            nc.vector.reciprocal(rinv[:, 0], rsum[:, 0]).then_inc(s_dve, seen.one())
            dve.wait_ge(s_dve, seen.steps)
            dve.wait_ge(s_att_out, seen(s_att_out))
            for t in range(2):
                nc.vector.scalar_tensor_tensor(h[:, t], ps[3][0:P, t * C:(t + 1) * C], rinv[:, 0, t:t + 1],
                                               h[:, t], ALU.mult, ALU.add).then_inc(s_dve, seen.one())
            dve.wait_ge(s_dve, seen.steps)

        def att_scalar(act, seen, causal):
            act.wait_ge(s_att_max, seen(s_att_max))
            exps(ps[6], 0, causal).then_inc(s_att_exp, 1)
            act.wait_ge(s_att_pT, seen(s_att_pT))
            n = (3 if causal else 4) * P
            nc.scalar.activation(prT[:, 0, 0:n], ps[2][0:P, 0:n], ACT.Copy).then_inc(s_att_pTc, 1)

        def att_tensor(pe, seen, q, k, val, causal):
            sims(ps[6], q, k, causal).then_inc(s_att_sim, 1)
            pe.wait_ge(s_att_exp, seen(s_att_exp))
            prs_T(ps[2], 0, causal).then_inc(s_att_pT, 1)
            pe.wait_ge(s_att_pTc, seen(s_att_pTc))
            for t in range(2):
                own = range(1 if causal and t == 0 else 2)
                for j in own:
                    last = nc.tensor.matmul(ps[3][0:P, t * C:(t + 1) * C], prT[:, 0, slot(j, t):slot(j, t) + P],
                                            val(j), start=j == 0, stop=j == own[-1])
            last.then_inc(s_att_out, 1)

        lattice_raw = rowbuf[0:64].rearrange("p s k c -> p (s k c)")[:, 0:EXPERTS0 * C]

        def fold_tensor(pe):
            pe.wait_ge(s_lattice, 16)
            for c in range(8):
                if c >= 4:
                    pe.wait_ge(s_folded, c - 3)
                for e in range(8):
                    last = nc.tensor.matmul(ps[(0, 1, 2, 5)[c % 4]][0:64, 64 * e:64 * e + 64],
                                            lattice_raw[:, 64 * (8 * c + e):64 * (8 * c + e) + 64], W("out_w"),
                                            start=True, stop=True)
                last.then_inc(s_fold, 1)
            pe.wait_ge(s_folded, 8)

        def fold_scalar(act):
            for c in range(8):
                act.wait_ge(s_fold, c + 1)
                nc.scalar.activation(latt[:, 512 * c:512 * c + 512], ps[(0, 1, 2, 5)[c % 4]][0:64, :], ACT.Copy)\
                    .then_inc(s_folded, 1)

        def front_sync(sp, seen, b):
            sp.dma_start(xT_sb[:], xT[bass.ds(b, 1)].rearrange("a c t -> (a c) t")).then_inc(s_x_loaded, 16)
            for t in range(2):
                src = bass.AP(x.tensor, b * (T_IN * C) + t * P * C, [[C, P], [1, WIN * C]])
                sp.dma_start(xwin[:, t], src).then_inc(s_x_loaded, 16)

        def front_vector(dve, seen, early):
            h = hF
            for _ in seen.work.held:
                weigh_rows(dve, seen)
            dve.wait_ge(s_tok_score, seen(s_tok_score))
            score = ps[3][0:P, 0:2 * WIN].rearrange("p (t s) -> p t s", t=2)
            nc.vector.tensor_reduce(s2[:, 0], score, AX.X, ALU.max).then_inc(s_dve, seen.one())
            dve.wait_ge(s_dve, seen.steps)
            nc.vector.tensor_tensor(e9[:], score, s2[:, 0].unsqueeze(2).broadcast_to([P, 2, WIN]),
                                    ALU.subtract).then_inc(s_tok_shift, 1)
            dve.wait_ge(s_tok_exp, seen(s_tok_exp))
            nc.vector.tensor_reduce(s2[:, 1], e9[:], AX.X, ALU.add).then_inc(s_dve, seen.one())
            dve.wait_ge(s_dve, seen.steps)
            nc.vector.reciprocal(s2[:, 2], s2[:, 1]).then_inc(s_dve, seen.one())
            dve.wait_ge(s_dve, seen.steps)
            nc.vector.tensor_tensor(e9[:], e9[:], s2[:, 2].unsqueeze(2).broadcast_to([P, 2, WIN]), ALU.mult)\
                .then_inc(s_dve, seen.one())
            dve.wait_ge(s_dve, seen.steps)
            dve.wait_ge(s_x_loaded, seen(s_x_loaded, 48))
            for t in range(2):
                win = xwin[:, t].rearrange("p (s c) -> p s c", s=WIN)
                nc.vector.tensor_tensor(win, win, e9[:, t].unsqueeze(2).broadcast_to([P, WIN, C]), ALU.mult)\
                    .then_inc(s_dve, seen.one())
            dve.wait_ge(s_dve, seen.steps)
            for t in range(2):
                nc.vector.tensor_reduce(h[:, t], xwin[:, t].rearrange("p (s c) -> p c s", s=WIN), AX.X, ALU.add)\
                    .then_inc(s_dve, seen.one())
            dve.wait_ge(s_dve, seen.steps)

            ln_vector(dve, seen, h, y, unit=True)
            att_vector(dve, seen, h, False)

            ln_vector(dve, seen, h, y, unit=True)
            dve.wait_ge(s_l0_logit, seen(s_l0_logit))
            nc.vector.tensor_copy(lg[:], ps[3][0:P, 0:128].rearrange("p (t e) -> p t e", t=2)).then_inc(s_dve, seen.one())
            dve.wait_ge(s_dve, seen.steps)
            for t in range(2):
                nc.vector.max(m8[:, t], lg[:, t]).then_inc(s_dve, seen.one())
            dve.wait_ge(s_dve, seen.steps)
            nc.vector.tensor_scalar(s2[:, 0], m8[:, :, 0], 1.0, None, ALU.mult).then_inc(s_dve, seen.one())
            dve.wait_ge(s_dve, seen.steps)
            nc.vector.memset(m8[:, :, TOPK_E:8], NEG).then_inc(s_dve, seen.one())
            nc.vector.tensor_tensor(sc[:], lg[:], s2[:, 0].unsqueeze(2).broadcast_to([P, 2, 64]),
                                    ALU.subtract).then_inc(s_l0_shift, 1)
            dve.wait_ge(s_dve, seen.steps)
            for t in range(2):
                nc.vector.match_replace(rep[:, t], m8[:, t], lg[:, t], NEG).then_inc(s_dve, seen.one())
            dve.wait_ge(s_dve, seen.steps)
            dve.wait_ge(s_l0_e, seen(s_l0_e))
            for t in range(2):
                nc.vector.scalar_tensor_tensor(sc[:, t], rep[:, t], -1.0e38, sc[:, t], ALU.is_lt, ALU.mult)\
                    .then_inc(s_dve, seen.one())
            dve.wait_ge(s_dve, seen.steps)
            nc.vector.tensor_reduce(s2[:, 1], sc[:], AX.X, ALU.add).then_inc(s_dve, seen.one())
            dve.wait_ge(s_dve, seen.steps)
            nc.vector.reciprocal(s2[:, 2], s2[:, 1]).then_inc(s_dve, seen.one())
            dve.wait_ge(s_dve, seen.steps)
            nc.vector.tensor_tensor(sc[:], sc[:], s2[:, 2].unsqueeze(2).broadcast_to([P, 2, 64]), ALU.mult)\
                .then_inc(s_dve, seen.one())
            dve.wait_ge(s_dve, seen.steps)
            parts = kvn[:].rearrange("p t (b c) -> p t b c", b=2)
            for n in range(16):
                t, c = divmod(n, 8)
                dve.wait_ge(s_l0_xw, seen(s_l0_xw))
                nc.vector.tensor_tensor(lw[:, n % 4].rearrange("p (e d) -> p e d", e=8),
                                        ps[(0, 1, 2, 5)[n % 4]][0:P, :].rearrange("p (e d) -> p e d", e=8),
                                        sc[:, t, 8 * c:8 * c + 8].unsqueeze(2).broadcast_to([P, 8, C]),
                                        ALU.mult).then_inc(s_l0_prod, 1)
                if n % 4 == 3:
                    dve.wait_ge(s_l0_prod, seen(s_l0_prod, 4))
                    nc.vector.tensor_reduce(parts[:, t, n // 4 % 2], lw[:].rearrange("p b (e d) -> p d (b e)", e=8), AX.X,
                                            ALU.add).then_inc(s_dve, seen.one())
                    dve.wait_ge(s_dve, seen.steps)
            nc.vector.tensor_tensor(parts[:, :, 0], parts[:, :, 0], parts[:, :, 1], ALU.add).then_inc(s_dve, seen.one())
            dve.wait_ge(s_dve, seen.steps)
            nc.vector.tensor_tensor(t64[:, :, 0:C], parts[:, :, 0], y[:], ALU.add).then_inc(s_dve, seen.one())
            dve.wait_ge(s_dve, seen.steps)
            nc.vector.tensor_tensor(t64[:, :, 0:C], t64[:, :, 0:C], two(R("out_b")), ALU.add).then_inc(s_dve, seen.one())
            dve.wait_ge(s_dve, seen.steps)
            ln_vector(dve, seen, t64[:, :, 0:C], u64[:, :, 0:C], unit=True)
            nc.vector.tensor_tensor(u64[:, :, 0:C], u64[:, :, 0:C], two(R("ln_g")), ALU.mult).then_inc(s_dve, seen.one())
            dve.wait_ge(s_dve, seen.steps)
            nc.vector.tensor_tensor(u64[:, :, 0:C], u64[:, :, 0:C], two(R("ln_b")), ALU.add).then_inc(s_dve, seen.one())
            dve.wait_ge(s_dve, seen.steps)
            nc.vector.tensor_tensor(h[:], h[:], u64[:, :, 0:C], ALU.add).then_inc(s_dve, seen.one())
            dve.wait_ge(s_dve, seen.steps)

            ln_vector(dve, seen, h, y)
            dve.wait_ge(s_l1_qkv, seen(s_l1_qkv))
            G = 2 * H1
            nc.vector.tensor_tensor(t64[:], ps[3][0:P, 0:256].rearrange("p (t c) -> p t c", t=2),
                                    two(R("l1_bkv")), ALU.add).then_inc(s_dve, seen.one())
            dve.wait_ge(s_dve, seen.steps)
            quad = t64[:].rearrange("p t (g d) -> p t g d", d=D1)
            nc.vector.tensor_reduce(g64[:], quad, AX.X, ALU.add).then_inc(s_dve, seen.one())
            dve.wait_ge(s_dve, seen.steps)
            nc.vector.tensor_scalar(g64[:], g64[:], 1.0 / D1, None, ALU.mult).then_inc(s_dve, seen.one())
            dve.wait_ge(s_dve, seen.steps)
            nc.vector.tensor_tensor(quad, quad, g64[:].unsqueeze(3).broadcast_to([P, 2, G, D1]), ALU.subtract)\
                .then_inc(s_dve, seen.one())
            dve.wait_ge(s_dve, seen.steps)
            nc.vector.tensor_tensor(u64[:], t64[:], t64[:], ALU.mult).then_inc(s_dve, seen.one())
            dve.wait_ge(s_dve, seen.steps)
            nc.vector.tensor_reduce(g64[:], u64[:].rearrange("p t (g d) -> p t g d", d=D1), AX.X,
                                    ALU.add).then_inc(s_l1_var, 1)
            dve.wait_ge(s_l1_std, seen(s_l1_std))
            nc.vector.tensor_scalar(g64[:], g64[:], 1e-5, None, ALU.add).then_inc(s_dve, seen.one())
            dve.wait_ge(s_dve, seen.steps)
            nc.vector.reciprocal(g64[:], g64[:]).then_inc(s_dve, seen.one())
            dve.wait_ge(s_dve, seen.steps)
            nc.vector.tensor_tensor(quad, quad, g64[:].unsqueeze(3).broadcast_to([P, 2, G, D1]), ALU.mult)\
                .then_inc(s_dve, seen.one())
            dve.wait_ge(s_dve, seen.steps)
            nc.vector.tensor_tensor(t64[:], t64[:], two(R("l1_w")), ALU.mult).then_inc(s_dve, seen.one())
            dve.wait_ge(s_dve, seen.steps)
            nc.vector.tensor_tensor(kvn[:], t64[:], two(R("l1_b")), ALU.add).then_inc(s_l1_kvn, 1)
            dve.wait_ge(s_l1_kv, seen(s_l1_kv))
            nc.vector.tensor_tensor(m64[:, 0:64], ps[5][0:64, 0:64], K("mask1", 64), ALU.mult).then_inc(s_l1_m, 1)
            dve.wait_ge(s_l1_attT, seen(s_l1_attT))
            nc.vector.tensor_tensor(qT[:, 1], ps[5][0:64, 128:128 + T], yT[:], ALU.add).then_inc(s_l1_ret, 1)
            dve.wait_ge(s_l1_proj, seen(s_l1_proj))
            nc.vector.tensor_tensor(t64[:, :, 0:C], ps[3][0:P, 0:128].rearrange("p (t c) -> p t c", t=2),
                                    two(R("l1_bproj")), ALU.add).then_inc(s_l1_pre, 1)
            dve.wait_ge(s_l1_gelu, seen(s_l1_gelu))
            nc.vector.tensor_tensor(u64[:, :, 0:C], u64[:, :, 0:C], y[:], ALU.add).then_inc(s_dve, seen.one())
            dve.wait_ge(s_dve, seen.steps)
            nc.vector.tensor_tensor(h[:], h[:], u64[:, :, 0:C], ALU.add).then_inc(s_dve, seen.one())
            dve.wait_ge(s_dve, seen.steps)

            ln_vector(dve, seen, h, y, unit=True)
            dve.wait_ge(s_e_gate, seen(s_e_gate))
            gl = t64[:, :, 0:E1]
            nc.vector.tensor_tensor(gl, ps[3][0:P, 0:2 * E1].rearrange("p (t e) -> p t e", t=2),
                                    two(R("l1_bg")), ALU.add).then_inc(s_dve, seen.one())
            dve.wait_ge(s_dve, seen.steps)
            nc.vector.tensor_reduce(s2[:, 0], gl, AX.X, ALU.max).then_inc(s_dve, seen.one())
            dve.wait_ge(s_dve, seen.steps)
            nc.vector.tensor_tensor(gl, gl, s2[:, 0].unsqueeze(2).broadcast_to([P, 2, E1]),
                                    ALU.subtract).then_inc(s_e_shift, 1)
            dve.wait_ge(s_e_exp, seen(s_e_exp))
            nc.vector.tensor_reduce(s2[:, 1], gl, AX.X, ALU.add).then_inc(s_dve, seen.one())
            dve.wait_ge(s_dve, seen.steps)
            nc.vector.reciprocal(s2[:, 2], s2[:, 1]).then_inc(s_dve, seen.one())
            dve.wait_ge(s_dve, seen.steps)
            nc.vector.tensor_tensor(gl, gl, s2[:, 2].unsqueeze(2).broadcast_to([P, 2, E1]), ALU.mult)\
                .then_inc(s_dve, seen.one())
            dve.wait_ge(s_dve, seen.steps)
            for t in range(2):
                nc.vector.max(m8[:, t], gl[:, t]).then_inc(s_dve, seen.one())
            dve.wait_ge(s_dve, seen.steps)
            nc.vector.memset(m8[:, :, 1:8], NEG).then_inc(s_dve, seen.one())
            dve.wait_ge(s_dve, seen.steps)
            for t in range(2):
                nc.vector.match_replace(rep[:, t, 0:E1], m8[:, t], gl[:, t], NEG).then_inc(s_dve, seen.one())
            dve.wait_ge(s_dve, seen.steps)
            for t in range(2):
                nc.vector.scalar_tensor_tensor(sc[:, t, 0:E1], rep[:, t, 0:E1], -1.0e38, gl[:, t], ALU.is_lt, ALU.mult)\
                    .then_inc(s_dve, seen.one())
            dve.wait_ge(s_dve, seen.steps)
            for t in range(2):
                dve.wait_ge(s_e_y, seen(s_e_y))
                nc.vector.tensor_tensor(lw[:, t].rearrange("p (e d) -> p e d", e=E1),
                                        ps[1 + t][0:P, :].rearrange("p (e d) -> p e d", e=E1),
                                        sc[:, t, 0:E1].unsqueeze(2).broadcast_to([P, E1, C]), ALU.mult)\
                    .then_inc(s_dve, seen.one())
                dve.wait_ge(s_dve, seen.steps)
            nc.vector.tensor_reduce(u64[:, :, 0:C], lw[:, 0:2].rearrange("p t (e c) -> p t c e", e=E1), AX.X, ALU.add)\
                .then_inc(s_dve, seen.one())
            dve.wait_ge(s_dve, seen.steps)
            nc.vector.tensor_tensor(h[:], h[:], u64[:, :, 0:C], ALU.add).then_inc(s_dve, seen.one())
            dve.wait_ge(s_dve, seen.steps)

            ln_vector(dve, seen, h, y, unit=True)
            dve.wait_ge(s_l2_qkv, seen(s_l2_qkv))
            qk = ps[0][0:C, 0:2 * T].rearrange("p (n j) -> p n j", n=2)
            swapped = ps[1][0:ROPE, 0:2 * T].rearrange("p (n j) -> p n j", n=2)
            cos = K("cos", C).unsqueeze(1).broadcast_to([C, 2, T])
            sin = K("sin", ROPE).unsqueeze(1).broadcast_to([ROPE, 2, T])
            nc.vector.tensor_tensor(qT[:], qk, cos, ALU.mult).then_inc(s_dve, seen.one())
            nc.vector.tensor_tensor(rope2[:], swapped, sin, ALU.mult).then_inc(s_dve, seen.one())
            dve.wait_ge(s_dve, seen.steps)
            nc.vector.tensor_tensor(qT[0:ROPE], qT[0:ROPE], rope2[:], ALU.add).then_inc(s_l2_rope, 1)
            att_vector(dve, seen, h, True)

            ln_vector(dve, seen, h, y, unit=True)
            for t in range(2):
                weigh_rows(dve, seen)
                weigh_rows(dve, seen)
                dve.wait_ge(s_pk_copied, seen(s_pk_copied))
                pick_vector(dve, seen, t)
                if early and t == 0:
                    dve.wait_ge(s_dve, seen.steps)
                    nc.vector.tensor_copy(idxG[:, 0], idxF[:, 0]).then_inc(s_early, 1)
            heads_vector(dve, seen)
            dve.wait_ge(s_pk_exp, seen(s_pk_exp))
            nc.vector.tensor_reduce(s16(0), wgtF[:].rearrange("p t h k -> p (t h) k"), AX.X, ALU.add)\
                .then_inc(s_dve, seen.one())
            dve.wait_ge(s_dve, seen.steps)
            nc.vector.reciprocal(s16(1), s16(0)).then_inc(s_dve, seen.one())
            dve.wait_ge(s_dve, seen.steps)
            nc.vector.tensor_tensor(wgtF[:].rearrange("p t h k -> p (t h) k"),
                                    wgtF[:].rearrange("p t h k -> p (t h) k"),
                                    s16(1).unsqueeze(2).broadcast_to([P, 16, PK]), ALU.mult)\
                .then_inc(s_dve, seen.one())
            dve.wait_ge(s_dve, seen.steps)

        def s16(n):
            return g64[:].rearrange("p t g -> p (t g)")[:, 16 * n:16 * n + 16]

        def top16(dve, seen, n, values, work, best, best_i, size):
            for g in range(n):
                nc.vector.max(best[:, g, 0:8], values(g)).then_inc(s_dve, seen.one())
            head_vector(dve, seen)
            dve.wait_ge(s_dve, seen.steps)
            for g in range(n):
                nc.vector.max_index(best_i[:, g, 0:8], best[:, g, 0:8], values(g)).then_inc(s_dve, seen.one())
            head_vector(dve, seen)
            for g in range(n):
                nc.vector.match_replace(work(g), best[:, g, 0:8], values(g), NEG).then_inc(s_dve, seen.one())
            head_vector(dve, seen)
            dve.wait_ge(s_dve, seen.steps)
            for g in range(n):
                nc.vector.max(best[:, g, 8:16], work(g)).then_inc(s_dve, seen.one())
            head_vector(dve, seen)
            dve.wait_ge(s_dve, seen.steps)
            for g in range(n):
                nc.vector.max_index(best_i[:, g, 8:16], best[:, g, 8:16], work(g)).then_inc(s_dve, seen.one())
            head_vector(dve, seen)
            dve.wait_ge(s_dve, seen.steps)

        def pick_vector(dve, seen, t):
            top16(dve, seen, 16, lambda g: pks[:, t, NK * g:NK * (g + 1)], lambda g: pkr[:, NK * g:NK * (g + 1)], v16, i16, NK)
            nc.vector.tensor_scalar(i16[:, H2:16], i16[:, H2:16], 6, None, ALU.logical_shift_left).then_inc(s_dve, seen.one())
            dve.wait_ge(s_dve, seen.steps)
            for src, dst, op in ((v16, cs, ALU.add), (i16, ci, ALU.bitwise_or)):
                for i0, i1, nj, at in CAND:
                    ni = i1 - i0
                    nc.vector.tensor_tensor(
                        dst[:, :, at:at + ni * nj].rearrange("p h (i j) -> p h i j", j=nj),
                        src[:, 0:H2, i0:i1].unsqueeze(3).broadcast_to([P, H2, ni, nj]),
                        src[:, H2:16, 0:nj].unsqueeze(2).broadcast_to([P, H2, ni, nj]), op).then_inc(s_dve, seen.one())
            dve.wait_ge(s_dve, seen.steps)
            for rank in (0, 8):
                src = cr if rank else cs
                for h in range(H2):
                    nc.vector.max(bv[:, h, rank:rank + 8], src[:, h]).then_inc(s_dve, seen.one())
                dve.wait_ge(s_dve, seen.steps)
                for h in range(H2):
                    nc.vector.match_replace(cr[:, h], bv[:, h, rank:rank + 8], src[:, h], NEG).then_inc(s_dve, seen.one())
                head_vector(dve, seen)
                dve.wait_ge(s_dve, seen.steps)
            bits = cs[:].bitcast(u32)
            high, low = (K(name).bitcast(u32).rearrange("p (h n) -> p h n", h=H2) for name in ("high_key", "low_key"))
            nc.vector.scalar_tensor_tensor(kbits[:, 0], bits, 7, high, ALU.logical_shift_right, ALU.bitwise_or)\
                .then_inc(s_dve, seen.one())
            nc.vector.tensor_scalar(kbits[:, 1], bits, 127, 15, ALU.bitwise_and, ALU.logical_shift_left)\
                .then_inc(s_dve, seen.one())
            nc.vector.tensor_tensor(ci[:], ci[:], low, ALU.bitwise_or).then_inc(s_dve, seen.one())
            dve.wait_ge(s_dve, seen.steps)
            nc.vector.tensor_tensor(kbits[:, 1], kbits[:, 1], ci[:], ALU.bitwise_or).then_inc(s_dve, seen.one())
            dve.wait_ge(s_dve, seen.steps)
            for m in range(2):
                nc.vector.scalar_tensor_tensor(key[:, m], cr[:], -1.0e38, key[:, m], ALU.is_lt, ALU.mult)\
                    .then_inc(s_dve, seen.one())
            dve.wait_ge(s_dve, seen.steps)
            for m in range(2):
                for h in range(H2):
                    nc.vector.max(best[:, m, h, 0:8], key[:, m, h]).then_inc(s_dve, seen.one())
            head_vector(dve, seen)
            dve.wait_ge(s_dve, seen.steps)
            for m in range(2):
                for h in range(H2):
                    nc.vector.match_replace(key[:, m, h], best[:, m, h, 0:8], key[:, m, h], 0.0).then_inc(s_dve, seen.one())
            dve.wait_ge(s_dve, seen.steps)
            for m in range(2):
                for h in range(H2):
                    nc.vector.max(best[:, m, h, 8:16], key[:, m, h]).then_inc(s_dve, seen.one())
            dve.wait_ge(s_dve, seen.steps)
            upper, lower = best[:, 0].bitcast(u32), best[:, 1].bitcast(u32)
            nc.vector.tensor_scalar(idxF[:, t], lower, ROWS_BITS - 1, None, ALU.bitwise_and).then_inc(s_dve, seen.one())
            nc.vector.tensor_scalar(sbits[:], lower, 15, 127, ALU.logical_shift_right, ALU.bitwise_and)\
                .then_inc(s_dve, seen.one())
            dve.wait_ge(s_dve, seen.steps)
            nc.vector.scalar_tensor_tensor(sbits[:], upper, 7, sbits[:], ALU.logical_shift_left, ALU.bitwise_or)\
                .then_inc(s_dve, seen.one())
            dve.wait_ge(s_dve, seen.steps)
            nc.vector.tensor_tensor(wgtF[:, t], sbits[:].bitcast(fp32), bv[:, :, 0:1].broadcast_to([P, H2, PK]),
                                    ALU.subtract).then_inc(s_pk_shift, 1)

        def front_scalar(act, seen, early):
            for _ in seen.work.held[0:1]:
                keep_sum(act, seen)
            for n in range(3):
                act.wait_ge(s_tok_z, seen(s_tok_z))
                parts, pairs = (128, 2) if n < 2 else (64, 1)
                nc.scalar.activation(th[0:parts, 2 * n:2 * n + pairs].rearrange("p a t -> p (a t)"),
                                     ps[n][0:parts, 0:pairs * T], ACT.Tanh,
                                     bias=V("tok_b")[0:parts]).then_inc(s_tok_tanh, 1)
            act.wait_ge(s_tok_shift, seen(s_tok_shift))
            nc.scalar.activation(e9[:], e9[:], ACT.Exp).then_inc(s_tok_exp, 1)
            if early:
                fold_scalar(act)
            for _ in seen.work.held[1:]:
                keep_sum(act, seen)
            ln_scalar(act, seen, yT)
            act.wait_ge(s_att_gT, seen(s_att_gT))
            nc.scalar.activation(qT[:, 0], ps[5][0:64, 0:T], ACT.Copy).then_inc(s_att_qk, 1)
            att_scalar(act, seen, False)
            ln_scalar(act, seen, yT, unit=True)
            act.wait_ge(s_l0_shift, seen(s_l0_shift))
            nc.scalar.activation(sc[:], sc[:], ACT.Exp).then_inc(s_l0_e, 1)
            ln_scalar(act, seen, unit=True)
            ln_scalar(act, seen, yT, unit=True)
            act.wait_ge(s_l1_q, seen(s_l1_q))
            nc.scalar.activation(qT[:, 0], ps[0][0:64, 0:T], ACT.Identity, bias=V("l1_bq")[0:64]).then_inc(s_l1_q, 1)
            act.wait_ge(s_l1_var, seen(s_l1_var))
            nc.scalar.activation(g64[:], g64[:], ACT.Sqrt, scale=1.0 / (D1 - 1)).then_inc(s_l1_std, 1)
            act.wait_ge(s_l1_pre, seen(s_l1_pre))
            nc.scalar.activation(u64[:, :, 0:C], t64[:, :, 0:C], ACT.Gelu).then_inc(s_l1_gelu, 1)
            ln_scalar(act, seen, yT)
            act.wait_ge(s_e_hT, seen(s_e_hT))
            for c in range(2):
                last = nc.scalar.activation(actT[:, c], ps[0][:, c * T:(c + 1) * T], ACT.Gelu, bias=V("l1_b1")[:, c:c + 1])
            last.then_inc(s_e_act, 1)
            act.wait_ge(s_e_shift, seen(s_e_shift))
            nc.scalar.activation(t64[:, :, 0:E1], t64[:, :, 0:E1], ACT.Exp).then_inc(s_e_exp, 1)
            ln_scalar(act, seen, yT, unit=True)
            act.wait_ge(s_l2_v, seen(s_l2_v))
            nc.scalar.activation(v_sb[:, :, 0:C], ps[5][0:P, 0:128].rearrange("p (t c) -> p t c", t=2),
                                 ACT.Copy).then_inc(s_l2_v, 1)
            att_scalar(act, seen, True)
            ln_scalar(act, seen, yTF, unit=True)
            act.wait_ge(s_pk_sim, seen(s_pk_sim))
            for t in range(2):
                for k in range(2):
                    last = nc.scalar.activation(pks[:, t, 512 * k:512 * k + 512], ps[(0, 1, 2, 5)[2 * t + k]][0:P, :], ACT.Copy)
                last.then_inc(s_pk_copied, 1)
                if t == 0:
                    act.wait_ge(s_pk_sim, seen(s_pk_sim))
            if seen.heads:
                heads_scalar(act, seen)
            elif seen.work.sums:
                for _ in range(5):
                    keep_sum(act, seen)
            act.wait_ge(s_pk_shift, seen(s_pk_shift, 2))
            nc.scalar.activation(wgtF[:], wgtF[:], ACT.Exp).then_inc(s_pk_exp, 1)

        def front_tensor(pe, seen, early):
            for _ in seen.work.held[0:1]:
                sum_rows(pe, seen)
            pe.wait_ge(s_x_loaded, seen(s_x_loaded, 48))
            for n in range(5):
                z = ps[n // 2][:, (n % 2) * T:(n % 2 + 1) * T]
                m = 128 if n < 4 else 64
                last = nc.tensor.matmul(z[0:m], W("tok_qry2", 0, m), xT_sb[:, WIN // 2:WIN // 2 + T], start=True, stop=False,
                                        skip_group_check=True)
                for half in range(m // 64):
                    s = 2 * n + half
                    last = nc.tensor.matmul(z[64 * half:64 * half + 64], W("tok_key"), xT_sb[:, s:s + T], start=False,
                                            stop=True, skip_group_check=True)
                if n % 2 or n == 4:
                    last.then_inc(s_tok_z, 1)
            pe.wait_ge(s_tok_tanh, seen(s_tok_tanh, 3))
            for t in range(2):
                for n in range(5):
                    k, cols = (128, 2) if n < 4 else (64, 1)
                    at = t * WIN + 2 * n
                    last = nc.tensor.matmul(ps[3][0:P, at:at + cols], th[0:k, n, tile(t)], V("tok_v")[0:k, 0:cols],
                                            start=True, stop=True)
            last.then_inc(s_tok_score, 1)
            if early:
                fold_tensor(pe)
            for _ in seen.work.held[1:]:
                sum_rows(pe, seen)
            ln_tensor(pe, seen, y)
            nc.tensor.matmul(ps[5][0:64, 0:T], l0_a[:], yT[:], start=True, stop=True).then_inc(s_att_gT, 1)
            pe.wait_ge(s_att_qk, seen(s_att_qk))
            att_tensor(pe, seen, qT[:, 0], yT[:], lambda j: y[:, j], False)
            ln_tensor(pe, seen, y, unit=True)
            for t in range(2):
                last = nc.tensor.matmul(ps[3][0:P, 64 * t:64 * t + 64], yT[:, tile(t)], W("gate"), start=True, stop=True)
            last.then_inc(s_l0_logit, 1)
            for n in range(16):
                t, c = divmod(n, 8)
                if n >= 4:
                    pe.wait_ge(s_l0_prod, seen(s_l0_prod))
                nc.tensor.matmul(ps[(0, 1, 2, 5)[n % 4]][0:P, :], yT[:, tile(t)], latt[:, 512 * c:512 * c + 512], start=True,
                                 stop=True).then_inc(s_l0_xw, 1)
            sum_rows(pe, seen)
            pe.wait_ge(s_ln_y, seen(s_ln_y))
            ln_tensor(pe, seen, y, unit=True)
            for t in range(2):
                last = nc.tensor.matmul(ps[3][0:P, 128 * t:128 * t + 128], yT[:, tile(t)], W("l1_kv"), start=True, stop=True)
            last.then_inc(s_l1_qkv, 1)
            nc.tensor.matmul(ps[0][0:64, 0:T], W("l1_q"), yT[:], start=True, stop=True).then_inc(s_l1_q, 1)
            pe.wait_ge(s_l1_kvn, seen(s_l1_kvn))
            for t in range(2):
                last = nc.tensor.matmul(ps[5][0:64, 0:64], kvn[:, t, 0:64], kvn[:, t, 64:128], start=t == 0, stop=t == 1)
            last.then_inc(s_l1_kv, 1)
            pe.wait_ge(s_l1_q, seen(s_l1_q, 2))
            pe.wait_ge(s_l1_m, seen(s_l1_m))
            nc.tensor.matmul(ps[5][0:64, 128:128 + T], m64[:, 0:64], qT[:, 0], start=True, stop=True).then_inc(s_l1_attT, 1)
            pe.wait_ge(s_l1_ret, seen(s_l1_ret))
            for t in range(2):
                last = nc.tensor.matmul(ps[3][0:P, C * t:C * t + C], qT[:, 1, tile(t)], W("l1_proj"), start=True, stop=True)
            last.then_inc(s_l1_proj, 1)
            ln_tensor(pe, seen, y)
            for c in range(2):
                last = nc.tensor.matmul(ps[0][:, c * T:(c + 1) * T], W("l1_w1", 128 * c, 128), yT[:], start=True, stop=True)
            last.then_inc(s_e_hT, 1)
            pe.wait_ge(s_e_act, seen(s_e_act))
            for t in range(2):
                for c in range(2):
                    last = nc.tensor.matmul(ps[3][0:P, E1 * t:E1 * t + E1], actT[:, c, tile(t)],
                                            V("l1_wg")[:, E1 * c:E1 * c + E1], start=c == 0, stop=c == 1)
            last.then_inc(s_e_gate, 1)
            for t in range(2):
                for c in range(2):
                    nc.tensor.matmul(ps[1 + t][0:P, :], actT[:, c, tile(t)], V("l1_wd")[:, 512 * c:512 * c + 512],
                                     start=c == 0, stop=False)
                nc.tensor.matmul(ps[1 + t][0:P, :], K("ones")[0:1], R("bd")[0:1], start=False, stop=True)\
                    .then_inc(s_e_y, 1)
            ln_tensor(pe, seen, y, unit=True)
            for n, w in enumerate((l2_qw, l2_kvw)):
                nc.tensor.matmul(ps[0][0:64, n * T:(n + 1) * T], w[:, 0:64], yT[:], start=True, stop=True)
                last = nc.tensor.matmul(ps[1][0:ROPE, n * T:(n + 1) * T], w[:, 64:80], yT[:], start=True, stop=True)
            last.then_inc(s_l2_qkv, 1)
            for t in range(2):
                last = nc.tensor.matmul(ps[5][0:P, C * t:C * t + C], yT[:, tile(t)], l2_kvw[:, 80:144], start=True, stop=True)
            last.then_inc(s_l2_v, 1)
            pe.wait_ge(s_l2_v, seen(s_l2_v, 2))
            pe.wait_ge(s_l2_rope, seen(s_l2_rope))
            att_tensor(pe, seen, qT[:, 0], qT[:, 1], lambda j: v_sb[:, j, 0:C], True)
            ln_tensor(pe, seen, y, unit=True)
            for k in range(4):
                last = nc.tensor.matmul(ps[(0, 1, 2, 5)[k]][0:P, :], yTF[:, tile(k // 2)],
                                        pk_w[:, 512 * (k % 2):512 * (k % 2) + 512], start=True, stop=True)
                if k % 2:
                    last.then_inc(s_pk_sim, 1)
            pe.wait_ge(s_pk_copied, seen(s_pk_copied, 2))

        def gather_pool(pool, work):
            for u in work.fetched:
                t, h = work.place(u, False)
                if work.freed(u):
                    pool.wait_ge(s_summed, work.freed(u))
                for k in range(PK):
                    pool.indirect_dma_start(rowbuf[:, u % SLOTS, k], None, table,
                                                bass.IndirectOffsetOnAxis(ap=idxG[:, t, h, k:k + 1], axis=0))\
                        .then_inc(fetched[u % SLOTS], 16)

        def fetches(batches, u):
            return (batches * len(range(u % SLOTS, UNITS, SLOTS)) + u // SLOTS + 1) * (16 * PK)

        def weigh_rows(dve, seen):
            u, held = seen.unit()
            if u is not None:
                t, h = seen.work.place(u, held)
                row = rowbuf[:, u % SLOTS]
                weights = wgtH[:, u - (UNITS - HELD)] if held else wgtG[:, t, h]
                dve.wait_ge(fetched[u % SLOTS], fetches(seen.work.batch - 1 if held else seen.work.batch, u))
                nc.vector.tensor_tensor(row, row, weights.unsqueeze(2).broadcast_to([P, PK, 2 * C]),
                                        ALU.mult).then_inc(s_weighed, 1)

        def sum_rows(pe, seen):
            u, held = seen.unit()
            if u is not None:
                if seen.units > 1:
                    pe.wait_ge(s_kept, seen(s_kept))
                pe.wait_ge(s_weighed, seen(s_weighed))
                for k in range(PK):
                    last = nc.tensor.matmul(ps[7][0:P, 0:2 * C], K("ident")[:, 0:P], rowbuf[:, u % SLOTS, k],
                                            start=k == 0, stop=k == PK - 1)
                last.then_inc(s_summed, 1)

        def keep_sum(act, seen):
            u, held = seen.unit()
            if u is not None:
                t, h = seen.work.place(u, held)
                act.wait_ge(s_summed, seen(s_summed))
                nc.scalar.activation((kvB if held or seen.work.final else kvG)[:, t, h], ps[7][0:P, 0:2 * C], ACT.Copy).then_inc(s_kept, 1)

        def head_vector(dve, seen):
            if not seen.heads or seen.head_steps == 2 * H2:
                return
            n, step = divmod(seen.head_steps, 2)
            seen.head_steps += 1
            if step == 0:
                dve.wait_ge(s_m_sim, seen(s_m_sim))
                maxima(ps[2 + n % 2], s_m_max, True)
            else:
                dve.wait_ge(s_m_exp, seen(s_m_exp))
                nc.vector.reciprocal(rinv[:, n % 2], rsum[:, n % 2]).then_inc(s_m_rinv, 1)

        def heads_vector(dve, seen, units=False):
            while seen.heads and seen.head_steps < 2 * H2:
                while seen.work.final and seen.units < len(seen.work.sums) and seen.work.sums[seen.units][0] <= seen.head_steps + 1:
                    weigh_rows(dve, seen)
                head_vector(dve, seen)
                if units and not seen.work.final and seen.head_steps % 4 == 0:
                    weigh_rows(dve, seen)

        def back_vector(dve, seen):
            h = hB
            dve.wait_ge(s_m_out, seen(s_m_out))
            nc.vector.tensor_tensor(h[:], h[:], ps[5][0:P, 0:128].rearrange("p (t c) -> p t c", t=2), ALU.add)\
                .then_inc(s_dve, seen.one())
            dve.wait_ge(s_dve, seen.steps)

            ln_vector(dve, seen, h, y, unit=True)
            dve.wait_ge(s_l3_q, seen(s_l3_q))
            nc.vector.tensor_scalar(qT[:, 0], ps[0][0:64, 0:T], 0.0, None, ALU.min).then_inc(s_dve, seen.one())
            nc.vector.tensor_scalar(kT[:, 0], ps[0][0:64, 0:T], 0.0, None, ALU.max).then_inc(s_dve, seen.one())
            dve.wait_ge(s_l3_kv, seen(s_l3_kv))
            kx = ps[1][0:P, 0:256].rearrange("p (t c) -> p t c", t=2)
            nc.vector.tensor_scalar(v_sb[:, :, 0:C], kx[:, :, C:2 * C], 1.0 / T, None, ALU.mult)\
                .then_inc(s_dve, seen.one())
            nc.vector.memset(v_sb[:, :, C:C + H3], 1.0).then_inc(s_dve, seen.one())
            nc.vector.tensor_scalar(u64[:, :, 0:C], kx[:, :, 0:C], 0.0, None, ALU.max).then_inc(s_dve, seen.one())
            nc.vector.tensor_scalar(t64[:, :, 0:C], kx[:, :, 0:C], 0.0, None, ALU.min).then_inc(s_l3_pre, 1)
            dve.wait_ge(s_dve, seen.steps)
            dve.wait_ge(s_l3_exp, seen(s_l3_exp))
            nc.vector.tensor_tensor(t64[:, :, 0:C], t64[:, :, 0:C], u64[:, :, 0:C], ALU.add)
            nc.vector.tensor_tensor(qT[:, 0], qT[:, 0], kT[:, 0], ALU.add).then_inc(s_l3_elu, 1)
            dve.wait_ge(s_l3_kvs, seen(s_l3_kvs))
            nc.vector.tensor_tensor(m64[:], ps[5][0:64, 0:72], K("mask3", 64), ALU.mult).then_inc(s_l3_m, 1)
            dve.wait_ge(s_l3_num, seen(s_l3_num))
            num = ps[3][0:P, 0:144].rearrange("p (t c) -> p t c", t=2)
            nc.vector.tensor_scalar(g64[:, :, 0:H3], num[:, :, C:C + H3], 1e-6, None, ALU.add).then_inc(s_dve, seen.one())
            dve.wait_ge(s_dve, seen.steps)
            nc.vector.reciprocal(g64[:, :, 0:H3], g64[:, :, 0:H3]).then_inc(s_dve, seen.one())
            dve.wait_ge(s_dve, seen.steps)
            nc.vector.tensor_scalar(g64[:, :, 0:H3], g64[:, :, 0:H3], float(T), None, ALU.mult)\
                .then_inc(s_dve, seen.one())
            dve.wait_ge(s_dve, seen.steps)
            for t in range(2):
                last = nc.vector.tensor_tensor(
                    t64[:, t, 0:C].rearrange("p (h d) -> p h d", h=H3), num[:, t, 0:C].rearrange("p (h d) -> p h d", h=H3),
                    g64[:, t, 0:H3].unsqueeze(2).broadcast_to([P, H3, D3]), ALU.mult)
            last.then_inc(s_l3_msg, 1)
            dve.wait_ge(s_l3_mm, seen(s_l3_mm))
            nc.vector.tensor_copy(t64[:, :, 0:C], ps[3][0:P, 0:128].rearrange("p (t c) -> p t c", t=2))\
                .then_inc(s_dve, seen.one())
            dve.wait_ge(s_dve, seen.steps)
            ln_vector(dve, seen, t64[:, :, 0:C], u64[:, :, 0:C], unit=True)
            nc.vector.tensor_tensor(u64[:, :, 0:C], u64[:, :, 0:C], two(R("g1")), ALU.mult).then_inc(s_dve, seen.one())
            dve.wait_ge(s_dve, seen.steps)
            nc.vector.tensor_tensor(u64[:, :, 0:C], u64[:, :, 0:C], two(R("b1")), ALU.add).then_inc(s_l3_msg2, 1)
            dve.wait_ge(s_l3_h, seen(s_l3_h))
            nc.vector.tensor_copy(t64[:, :, 0:C], ps[3][0:P, 0:128].rearrange("p (t c) -> p t c", t=2))\
                .then_inc(s_dve, seen.one())
            dve.wait_ge(s_dve, seen.steps)
            ln_vector(dve, seen, t64[:, :, 0:C], u64[:, :, 0:C], unit=True)
            nc.vector.tensor_tensor(u64[:, :, 0:C], u64[:, :, 0:C], two(R("g2")), ALU.mult).then_inc(s_dve, seen.one())
            dve.wait_ge(s_dve, seen.steps)
            nc.vector.tensor_tensor(u64[:, :, 0:C], u64[:, :, 0:C], two(R("b2")), ALU.add).then_inc(s_dve, seen.one())
            dve.wait_ge(s_dve, seen.steps)
            nc.vector.tensor_tensor(u64[:, :, 0:C], u64[:, :, 0:C], y[:], ALU.add).then_inc(s_dve, seen.one())
            dve.wait_ge(s_dve, seen.steps)
            nc.vector.tensor_tensor(h[:], h[:], u64[:, :, 0:C], ALU.add).then_inc(s_dve, seen.one())
            dve.wait_ge(s_dve, seen.steps)

            ln_vector(dve, seen, h, y, unit=True)
            dve.wait_ge(s_c_w, seen(s_c_w))
            nc.vector.tensor_scalar(sm[:, 0], ps[5][0:P, 0:T], R("cap_br"), None, ALU.add).then_inc(s_dve, seen.one())
            dve.wait_ge(s_dve, seen.steps)
            for t in range(2):
                own = K("own")[:, t * T:(t + 1) * T]
                tri = K("tri")[:, t * T:(t + 1) * T]
                nc.vector.tensor_tensor(sm[:, 1], sm[:, 0], own, ALU.mult).then_inc(s_dve, seen.one())
                dve.wait_ge(s_dve, seen.steps)
                nc.vector.tensor_reduce(cnt[:, t:t + 1], sm[:, 1], AX.X, ALU.add).then_inc(s_dve, seen.one())
                dve.wait_ge(s_dve, seen.steps)
                nc.vector.scalar_tensor_tensor(sm[:, 1], sm[:, 0], cnt[:, t:t + 1], tri, ALU.is_equal, ALU.mult)\
                    .then_inc(s_dve, seen.one())
                dve.wait_ge(s_dve, seen.steps)
                nc.vector.scalar_tensor_tensor(sm[:, 1], sm[:, 0], cnt[:, t:t + 1], sm[:, 1], ALU.is_gt, ALU.add)\
                    .then_inc(s_dve, seen.one())
                dve.wait_ge(s_dve, seen.steps)
                nc.vector.tensor_reduce(cnt[:, 2 + t:3 + t], sm[:, 1], AX.X, ALU.add).then_inc(s_dve, seen.one())
                dve.wait_ge(s_dve, seen.steps)
            nc.vector.scalar_tensor_tensor(cnt[:, 4:6], cnt[:, 2:4], float(CAP), cnt[:, 0:2], ALU.is_lt, ALU.mult)\
                .then_inc(s_dve, seen.one())
            dve.wait_ge(s_dve, seen.steps)
            dve.wait_ge(s_c_y, seen(s_c_y))
            nc.vector.tensor_tensor(t64[:, :, 0:C], ps[3][0:P, 0:128].rearrange("p (t c) -> p t c", t=2),
                                    two(R("cap_b2")), ALU.add).then_inc(s_dve, seen.one())
            dve.wait_ge(s_dve, seen.steps)
            nc.vector.tensor_tensor(h[:], h[:], y[:], ALU.add).then_inc(s_dve, seen.one())
            dve.wait_ge(s_dve, seen.steps)
            for t in range(2):
                last = nc.vector.scalar_tensor_tensor(h[:, t], t64[:, t, 0:C], cnt[:, 4 + t:5 + t], h[:, t], ALU.mult, ALU.add)
            last.then_inc(s_c_out, 1)
            dve.wait_ge(s_c_out, seen(s_c_out))

        def heads_scalar(act, seen):
            for n in range(H2 + 1):
                if n < H2:
                    i = n % 2
                    while seen.work.final and seen.units < len(seen.work.sums) and seen.work.sums[seen.units][0] <= 2 * n + 1:
                        keep_sum(act, seen)
                    act.wait_ge(s_m_prep, seen(s_m_prep))
                    nc.scalar.activation(kT[:, i], ps[i][0:64, 0:T], ACT.Copy)
                    nc.scalar.activation(qT[:, i], ps[i][0:64, T:2 * T], ACT.Copy, scale=C ** -0.5).then_inc(s_m_copied, 1)
                if n:
                    j = (n - 1) % 2
                    act.wait_ge(s_m_pT, seen(s_m_pT))
                    nc.scalar.activation(prT[:, j, 0:3 * P], ps[4][0:P, 0:3 * P], ACT.Copy).then_inc(s_m_pTc, 1)
                    act.wait_ge(s_m_oT, seen(s_m_oT))
                    nc.scalar.activation(outT[:, j], ps[6][0:64, 0:T], ACT.Copy).then_inc(s_m_oTc, 1)
                if n < H2:
                    act.wait_ge(s_m_max, seen(s_m_max))
                    exps(ps[2 + i], i, True).then_inc(s_m_exp, 1)
                    act.wait_ge(s_m_rinv, seen(s_m_rinv))
                    for t in range(2):
                        row = pr[:, i, t * T:t * T + (t + 1) * P]
                        last = nc.scalar.activation(row, row, ACT.Copy, scale=rinv[:, i, t:t + 1])
                    last.then_inc(s_m_norm, 1)
                if n in (2, 3, 6, 7) and not seen.work.final:
                    keep_sum(act, seen)

        def back_scalar(act, seen):
            ln_scalar(act, seen, yT, unit=True)
            act.wait_ge(s_l3_pre, seen(s_l3_pre))
            nc.scalar.activation(t64[:, :, 0:C], t64[:, :, 0:C], ACT.Exp)
            nc.scalar.activation(qT[:, 0], qT[:, 0], ACT.Exp).then_inc(s_l3_exp, 1)
            act.wait_ge(s_l3_msgT, seen(s_l3_msgT))
            nc.scalar.activation(kT[:, 0], ps[4][0:64, 0:T], ACT.Copy).then_inc(s_l3_msgTc, 1)
            ln_scalar(act, seen, unit=True)
            act.wait_ge(s_l3_msgT, seen(s_l3_msgT))
            nc.scalar.activation(kT[:, 0], ps[4][0:64, 0:T], ACT.Copy).then_inc(s_l3_msgTc, 1)
            act.wait_ge(s_l3_hT, seen(s_l3_hT))
            nc.scalar.activation(actT[:, 0], ps[0][:, 0:T], ACT.Relu).then_inc(s_l3_relu, 1)
            ln_scalar(act, seen, unit=True)
            ln_scalar(act, seen, yT, unit=True)
            act.wait_ge(s_c_hT, seen(s_c_hT))
            for c in range(2):
                last = nc.scalar.activation(actT[:, c], ps[0][:, c * T:(c + 1) * T], ACT.Gelu_apprx_tanh,
                                            bias=V("cap_b1")[:, c:c + 1])
            last.then_inc(s_c_act, 1)

        def head_out(n):
            for t in range(2):
                last = nc.tensor.matmul(ps[5][0:P, C * t:C * t + C], outT[:, n % 2, tile(t)], W("l2f_o", C * n, C),
                                        start=n == 0 and t == 0, stop=n == H2 - 1, skip_group_check=True)
            return last

        def heads_tensor(pe, seen):
            if seen.work.held:
                pe.wait_ge(s_kept, HELD)
            for n in range(H2 + 1):
                if n < H2:
                    i = n % 2
                    while seen.work.final and seen.units < len(seen.work.sums) and seen.work.sums[seen.units][0] <= 2 * n + 1:
                        sum_rows(pe, seen)
                    if seen.work.final and seen.units:
                        pe.wait_ge(s_kept, seen.units)
                    for t in range(2):
                        nc.tensor.transpose(ps[i][0:64, tile(t)], kvB[:, t, n, 0:C], K("ident")[:, 0:P])
                    nc.tensor.matmul(ps[i][0:64, T:2 * T], W("l2f_q", C * n, C), yTB[:], start=True,
                                     stop=True).then_inc(s_m_prep, 1)
                    pe.wait_ge(s_m_copied, seen(s_m_copied))
                    sims(ps[2 + i], qT[:, i], kT[:, i], True).then_inc(s_m_sim, 1)
                if n:
                    j = (n - 1) % 2
                    pe.wait_ge(s_m_norm, seen(s_m_norm))
                    prs_T(ps[4], j, True).then_inc(s_m_pT, 1)
                    if n > 1:
                        pe.wait_ge(s_m_oTc, seen(s_m_oTc))
                        head_out(n - 2)
                    pe.wait_ge(s_m_pTc, seen(s_m_pTc))
                    nc.tensor.matmul(ps[6][0:64, 0:T], kvB[:, 0, n - 1, C:2 * C], prT[:, j, 0:T], start=True, stop=False,
                                     skip_group_check=True)
                    nc.tensor.matmul(ps[6][0:64, P:T], kvB[:, 1, n - 1, C:2 * C], prT[:, j, T:T + P], start=False, stop=True,
                                     skip_group_check=True).then_inc(s_m_oT, 1)
                if n in (2, 3, 6, 7) and not seen.work.final:
                    sum_rows(pe, seen)
            pe.wait_ge(s_m_oTc, seen(s_m_oTc))
            head_out(H2 - 1).then_inc(s_m_out, 1)

        def back_tensor(pe, seen):
            ln_tensor(pe, seen, y, unit=True)
            nc.tensor.matmul(ps[0][0:64, 0:T], W("l3_q"), yT[:], start=True, stop=True).then_inc(s_l3_q, 1)
            for t in range(2):
                nc.tensor.matmul(ps[1][0:P, 128 * t:128 * t + C], yT[:, tile(t)], W("l3_k"), start=True, stop=True)
                last = nc.tensor.matmul(ps[1][0:P, 128 * t + C:128 * t + 2 * C], yT[:, tile(t)], W("l3_v"), start=True, stop=True)
            last.then_inc(s_l3_kv, 1)
            pe.wait_ge(s_l3_elu, seen(s_l3_elu))
            for t in range(2):
                last = nc.tensor.matmul(ps[5][0:64, 0:72], t64[:, t, 0:C], v_sb[:, t], start=t == 0, stop=t == 1)
            last.then_inc(s_l3_kvs, 1)
            pe.wait_ge(s_l3_m, seen(s_l3_m))
            for t in range(2):
                last = nc.tensor.matmul(ps[3][0:P, 72 * t:72 * t + 72], qT[:, 0, tile(t)], m64[:], start=True, stop=True)
            last.then_inc(s_l3_num, 1)
            pe.wait_ge(s_l3_msg, seen(s_l3_msg))
            for t in range(2):
                last = nc.tensor.transpose(ps[4][0:64, tile(t)], t64[:, t, 0:C], K("ident")[:, 0:P])
            last.then_inc(s_l3_msgT, 1)
            pe.wait_ge(s_l3_msgTc, seen(s_l3_msgTc))
            for t in range(2):
                last = nc.tensor.matmul(ps[3][0:P, C * t:C * t + C], kT[:, 0, tile(t)], W("l3_m"), start=True, stop=True)
            last.then_inc(s_l3_mm, 1)
            sum_rows(pe, seen)
            pe.wait_ge(s_l3_msg2, seen(s_l3_msg2))
            for t in range(2):
                last = nc.tensor.transpose(ps[4][0:64, tile(t)], u64[:, t, 0:C], K("ident")[:, 0:P])
            last.then_inc(s_l3_msgT, 1)
            nc.tensor.matmul(ps[0][:, 0:T], W("l3_w1x"), yT[:], start=True, stop=False)
            pe.wait_ge(s_l3_msgTc, seen(s_l3_msgTc))
            nc.tensor.matmul(ps[0][:, 0:T], W("l3_w1m"), kT[:, 0], start=False, stop=True).then_inc(s_l3_hT, 1)
            pe.wait_ge(s_l3_relu, seen(s_l3_relu))
            for t in range(2):
                last = nc.tensor.matmul(ps[3][0:P, C * t:C * t + C], actT[:, 0, tile(t)], V("l3_w2"), start=True, stop=True)
            last.then_inc(s_l3_h, 1)
            sum_rows(pe, seen)
            pe.wait_ge(s_ln_y, seen(s_ln_y, 2))
            ln_tensor(pe, seen, y, unit=True)
            nc.tensor.matmul(ps[5][0:P, 0:T], W("cap_wr"), yT[:], start=True, stop=True).then_inc(s_c_w, 1)
            for c in range(2):
                last = nc.tensor.matmul(ps[0][:, c * T:(c + 1) * T], W("cap_w1", 128 * c, 128), yT[:], start=True, stop=True)
            last.then_inc(s_c_hT, 1)
            pe.wait_ge(s_c_act, seen(s_c_act))
            for t in range(2):
                for c in range(2):
                    last = nc.tensor.matmul(ps[3][0:P, C * t:C * t + C], actT[:, c, tile(t)],
                                            V("cap_w2")[:, C * c:C * c + C], start=c == 0, stop=c == 1)
            last.then_inc(s_c_y, 1)

        def back_sync(sp, seen, b):
            sp.wait_ge(s_c_out, seen(s_c_out))
            sp.dma_start(out[bass.ds(b, 1)].rearrange("a (t p) c -> p (a t) c", p=P), hB[:])\
                .then_inc(s_stored, 16)
            sp.wait_ge(s_stored, seen(s_stored, 16))

        def turn(b, front, back, work):
            early = front and not back and not work.sums
            middle = not early and not work.final
            with nc.Block() as block:
                @block.sync
                def _(sp):
                    seen = Count()
                    if front:
                        front_sync(sp, seen, b)
                    if early:
                        sp.dma_start(lattice_raw, lattice).then_inc(s_lattice, 16)
                    if back:
                        back_sync(sp, seen, b - 2)

                @block.vector
                def _(dve):
                    seen = Count(work, heads=back)
                    if front:
                        front_vector(dve, seen, early)
                    elif back:
                        for _ in work.held:
                            weigh_rows(dve, seen)
                        heads_vector(dve, seen, units=True)
                    if back:
                        back_vector(dve, seen)
                    for _ in seen.left():
                        weigh_rows(dve, seen)
                    if back:
                        dve.wait_ge(s_stored, seen(s_stored, 16))
                    if middle:
                        nc.vector.tensor_copy(hB[:], hG[:]).then_inc(s_dve, seen.one())
                        nc.vector.tensor_copy(yTB[:], yTG[:]).then_inc(s_dve, seen.one())
                        nc.vector.tensor_copy(wgtH[:], wgtG[:, 1, H2 - HELD:H2]).then_inc(s_dve, seen.one())
                        dve.wait_ge(s_dve, seen.steps)
                    if front:
                        nc.vector.tensor_copy(hG[:], hF[:]).then_inc(s_dve, seen.one())
                        nc.vector.tensor_copy(yTG[:], yTF[:]).then_inc(s_dve, seen.one())
                        nc.vector.tensor_copy(wgtG[:], wgtF[:]).then_inc(s_dve, seen.one())
                        if early:
                            nc.vector.tensor_copy(idxG[:, 1], idxF[:, 1]).then_inc(s_dve, seen.one())
                        else:
                            for u in range(UNITS - HELD, UNITS):
                                dve.wait_ge(fetched[u % SLOTS], fetches(work.batch, u))
                            nc.vector.tensor_copy(idxG[:], idxF[:]).then_inc(s_dve, seen.one())
                        dve.wait_ge(s_dve, seen.steps)

                @block.scalar
                def _(act):
                    seen = Count(work, heads=back)
                    if front:
                        front_scalar(act, seen, early)
                    elif back:
                        for _ in work.held:
                            keep_sum(act, seen)
                        heads_scalar(act, seen)
                    if back:
                        back_scalar(act, seen)
                    for _ in seen.left():
                        keep_sum(act, seen)
                    if middle:
                        act.wait_ge(s_kept, len(work.sums))
                        if back:
                            act.wait_ge(s_m_oT, H2)
                        nc.scalar.activation(kvB[:, 0], kvG[:, 0], ACT.Copy).then_inc(s_handed, 1)
                        nc.scalar.activation(kvB[:, 1, 0:H2 - HELD], kvG[:, 1, 0:H2 - HELD], ACT.Copy).then_inc(s_handed, 1)
                        act.wait_ge(s_handed, 2)

                @block.tensor
                def _(pe):
                    seen = Count(work)
                    if front:
                        front_tensor(pe, seen, early)
                    elif back:
                        for _ in work.held:
                            sum_rows(pe, seen)
                    if back:
                        heads_tensor(pe, seen)
                        back_tensor(pe, seen)
                    for _ in seen.left():
                        sum_rows(pe, seen)

                @block.gpsimd
                def _(pool):
                    if early:
                        pool.wait_ge(s_early, 1)
                    gather_pool(pool, work)
            nc.all_engine_barrier(sems_to_clear=cleared)

        eps = sb("eps", [P, 1])
        with nc.Block() as block:
            @block.sync
            def _(sp):
                for dst, src in ((w64_sb[:], w64), (w128_sb[:], w128), (rows_sb[:], rows.partition_broadcast(P)),
                                 (const_sb[:], const), (pk_sb[:, 0], pk_q), (pk_sb[:, 1], pk_k)):
                    sp.dma_start(dst, src).then_inc(s_x_loaded, 16)

            @block.vector
            def _(dve):
                nc.vector.memset(eps[:], 1e-5).then_inc(s_dve, 1)
                dve.wait_ge(s_dve, 1)

            @block.tensor
            def _(pe):
                pe.wait_ge(s_x_loaded, 6 * 16)
                nc.tensor.matmul(ps[0][0:64, 0:64], W("l0_wq"), W("l0_wk"), start=True, stop=True)
                nc.tensor.matmul(ps[0][0:64, 64:144], W("qcomp"), W("q_rcs"), start=True, stop=True)
                nc.tensor.matmul(ps[0][0:64, 144:288], W("kvcomp"), W("kv_rcsv"), start=True, stop=True)\
                    .then_inc(s_setup, 1)
                for g in range(16):
                    last = nc.tensor.matmul(ps[1 + g // 8][0:64, 64 * (g % 8):64 * (g % 8) + 64], pk_sb[:, 0, 64 * g:64 * g + 64],
                                            pk_sb[:, 1, 64 * g:64 * g + 64], start=True, stop=True)
                last.then_inc(s_setup, 1)

            @block.scalar
            def _(act):
                act.wait_ge(s_setup, 2)
                nc.scalar.activation(l0_a[:], ps[0][0:64, 0:64], ACT.Copy, scale=C ** -0.5)
                nc.scalar.activation(l2_qw[:], ps[0][0:64, 64:144], ACT.Copy, scale=64 ** -0.5)
                nc.scalar.activation(l2_kvw[:], ps[0][0:64, 144:288], ACT.Copy)
                for c in range(2):
                    last = nc.scalar.activation(pk_w[:, 512 * c:512 * c + 512], ps[1 + c][0:64, :], ACT.Copy)
                last.then_inc(s_act, 1)
                act.wait_ge(s_act, 1)
        nc.all_engine_barrier(sems_to_clear=cleared)

        own, over = range(UNITS - HELD), range(UNITS - HELD, UNITS)
        turn(0, True, False, Work(0, fetched=range(EARLY)))
        turn(1, True, False, Work(0, fetched=range(EARLY, UNITS), fresh=own))
        with nc.Fori(2, B) as b:
            turn(b, True, True, Work(b - 1, fetched=range(UNITS), held=over, fresh=own))
        turn(B, False, True, Work(B - 1, fetched=range(SHARED), held=over, fresh=range(SHARED - HELD), last=True))
        turn(B + 1, False, True, Work(B - 1, fetched=range(SHARED, UNITS), fresh=range(SHARED - HELD, UNITS), last=True,
                                      final=True))


def kernel(**inputs):
    import concourse.bacc as bacc
    from concourse.bass_utils import run_bass_kernel_spmd

    f = {k: np.asarray(v) for k, v in inputs.items()}

    def pack(table, parts, have):
        cols = []
        for name, n in table:
            a = np.asarray(have[name]).reshape(-1, n)
            cols.append(np.pad(a, ((0, parts - a.shape[0]), (0, 0))))
        return np.ascontiguousarray(np.concatenate(cols, axis=1), dtype=np.float32)

    qkv = f["L1_attn_W_qkv"].reshape(H1, 3, D1, C)
    bqkv = f["L1_attn_b_qkv"].reshape(H1, 3, D1)
    swap = np.arange(ROPE) ^ 1
    halves = lambda a: np.concatenate([a[:128], a[128:]], axis=1)
    w64 = pack(W64, 64, {
        "tok_key": f["L0_tok_W_key"], "tok_qry2": np.concatenate([f["L0_tok_W_qry"]] * 2, axis=1),
        "l0_wq": f["L0_attn_Wq"], "l0_wk": f["L0_attn_Wk"], "gate": f["L0_ffn_gate_w"].T, "out_w": f["L0_ffn_out_w"].T,
        "l1_q": qkv[:, 0].reshape(C, C).T,
        "l1_kv": np.concatenate([qkv[:, 1].reshape(C, C).T, qkv[:, 2].reshape(C, C).T], axis=1),
        "l1_proj": f["L1_attn_W_proj"].T, "l1_w1": f["L1_ffn_W1"],
        "qcomp": f["L2_attn_Wq_comp"].T, "kvcomp": f["L2_attn_Wkv_comp"].T,
        "q_rcs": np.concatenate([f["L2_attn_Wqr"], f["L2_attn_Wqc"], f["L2_attn_Wqr"][:, swap]], axis=1),
        "kv_rcsv": np.concatenate([f["L2_attn_Wkr"], f["L2_attn_Wkc"], f["L2_attn_Wkr"][:, swap], f["L2_attn_Wv"]], axis=1),
        "l2f_q": f["L2_ffn_Wq"], "l2f_o": f["L2_ffn_Wo"].reshape(H2, C, C).transpose(1, 0, 2).reshape(C, H2 * C),
        "l3_q": f["L3_attn_Wq"], "l3_k": f["L3_attn_Wk"], "l3_v": f["L3_attn_Wv"], "l3_m": f["L3_attn_Wm"],
        "l3_w1x": f["L3_attn_W1"][:C], "l3_w1m": f["L3_attn_W1"][C:], "cap_w1": f["L3_ffn_w1"],
        "cap_wr": np.repeat(f["L3_ffn_wr"], P, axis=1)})
    zero = np.zeros((C, 1), np.float32)
    tv, tb = f["L0_tok_v"].reshape(C, 1), f["L0_tok_b"].reshape(C, 1)
    w128 = pack(W128, 128, {
        "tok_v": np.concatenate([np.concatenate([tv, zero], 1), np.concatenate([zero, tv], 1)]),
        "tok_b": np.concatenate([tb, tb]), "l1_bq": bqkv[:, 0].reshape(C, 1),
        "l1_b1": f["L1_ffn_b1"].reshape(2, 128).T, "cap_b1": f["L3_ffn_b1"].reshape(2, 128).T,
        "l1_wg": halves(f["L1_ffn_Wg"]), "l1_wd": halves(f["L1_ffn_Wd"].transpose(1, 0, 2).reshape(HID, E1 * C)),
        "l3_w2": f["L3_attn_W2"], "cap_w2": halves(f["L3_ffn_w2"])})
    kvw = lambda a, b: np.concatenate([a.reshape(-1), b.reshape(-1)])
    rows = {
        "out_b": f["L0_ffn_out_b"], "ln_g": f["L0_ffn_ln_g"], "ln_b": f["L0_ffn_ln_b"],
        "l1_bkv": kvw(bqkv[:, 1], bqkv[:, 2]), "l1_w": kvw(f["L1_attn_kln_w"], f["L1_attn_vln_w"]),
        "l1_b": kvw(f["L1_attn_kln_b"], f["L1_attn_vln_b"]), "l1_bproj": f["L1_attn_b_proj"], "l1_bg": f["L1_ffn_bg"],
        "g1": f["L3_attn_g1"], "b1": f["L3_attn_b1"], "g2": f["L3_attn_g2"], "b2": f["L3_attn_b2"],
        "cap_b2": f["L3_ffn_b2"], "cap_br": f["L3_ffn_br"], "bd": f["L1_ffn_bd"].reshape(-1)}
    rows = np.concatenate([np.asarray(rows[n], np.float32) for n, _ in ROWS])

    i, j = np.arange(T)[:, None], np.arange(T)[None, :]
    tiles = lambda m: m.reshape(2, P, T).transpose(1, 0, 2).reshape(P, 2 * T)
    half = ROPE // 2
    theta = (1.0 / np.float32(10000.0) ** (np.arange(half, dtype=np.float32) / np.float32(half))).astype(np.float32)
    angle = (np.arange(T, dtype=np.float32)[:, None] * theta[None, :]).T
    cos = np.ones((C, T), np.float32)
    cos[:ROPE] = np.repeat(np.cos(angle), 2, axis=0)
    sin = np.repeat(np.sin(angle), 2, axis=0)
    sin[0::2] *= -1
    place = (np.arange(n_cand, dtype=np.uint32) + 1) << 25
    block = lambda n, d: np.kron(np.eye(n), np.ones((d, d)))
    const = pack(CONST, 128, {
        "ident": np.eye(128), "causal": np.where(j <= i, 0.0, MASKED)[:P, :P], "tri": tiles((j < i) * 1.0),
        "own": tiles((i == j) * 1.0), "high_key": np.broadcast_to(np.tile(place, H2).view(np.float32), (P, H2 * n_cand)),
        "low_key": np.broadcast_to(np.bitwise_or.outer(np.arange(H2, dtype=np.uint32) * NKV, place).reshape(-1).view(np.float32),
                                   (P, H2 * n_cand)), "cos": cos, "sin": sin,
        "mask1": block(H1, D1) / T, "mask3": np.concatenate([block(H3, D3), np.kron(np.eye(H3), np.ones((D3, 1)))], axis=1),
        "ones": np.ones((1, P))})
    arrays = {
        "x": f["x"], "xT": np.ascontiguousarray(f["x"].transpose(0, 2, 1)), "w64": w64, "w128": w128,
        "lattice": np.ascontiguousarray(f["L0_ffn_lattice_weights"].transpose(2, 0, 1).reshape(C, EXPERTS0 * C)),
        "pk_q": np.ascontiguousarray(f["L2_ffn_Wq_pk"].reshape(C, 16, 32).transpose(2, 1, 0).reshape(32, 16 * C)),
        "pk_k": np.ascontiguousarray(f["L2_ffn_pk_keys"].transpose(3, 0, 2, 1).reshape(32, 16 * NK)),
        "rows": rows, "const": const,
        "table": np.concatenate([f["L2_ffn_keys_table"], f["L2_ffn_values_table"]], axis=1)}
    nc = bacc.Bacc("TRN2", target_bir_lowering=False, num_devices=1)
    args = [nc.dram_tensor(n, a.shape, mybir.dt.from_np(a.dtype), kind="ExternalInput").ap() for n, a in arrays.items()]
    out = nc.dram_tensor("out", (B, T, C), mybir.dt.float32, kind="ExternalOutput").ap()
    tower(nc, *args, out)
    r = run_bass_kernel_spmd(nc, [arrays], core_ids=[0])
    return r.results[0]["out"]
```
